# Optimizing a Trainium2 kernel written in Bass

```python
import numpy as np
import jax
import jax.numpy as jnp

def _softmax(x, axis=-1):
    return jax.nn.softmax(x, axis=axis)

def _gelu(x):
    return jax.nn.gelu(x, approximate=True)

def _silu(x):
    return jax.nn.silu(x)

def _sigmoid(x):
    return jax.nn.sigmoid(x)

def _layernorm(x, axis=-1, eps=1e-05):
    m = jnp.mean(x, axis=axis, keepdims=True)
    v = jnp.var(x, axis=axis, keepdims=True)
    return (x - m) / jnp.sqrt(v + eps)

def _scatter_add(tgt, idx, src, axis=0):
    return tgt.at[idx].add(src)

def _segment_sum(src, seg, n):
    return jax.ops.segment_sum(src, seg, n)
kernel_name = 'mk_decoder_preln_d1_seqx_r4_a67b9c'

def setup_inputs(seed: int=0):
    np.random.seed(seed)
    _w = jnp.asarray

    def _rec_inputs():
        import jax
        import jax.numpy as jnp
        _rk = jax.random.key(seed)
        x = 7.22e-05 + 1 * jax.random.normal(jax.random.fold_in(_rk, 1), (16, 256, 256), jnp.float32)
        _lenS = 256 - jax.random.randint(jax.random.fold_in(_rk, 7), (16,), 0, max(1, 256 // 4) + 1, jnp.int32)
        _lenS2 = 256 - jax.random.randint(jax.random.fold_in(_rk, 8), (16,), 0, max(1, 256 // 4) + 1, jnp.int32)
        _ctx_1024P = jax.random.normal(jax.random.fold_in(_rk, 11), (16, 16, 256), jnp.float32)
        _ctx_1024c = jax.random.dirichlet(jax.random.fold_in(_rk, 511), 0.3 * jnp.ones((16,), jnp.float32), (16, 256))
        _ctx_1024t = jnp.einsum('bsk,bkd->bsd', _ctx_1024c, _ctx_1024P)
        _ctx_1024t = _ctx_1024t * jax.lax.rsqrt(jnp.mean(jnp.square(_ctx_1024t)) + 1e-12) * 0.953939
        ctx_1024 = 4.13588e-05 + 0.999923 * (_ctx_1024t + 0.3 * jax.random.normal(jax.random.fold_in(_rk, 611), (16, 256, 256), jnp.float32))
        return (x, ctx_1024)
    x, ctx_1024 = _rec_inputs()

    def _L0_attn_setup():
        import jax, jax.numpy as jnp
        import numpy as np
        B, S, E, H = (4, 512, 256, 16)
        D = E // H
        LN_EPS = 1e-05
        key = jax.random.key(seed)
        ks = jax.random.split(key, 12)
        lim = 1.0 / np.sqrt(E)
        u = lambda k, shp: jax.random.uniform(k, shp, jnp.float32, -lim, lim)
        return {'x': jax.random.normal(ks[0], (B, S, E), jnp.float32), 'wq': u(ks[1], (E, E)), 'bq': u(ks[2], (E,)), 'wk': u(ks[3], (E, E)), 'bk': u(ks[4], (E,)), 'wv': u(ks[5], (E, E)), 'bv': u(ks[6], (E,)), 'wo': u(ks[7], (E, E)), 'bo': u(ks[8], (E,)), 'freq_filter': jax.random.normal(ks[9], (H, D), jnp.float32) * 0.1, 'phase_shift': jax.random.normal(ks[10], (H, D), jnp.float32) * 0.1, 'ln_gamma': jnp.ones((E,), jnp.float32), 'ln_beta': jnp.zeros((E,), jnp.float32)}
    _L0_attn_all = _L0_attn_setup()
    _L0_attn_in = {k: v for k, v in _L0_attn_all.items() if k in ('wq', 'bq', 'wk', 'bk', 'wv', 'bv', 'wo', 'bo', 'freq_filter', 'phase_shift', 'ln_gamma', 'ln_beta')}
    del _L0_attn_all

    def _L0_xattn_setup():
        import jax, jax.numpy as jnp
        import numpy as np
        from jax import lax
        NUM_HEADS = 16
        DIM = 256
        BATCH = 4
        SEQ = 512
        key = jax.random.key(seed)
        ks = jax.random.split(key, 12)
        f32 = jnp.float32
        q = jax.random.normal(ks[0], (BATCH, SEQ, DIM), dtype=f32)
        k = jax.random.normal(ks[1], (BATCH, SEQ, DIM), dtype=f32)
        v = jax.random.normal(ks[2], (BATCH, SEQ, DIM), dtype=f32)
        lim = 1.0 / np.sqrt(DIM)
        Wi = jax.random.uniform(ks[3], (DIM, DIM), minval=-lim, maxval=lim, dtype=f32)
        bi = jax.random.uniform(ks[4], (DIM,), minval=-lim, maxval=lim, dtype=f32)
        Wg = jax.random.uniform(ks[5], (DIM, DIM), minval=-lim, maxval=lim, dtype=f32)
        bg = jax.random.uniform(ks[6], (DIM,), minval=-lim, maxval=lim, dtype=f32)
        Wo = jax.random.uniform(ks[7], (DIM, DIM), minval=-lim, maxval=lim, dtype=f32)
        bo = jax.random.uniform(ks[8], (DIM,), minval=-lim, maxval=lim, dtype=f32)
        A = jax.random.normal(ks[9], (DIM, DIM), dtype=f32) * 0.1
        Bm = jax.random.normal(ks[10], (DIM, DIM), dtype=f32) * 0.1
        decay = jnp.full((1, NUM_HEADS, 1), 0.9, dtype=f32)
        return dict(q=q, k=k, v=v, Wi=Wi, bi=bi, Wg=Wg, bg=bg, A=A, Bm=Bm, Wo=Wo, bo=bo, decay=decay)
    _L0_xattn_all = _L0_xattn_setup()
    _L0_xattn_in = {k: v for k, v in _L0_xattn_all.items() if k in ('Wi', 'bi', 'Wg', 'bg', 'A', 'Bm', 'Wo', 'bo', 'decay')}
    del _L0_xattn_all

    def _L0_ffn_setup():
        import math
        import jax, jax.numpy as jnp
        import numpy as np
        B, S, H = (4, 512, 256)
        E, K, I = (8, 2, 256)
        NSH = 2
        CF, RSF = (1.25, 1.0)
        key = jax.random.key(seed)
        ks = jax.random.split(key, 8)
        w = lambda k, sh: jax.random.normal(k, sh, dtype=jnp.float32) * 0.02
        return {'hidden_states': jax.random.normal(ks[0], (B, S, H), dtype=jnp.float32), 'gate_w': w(ks[1], (E, H)), 'we_gate': w(ks[2], (E, I, H)), 'we_up': w(ks[3], (E, I, H)), 'we_down': w(ks[4], (E, H, I)), 'ws_gate': w(ks[5], (NSH * I, H)), 'ws_up': w(ks[6], (NSH * I, H)), 'ws_down': w(ks[7], (H, NSH * I))}
    _L0_ffn_all = _L0_ffn_setup()
    _L0_ffn_in = {k: v for k, v in _L0_ffn_all.items() if k in ('gate_w', 'we_gate', 'we_up', 'we_down', 'ws_gate', 'ws_up', 'ws_down')}
    del _L0_ffn_all
    return {'x': x, 'ctx_1024': ctx_1024, 'L0_attn_wq': _L0_attn_in['wq'], 'L0_attn_bq': _L0_attn_in['bq'], 'L0_attn_wk': _L0_attn_in['wk'], 'L0_attn_bk': _L0_attn_in['bk'], 'L0_attn_wv': _L0_attn_in['wv'], 'L0_attn_bv': _L0_attn_in['bv'], 'L0_attn_wo': _L0_attn_in['wo'], 'L0_attn_bo': _L0_attn_in['bo'], 'L0_attn_freq_filter': _L0_attn_in['freq_filter'], 'L0_attn_phase_shift': _L0_attn_in['phase_shift'], 'L0_attn_ln_gamma': _L0_attn_in['ln_gamma'], 'L0_attn_ln_beta': _L0_attn_in['ln_beta'], 'L0_xattn_Wi': _L0_xattn_in['Wi'], 'L0_xattn_bi': _L0_xattn_in['bi'], 'L0_xattn_Wg': _L0_xattn_in['Wg'], 'L0_xattn_bg': _L0_xattn_in['bg'], 'L0_xattn_A': _L0_xattn_in['A'], 'L0_xattn_Bm': _L0_xattn_in['Bm'], 'L0_xattn_Wo': _L0_xattn_in['Wo'], 'L0_xattn_bo': _L0_xattn_in['bo'], 'L0_xattn_decay': _L0_xattn_in['decay'], 'L0_ffn_gate_w': _L0_ffn_in['gate_w'], 'L0_ffn_we_gate': _L0_ffn_in['we_gate'], 'L0_ffn_we_up': _L0_ffn_in['we_up'], 'L0_ffn_we_down': _L0_ffn_in['we_down'], 'L0_ffn_ws_gate': _L0_ffn_in['ws_gate'], 'L0_ffn_ws_up': _L0_ffn_in['ws_up'], 'L0_ffn_ws_down': _L0_ffn_in['ws_down']}

def reference(x, ctx_1024, L0_attn_wq, L0_attn_bq, L0_attn_wk, L0_attn_bk, L0_attn_wv, L0_attn_bv, L0_attn_wo, L0_attn_bo, L0_attn_freq_filter, L0_attn_phase_shift, L0_attn_ln_gamma, L0_attn_ln_beta, L0_xattn_Wi, L0_xattn_bi, L0_xattn_Wg, L0_xattn_bg, L0_xattn_A, L0_xattn_Bm, L0_xattn_Wo, L0_xattn_bo, L0_xattn_decay, L0_ffn_gate_w, L0_ffn_we_gate, L0_ffn_we_up, L0_ffn_we_down, L0_ffn_ws_gate, L0_ffn_ws_up, L0_ffn_ws_down):
    import jax
    import jax.numpy as jnp

    def _L0_attn_ref(x, wq, bq, wk, bk, wv, bv, wo, bo, freq_filter, phase_shift, ln_gamma, ln_beta):
        import jax, jax.numpy as jnp
        import numpy as np
        B, S, E, H = (4, 512, 256, 16)
        D = E // H
        LN_EPS = 1e-05
        Bq, Sq, Eq = x.shape

        def proj(w, b):
            y = jnp.einsum('bse,fe->bsf', x, w) + b
            return y.reshape(Bq, Sq, H, D).transpose(0, 2, 1, 3)
        q, k, v = (proj(wq, bq), proj(wk, bk), proj(wv, bv))
        q_fft = jnp.fft.rfft(q, axis=2)
        k_fft = jnp.fft.rfft(k, axis=2)
        v_fft = jnp.fft.rfft(v, axis=2)
        freq_mod = (jnp.exp(1j * phase_shift.astype(jnp.complex64)) * freq_filter.astype(jnp.complex64))[None, :, None, :]
        q_filt = q_fft * freq_mod
        k_filt = k_fft * freq_mod
        conv_qk = q_filt * jnp.conj(k_filt)
        attn_fft = jnp.abs(conv_qk)
        attn_time = jnp.fft.irfft(attn_fft.astype(jnp.complex64), n=Sq, axis=2)
        attn = jax.nn.softmax(attn_time, axis=2)
        out_fft = jnp.fft.rfft(attn, axis=2) * v_fft
        out = jnp.fft.irfft(out_fft, n=Sq, axis=2)
        out = out.transpose(0, 2, 1, 3).reshape(Bq, Sq, Eq)
        out = jnp.einsum('bse,fe->bsf', out, wo) + bo
        h = x + out
        mu = jnp.mean(h, axis=-1, keepdims=True)
        var = jnp.var(h, axis=-1, keepdims=True)
        return (h - mu) * jax.lax.rsqrt(var + LN_EPS) * ln_gamma + ln_beta

    def _L0_xattn_ref(q, k, v, Wi, bi, Wg, bg, A, Bm, Wo, bo, decay):
        import jax, jax.numpy as jnp
        import numpy as np
        from jax import lax
        NUM_HEADS = 16
        DIM = 256
        BATCH = 4
        SEQ = 512
        B, S, D = q.shape
        H = decay.shape[1]
        hd = D // H
        qh = jnp.moveaxis(q.reshape(B, S, H, hd), 1, 0)
        kh = jnp.moveaxis(k.reshape(B, S, H, hd), 1, 0)
        vh = jnp.moveaxis(v.reshape(B, S, H, hd), 1, 0)

        def step(carry, xs):
            r, state = carry
            qt, kt, vt = xs
            r = decay * r + kt * vt
            retained = (qt * r).reshape(B, D)
            inp = retained @ Wi.T + bi
            gate = jax.nn.sigmoid(inp @ Wg.T + bg)
            blended = gate * state + (1.0 - gate) * inp
            state = jnp.tanh(blended @ A.T + inp @ Bm.T)
            out = state @ Wo.T + bo
            return ((r, state), out)
        r0 = jnp.zeros((B, H, hd), dtype=q.dtype)
        s0 = jnp.zeros((B, D), dtype=q.dtype)
        _, outs = lax.scan(step, (r0, s0), (qh, kh, vh))
        return jnp.moveaxis(outs, 0, 1)

    def _L0_ffn_ref(hidden_states, gate_w, we_gate, we_up, we_down, ws_gate, ws_up, ws_down):
        import math
        import jax, jax.numpy as jnp
        import numpy as np
        B, S, H = (4, 512, 256)
        E, K, I = (8, 2, 256)
        NSH = 2
        CF, RSF = (1.25, 1.0)
        orig_shape = hidden_states.shape
        x = hidden_states.reshape(-1, H)
        N = x.shape[0]
        logits = x.astype(jnp.float32) @ gate_w.astype(jnp.float32).T
        scores = jax.nn.softmax(logits, axis=-1)
        topk_w, topk_idx = jax.lax.top_k(scores, K)
        topk_w = topk_w / (topk_w.sum(-1, keepdims=True) + 1e-20) * RSF
        capacity = math.ceil(CF * N * K / E)
        flat = topk_idx.reshape(-1)
        one_hot = jax.nn.one_hot(flat, E, dtype=jnp.int32)
        pos = jnp.cumsum(one_hot, axis=0) - 1
        pos_tok = jnp.take_along_axis(pos, flat[:, None], axis=1)[:, 0]
        keep = (pos_tok < capacity).reshape(N, K)
        topk_w = topk_w * keep.astype(topk_w.dtype)
        comb = jnp.zeros((N, E), jnp.float32).at[jnp.arange(N)[:, None], topk_idx].add(topk_w)
        g = jnp.einsum('nh,eih->nei', x, we_gate)
        u = jnp.einsum('nh,eih->nei', x, we_up)
        eo = jnp.einsum('nei,ehi->neh', jax.nn.silu(g) * u, we_down)
        y = jnp.einsum('neh,ne->nh', eo, comb)
        sh = jax.nn.silu(x @ ws_gate.T) * (x @ ws_up.T) @ ws_down.T
        return (y + sh).reshape(orig_shape)
    x = x + _L0_attn_ref(_layernorm(x, axis=-1), L0_attn_wq, L0_attn_bq, L0_attn_wk, L0_attn_bk, L0_attn_wv, L0_attn_bv, L0_attn_wo, L0_attn_bo, L0_attn_freq_filter, L0_attn_phase_shift, L0_attn_ln_gamma, L0_attn_ln_beta)
    x = x + _L0_xattn_ref(_layernorm(x, axis=-1), ctx_1024, ctx_1024, L0_xattn_Wi, L0_xattn_bi, L0_xattn_Wg, L0_xattn_bg, L0_xattn_A, L0_xattn_Bm, L0_xattn_Wo, L0_xattn_bo, L0_xattn_decay)
    x = x + _L0_ffn_ref(_layernorm(x, axis=-1), L0_ffn_gate_w, L0_ffn_we_gate, L0_ffn_we_up, L0_ffn_we_down, L0_ffn_ws_gate, L0_ffn_ws_up, L0_ffn_ws_down)
    return x

_drawn_inputs = setup_inputs


def setup_inputs(seed=0):
    import zlib

    import numpy as np

    out = dict(_drawn_inputs(seed))
    spreads = {'L0_attn_ln_gamma': (1.0, 0.2),
     'L0_attn_ln_beta': (0.0, 0.1),
     'L0_xattn_decay': (0.8999999761581421, 0.2)}
    factors = {'L0_attn_wq': 3.117,
     'L0_attn_bq': 64.0,
     'L0_attn_wk': 3.357,
     'L0_attn_bk': 64.0,
     'L0_attn_phase_shift': 64.0,
     'L0_xattn_bi': 8.0,
     'L0_xattn_bg': 21.816,
     'L0_xattn_bo': 3.376,
     'L0_ffn_gate_w': 8.0,
     'L0_ffn_we_gate': 8.0,
     'L0_ffn_we_up': 8.0,
     'L0_ffn_we_down': 8.0,
     'L0_ffn_ws_gate': 5.003,
     'L0_ffn_ws_up': 4.955,
     'L0_ffn_ws_down': 4.966}
    for name, (base, spread) in spreads.items():
        noise = np.random.default_rng([zlib.crc32(name.encode()), seed]).standard_normal(out[name].shape)
        drawn = base * np.exp(spread * noise) if base else spread * noise
        out[name] = jnp.asarray(drawn.astype(out[name].dtype))
    for name, factor in factors.items():
        out[name] = (out[name] * factor).astype(out[name].dtype)
    return out
```

```python
from contextlib import ExitStack

import numpy as np

import concourse.bass as bass
from concourse import mybir

P = 128
B, S, E = 16, 256, 256
KB = E // P
SB = S // P
NF = S // 2
HEADS = 16
EPS = 1e-5
F32 = mybir.dt.float32
BF16 = mybir.dt.bfloat16
U32 = mybir.dt.uint32
ALU = mybir.AluOpType
ACT = mybir.ActivationFunctionType
AX = mybir.AxisListType


def dft_constants():
    t = np.arange(S, dtype=np.float64)
    f = np.arange(NF, dtype=np.float64)
    ang = 2 * np.pi / S * ((np.outer(t, f)) % S)
    nyq = 1.0 - 2.0 * (t % 2)
    weight = np.where(f == 0, 1.0, 2.0)
    sin = np.sin(ang)
    sin[:, 0] = nyq
    forward = np.concatenate([np.cos(ang), sin], 1)
    inverse = np.concatenate([weight * np.cos(ang), np.where(f == 0, 1.0, 2.0) * sin], 1).T / S
    sym = np.cos(ang[:NF]).T
    minus0 = weight[:, None] * (sym - 1.0) / S
    nyq_minus0 = (nyq[:NF] - 1.0) / S
    last_minus0 = weight * ((1.0 - 2.0 * (f % 2)) - 1.0) / S
    tw = np.where(t[:NF] == 0, 1.0, 2.0)
    even = tw[:, None] * np.cos(ang[:NF])
    even_ny = even.copy()
    even_ny[:, 0] = tw * nyq[:NF]
    last = 1.0 - 2.0 * (f % 2)
    row = np.concatenate([nyq_minus0, last])[None, :]
    col = last_minus0[:, None]
    mask = np.where(f == 0, 0.0, 1.0)[:, None]
    cast = lambda a: np.ascontiguousarray(a, dtype=np.float32)
    return {
        "forward": cast(forward), "inverse": cast(inverse),
        "minus0": cast(minus0), "evens": cast(np.concatenate([even, even_ny], 1)),
        "rows": cast(row), "cols": cast(np.concatenate([col, mask], 1)),
    }


def misc_constants():
    k = np.arange(P)
    return {
        "ident": np.eye(P, dtype=np.float32),
        "earlier": (k[:, None] < k[None, :]).astype(np.float32),
        "dc3": np.repeat(np.where(np.arange(P) == 0, float(S), 0.0)[None, :], 3, 0).astype(np.float32),
        "eye3": np.eye(3, dtype=np.float32),
        "rank_tie": np.broadcast_to((np.arange(8)[:, None] > np.arange(8)[None, :]).astype(np.float32).reshape(1, 64), (P, 64)).copy(),
        "slot0": np.broadcast_to((np.arange(8) * CAP).astype(np.float32)[None, :], (P, 8)).copy(),
    }


NEXP = 8
CAP = 1280
NT = B * SB
CH = 16
NSH = 4
NSLOT = NEXP * CAP
ECH = CAP // 256


def build(nc, a, out):
    ctx = ExitStack()
    with ctx:
        def sb(name, shape, dt=F32, stack=ctx):
            return stack.enter_context(nc.sbuf_tensor(name, shape, dt))

        def sem(name, stack=ctx):
            return stack.enter_context(nc.semaphore(name))

        bank = [ctx.enter_context(nc.psum_tensor(f"bank{i}", [P, 512], F32)) for i in range(8)]
        resid = sb("resid", [P, B, SB, E])
        tok2 = sb("tok2", [P, B * SB * E])
        tok3 = sb("tok3", [P, B * SB * E])
        ln_x = tok2[:, :].rearrange("p (b k e) -> p b k e", b=B, k=SB)
        gate_all = tok2[:, :].rearrange("p (k b s) -> p k b s", k=KB, b=B)
        inp_all = tok3[:, :].rearrange("p (k b s) -> p k b s", k=KB, b=B)
        mhalf = sb("mhalf", [P, 2])

        w = {name: sb(name, [P, KB, E]) for name in ("wi_t", "wg_t", "a_t", "bm_t", "wxo_t")}
        w["ws_gate_t"] = sb("ws_gate_t", [P, KB, NSH * P])
        w["ws_up_t"] = sb("ws_up_t", [P, KB, NSH * P])
        w["ws_down_t"] = sb("ws_down_t", [P, NSH, E])
        w["gate_t"] = sb("gate_t", [P, KB, NEXP])
        cols = {name: sb("col_" + name, [P, KB]) for name in ("bi", "bg", "decay")}
        ident = sb("ident", [P, P])
        dispatched = nc.dram_tensor("dispatched", (NSLOT, E), F32, kind="Internal").ap()
        expert_out = nc.dram_tensor("expert_out", (NSLOT + P, E), F32, kind="Internal").ap()
        bxo = sb("bxo", [P, E])

        attention(nc, a, sb, sem, bank, resid, ln_x, mhalf, inp_all, w, cols, ident, bxo, dispatched, expert_out)
        recurrence_inputs(nc, sb, sem, bank, resid, gate_all, inp_all, mhalf, w, cols, ident)
        recurrence(nc, sb, sem, bank, gate_all, inp_all, w)
        ffn(nc, a, sb, sem, bank, resid, ln_x, inp_all, mhalf, out, w, ident, bxo, dispatched, expert_out)


def attention(nc, a, sb_, sem_, bank, resid, ln_x, mhalf, ctx_all, later_w, later_cols, ident, bxo, dispatched, expert_out):
    ctx = ExitStack()
    with ctx:
        def sb(name, shape, dt=F32):
            return sb_(name, shape, dt, ctx)

        def sem(name):
            return sem_(name, ctx)

        wqk = sb("wqk", [P, KB, 2 * E])
        wv = sb("wv", [P, KB, E])
        wo = sb("wo", [P, KB, E])
        fwd = sb("fwd", [P, SB, 2 * NF])
        inv = sb("inv", [P, 2, S])
        minus0 = sb("minus0", [P, NF])
        evens = sb("evens", [P, 2 * NF])
        rows = sb("rows", [1, 2 * NF])
        cols = sb("cols", [P, 2])
        gamma = sb("gamma", [P, E])
        beta = sb("beta", [P, E])
        filt = sb("filt", [P, 2 * E])
        bias3 = sb("bias3", [3, 4 * E])
        bias_hi = sb("bias_hi", [3, 4 * E], BF16)
        bias_mid = sb("bias_mid", [3, 4 * E], BF16)
        bias_lo = sb("bias_lo", [3, 4 * E], BF16)
        bias_r = sb("bias_r", [3, 4 * E])
        bias_p = sb("bias_p", [3, 4 * E])
        bias_parts = sb("bias_parts", [3, 4 * E], BF16)
        dc3f = sb("dc3f", [3, P])
        dc3 = sb("dc3", [3, P], BF16)
        ones3 = sb("ones3", [3, P], BF16)
        eye3 = sb("eye3", [3, 3])
        one = sb("one", [1, 1])
        st1 = sb("st1", [P, SB, 6])
        mv1 = sb("mv1", [P, SB, 2])
        ve1 = sb("ve1", [P, SB])
        rstd1 = sb("rstd1", [P, SB])
        xn = sb("xn", [P, SB, E])
        fxt = sb("fxt", [P, KB, 2 * NF])
        sqc = sb("sqc", [P, 2 * E])
        sqs = sb("sqs", [P, 2 * E])
        mag = sb("mag", [P, 2 * E])
        p2 = sb("p2", [P, 2 * E])
        pm = sb("pm", [P, E])
        pn = sb("pn", [1, E])
        em = sb("em", [P, E])
        en = sb("en", [1, E])
        vs = sb("vs", [P, 2, E])
        gs = sb("gs", [P, 2, E])
        rz = sb("rz", [P, KB])
        ot = sb("ot", [P, KB, S])
        hh = sb("hh", [P, SB, E])
        tt = sb("tt", [P, SB, E])
        st2 = sb("st2", [P, SB, 6])
        mv2 = sb("mv2", [P, SB, 2])
        ve2 = sb("ve2", [P, SB])
        rstd2 = sb("rstd2", [P, SB])

        waited = sem("waited")
        loaded = sem("weights_loaded")
        rows_loaded = sem("rows_loaded")
        x_loaded = sem("x_loaded")
        fixed = sem("constants_ready")
        prep = sem("bias_steps")
        scaled = sem("filter_applied")
        ln1_stats, ln1_aggr, ln1_ve, ln1_rstd = sem("ln1_stats"), sem("ln1_aggr"), sem("ln1_ve"), sem("ln1_rstd")
        xn_ready, xn_saved = sem("xn_ready"), sem("xn_saved")
        dft_done, fx_copied, qk_done, v_done, v_copied = sem("dft_done"), sem("fx_copied"), sem("qk_done"), sem("v_done"), sem("v_copied")
        sq_done, mag_done, p2_done, p_ready, a_done = sem("sq_done"), sem("mag_done"), sem("p2_done"), sem("p_ready"), sem("a_done")
        e_ready, A_done, g_ready, rz_ready = sem("e_ready"), sem("A_done"), sem("g_ready"), sem("rz_ready")
        ot_done, ot_ready, y_done, h_ready = sem("ot_done"), sem("ot_ready"), sem("y_done"), sem("h_ready")
        ln2_stats, ln2_aggr, ln2_ve, ln2_rstd = sem("ln2_stats"), sem("ln2_aggr"), sem("ln2_ve"), sem("ln2_rstd")
        bx_ready, t_ready, x2_ready = sem("bx_ready"), sem("t_ready"), sem("x2_ready")

        def kxm(w):
            return w.rearrange("(k p) n -> p k n", p=P)

        def bcast(v, n):
            return v.rearrange("(o n) -> o n", o=1).broadcast_to([n, v.shape[0]])

        later = sem("later_loaded")
        zeros_ready, zero_stored = sem("zeros_ready"), sem("zero_stored")
        zeros = sb("zeros", [P, 8 * E])

        NLOAD = 10

        def program(body, eng):
            body(0, front=True, back=False)
            with eng.Fori(1, B) as i:
                body(i, front=True, back=True)
            body(B, front=False, back=True)

        with nc.Block() as block:
            @block.sync
            def _(sp):
                sp.dma_start(resid[:, 0], a["x"][0].rearrange("(k p) e -> p k e", p=P)).then_inc(x_loaded, 16)
                sp.dma_start(fwd[:, :, :], kxm(a["forward"])).then_inc(loaded, 16)
                sp.dma_start(wqk[:, :, 0:E], kxm(a["wq_t"])).then_inc(loaded, 16)
                sp.dma_start(wqk[:, :, E:2 * E], kxm(a["wk_t"])).then_inc(loaded, 16)
                sp.dma_start(wv[:, :, :], kxm(a["wv_t"])).then_inc(loaded, 16)
                sp.dma_start(wo[:, :, :], kxm(a["wo_t"])).then_inc(loaded, 16)
                sp.dma_start(inv[:, :, :], kxm(a["inverse"])).then_inc(loaded, 16)
                sp.dma_start(minus0[:, :], a["minus0"]).then_inc(loaded, 16)
                sp.dma_start(evens[:, :], a["evens"]).then_inc(loaded, 16)
                sp.dma_start(rows[:, :], a["rows"]).then_inc(loaded, 16)
                sp.dma_start(cols[:, :], a["cols"]).then_inc(loaded, 16)
                with sp.Fori(1, B) as i:
                    sp.wait_ge(x_loaded, i * 16)
                    sp.dma_start(resid[:, i], a["x"].rearrange("b (k p) e -> p b k e", p=P)[:, i]).then_inc(x_loaded, 16)
                for k in range(KB):
                    sp.dma_start(ctx_all[:, k], a["ctx_t"].rearrange("b p k s -> k p b s")[k]).then_inc(later, 16)
                for name, tile in later_w.items():
                    sp.dma_start(tile[:, :, :], kxm(a[name])).then_inc(later, 16)
                for name, tile in later_cols.items():
                    sp.dma_start(tile[:, :], a[name].rearrange("(k p) -> p k", p=P), allow_slow_non_contiguous=True).then_inc(later, 16)
                sp.dma_start(ident[:, :], a["ident"]).then_inc(later, 16)
                sp.dma_start(bxo[:, :], bcast(a["bxo"], P)).then_inc(later, 16)
                sp.wait_ge(zeros_ready, 1)
                with sp.Fori(0, NSLOT // (P * 8)) as r:
                    sp.dma_start(dispatched.rearrange("(r p j) e -> p r (j e)", p=P, j=8)[:, r, :], zeros[:, :]).then_inc(zero_stored, 16)
                sp.dma_start(expert_out[NSLOT:NSLOT + P, :], zeros[:, 0:E]).then_inc(zero_stored, 16)
                sp.wait_ge(zero_stored, 16 * (NSLOT // (P * 8) + 1))
                sp.wait_ge(later, 16 * (KB + len(later_w) + len(later_cols) + 2))

            @block.gpsimd
            def _(pool):
                nc.gpsimd.memset(zeros[:, :], 0.0).then_inc(zeros_ready, 1)
                nc.gpsimd.memset(mhalf[:, :], -0.5).then_inc(fixed, 1)
                nc.gpsimd.memset(ones3[:, :], 1.0).then_inc(fixed, 1)
                nc.gpsimd.memset(one[:, :], 1.0).then_inc(fixed, 1)
                pool.wait_ge(fixed, 3)

                def body(i, front, back):
                    if front:
                        pool.wait_ge(ln1_aggr, (i + 1) * 2)
                        pool.sem_inc(waited, 1)
                        nc.gpsimd.tensor_scalar(ve1[:, :], mv1[:, :, 1], EPS, None, ALU.add).then_inc(ln1_ve, 1)
                        pool.wait_ge(ln1_ve, i + 1)
                        nc.gpsimd.tensor_tensor(rstd1[:, :], ve1[:, :], mhalf[:, :], ALU.pow).then_inc(ln1_rstd, 1)
                        pool.wait_ge(xn_ready, (i + 1) * 2)
                        nc.gpsimd.tensor_copy(ln_x[:, i], xn[:, :, :]).then_inc(xn_saved, 1)
                    if back:
                        j = i - 1
                        nc.gpsimd.tensor_tensor(resid[:, j], resid[:, j], beta[:, :].rearrange("p (o e) -> p o e", o=1).broadcast_to([P, SB, E]), ALU.add).then_inc(bx_ready, 1)
                        pool.wait_ge(ln2_aggr, (j + 1) * 2)
                        pool.sem_inc(waited, 1)
                        nc.gpsimd.tensor_scalar(ve2[:, :], mv2[:, :, 1], EPS, None, ALU.add).then_inc(ln2_ve, 1)
                        pool.wait_ge(ln2_ve, j + 1)
                        nc.gpsimd.tensor_tensor(rstd2[:, :], ve2[:, :], mhalf[:, :], ALU.pow).then_inc(ln2_rstd, 1)
                pool.wait_ge(loaded, 16 * NLOAD)
                pool.wait_ge(rows_loaded, 16 * NLOAD)
                program(body, pool)

            @block.scalar
            def _(act):
                act.dma_start(gamma[:, :], bcast(a["ln_gamma"], P)).then_inc(rows_loaded, 16)
                act.dma_start(beta[:, :], bcast(a["ln_beta"], P)).then_inc(rows_loaded, 16)
                for h in range(2):
                    act.dma_start(filt[:, h * E:(h + 1) * E], bcast(a["freq_filter"], P)).then_inc(rows_loaded, 16)
                for n, v in enumerate(("bq", "bk", "bv", "bo")):
                    act.dma_start(bias3[:, n * E:(n + 1) * E], bcast(a[v], 3)).then_inc(rows_loaded, 16)
                act.dma_start(dc3f[:, :], a["dc3"]).then_inc(rows_loaded, 16)
                act.dma_start(eye3[:, :], a["eye3"]).then_inc(rows_loaded, 16)

                def body(i, front, back):
                    j = i - 1
                    if front:
                        act.wait_ge(dft_done, i + 1)
                        if back:
                            act.wait_ge(v_done, i)
                        nc.scalar.activation(fxt[:, :, :].rearrange("p k f -> p (k f)"), bank[0][:, :], ACT.Copy).then_inc(fx_copied, 1)
                    if back:
                        act.wait_ge(a_done, j + 1)
                        nc.scalar.activation(em[:, :], bank[4][:, 0:E], ACT.Exp).then_inc(e_ready, 1)
                        nc.scalar.activation(en[:, :], bank[4][0:1, E:2 * E], ACT.Exp).then_inc(e_ready, 1)
                    if front:
                        act.wait_ge(qk_done, i + 1)
                        if back:
                            act.wait_ge(p2_done, 2 * i)
                        nc.scalar.activation(sqc[:, :], bank[1][:, :], ACT.Square).then_inc(sq_done, 1)
                        nc.scalar.activation(sqs[:, :], bank[2][:, :], ACT.Square).then_inc(sq_done, 1)
                        act.wait_ge(p2_done, i * 2 + 2)
                        if back:
                            act.wait_ge(a_done, i)
                        nc.scalar.activation(pm[:, :], p2[:, 0:E], ACT.Sqrt).then_inc(p_ready, 1)
                        nc.scalar.activation(pn[:, :], p2[0:1, E:2 * E], ACT.Sqrt).then_inc(p_ready, 1)
                    if back:
                        act.wait_ge(ot_done, j + 1)
                        act.wait_ge(rz_ready, j + 1)
                        for n in range(KB):
                            nc.scalar.activation(ot[:, n, :], bank[6][:, n * S:(n + 1) * S], ACT.Copy, scale=rz[:, n:n + 1]).then_inc(ot_ready, 1)
                    if front:
                        act.wait_ge(v_done, i + 1)
                        if back:
                            act.wait_ge(g_ready, i)
                        nc.scalar.activation(vs[:, :, :].rearrange("p k f -> p (k f)"), bank[3][:, :], ACT.Copy).then_inc(v_copied, 1)
                program(body, act)

            @block.vector
            def _(dve):
                dve.sem_inc(h_ready, 1)
                dve.wait_ge(fixed, 3)
                dve.wait_ge(loaded, 16 * NLOAD)
                dve.wait_ge(rows_loaded, 16 * NLOAD)
                nc.vector.tensor_tensor(bias3[:, 0:2 * E], bias3[:, 0:2 * E], filt[0:3, :], ALU.mult).then_inc(prep, 1)
                nc.vector.tensor_copy(dc3[:, :], dc3f[:, :]).then_inc(prep, 1)
                dve.wait_ge(prep, 2)
                nc.vector.tensor_copy(bias_hi[:, :], bias3[:, :]).then_inc(prep, 1)
                dve.wait_ge(prep, 3)
                nc.vector.tensor_tensor(bias_r[:, :], bias3[:, :], bias_hi[:, :], ALU.subtract).then_inc(prep, 1)
                dve.wait_ge(prep, 4)
                nc.vector.tensor_copy(bias_mid[:, :], bias_r[:, :]).then_inc(prep, 1)
                dve.wait_ge(prep, 5)
                nc.vector.tensor_tensor(bias3[:, :], bias_r[:, :], bias_mid[:, :], ALU.subtract).then_inc(prep, 1)
                dve.wait_ge(prep, 6)
                nc.vector.tensor_copy(bias_lo[:, :], bias3[:, :]).then_inc(prep, 1)
                dve.wait_ge(prep, 7)
                nc.vector.tensor_scalar(bias_r[:, :], bias_hi[:, :], eye3[:, 0:1], None, ALU.mult).then_inc(prep, 1)
                dve.wait_ge(prep, 8)
                nc.vector.scalar_tensor_tensor(bias_p[:, :], bias_mid[:, :], eye3[:, 1:2], bias_r[:, :], ALU.mult, ALU.add).then_inc(prep, 1)
                dve.wait_ge(prep, 9)
                nc.vector.scalar_tensor_tensor(bias_parts[:, :], bias_lo[:, :], eye3[:, 2:3], bias_p[:, :], ALU.mult, ALU.add).then_inc(prep, 1)
                for k in range(KB):
                    nc.vector.tensor_tensor(wqk[:, k, :], wqk[:, k, :], filt[:, :], ALU.mult).then_inc(scaled, 1)

                def layernorm1(i, first):
                    dve.wait_ge(x_loaded, (i + 1) * 16)
                    for k in range(SB):
                        nc.vector.bn_stats(st1[:, k, :], resid[:, i, k, :]).then_inc(ln1_stats, 1)
                    dve.wait_ge(ln1_stats, (i + 1) * 2)
                    if not first:
                        dve.wait_ge(ln1_rstd, i)
                    dve.sem_inc(waited, 1)
                    for k in range(SB):
                        nc.vector.bn_aggr(mv1[:, k, :], st1[:, k, :]).then_inc(ln1_aggr, 1)
                    dve.wait_ge(ln1_rstd, i + 1)
                    if not first:
                        dve.wait_ge(dft_done, i)
                        dve.wait_ge(xn_saved, i)
                    for k in range(SB):
                        nc.vector.tensor_scalar(xn[:, k, :], resid[:, i, k, :], mv1[:, k, 0:1], rstd1[:, k:k + 1], ALU.subtract, ALU.mult).then_inc(xn_ready, 1)

                def body(i, front, back):
                    j = i - 1
                    if front:
                        layernorm1(i, not back)
                        dve.wait_ge(sq_done, i * 2 + 2)
                        nc.vector.scalar_tensor_tensor(mag[:, :], sqs[:, :], cols[:, 1:2], sqc[:, :], ALU.mult, ALU.add).then_inc(mag_done, 1)
                        if back:
                            dve.wait_ge(p_ready, 2 * i)
                        nc.vector.tensor_tensor(p2[0:1, E:2 * E], sqs[0:1, 0:E], sqs[0:1, E:2 * E], ALU.mult).then_inc(p2_done, 1)
                        dve.wait_ge(mag_done, i + 1)
                        nc.vector.tensor_tensor(p2[:, 0:E], mag[:, 0:E], mag[:, E:2 * E], ALU.mult).then_inc(p2_done, 1)
                    if back:
                        dve.wait_ge(A_done, j + 1)
                        dve.wait_ge(v_copied, j + 1)
                        nc.vector.tensor_tensor(gs[:, :, :].rearrange("p k f -> p (k f)"), bank[5][:, :], vs[:, :, :].rearrange("p k f -> p (k f)"), ALU.mult).then_inc(g_ready, 1)
                        nc.vector.reciprocal(rz[:, :], bank[4][:, 0:KB]).then_inc(rz_ready, 1)
                        dve.wait_ge(y_done, j + 1)
                        dve.wait_ge(xn_saved, j + 1)
                        nc.vector.tensor_tensor(hh[:, :, :].rearrange("p k e -> p (k e)"), bank[7][:, :], ln_x[:, j].rearrange("p k e -> p (k e)"), ALU.add).then_inc(h_ready, 1)
                        dve.wait_ge(h_ready, j + 2)
                        for k in range(SB):
                            nc.vector.bn_stats(st2[:, k, :], hh[:, k, :]).then_inc(ln2_stats, 1)
                        dve.wait_ge(ln2_stats, j * 2 + 2)
                        dve.sem_inc(waited, 1)
                        for k in range(SB):
                            nc.vector.bn_aggr(mv2[:, k, :], st2[:, k, :]).then_inc(ln2_aggr, 1)
                        dve.wait_ge(ln2_aggr, j * 2 + 2)
                        for k in range(SB):
                            nc.vector.scalar_tensor_tensor(tt[:, k, :], hh[:, k, :], mv2[:, k, 0:1], gamma[:, :], ALU.subtract, ALU.mult).then_inc(t_ready, 1)
                        dve.wait_ge(t_ready, j * 2 + 2)
                        dve.wait_ge(ln2_rstd, j + 1)
                        dve.wait_ge(bx_ready, j + 1)
                        for k in range(SB):
                            nc.vector.scalar_tensor_tensor(resid[:, j, k, :], tt[:, k, :], rstd2[:, k:k + 1], resid[:, j, k, :], ALU.mult, ALU.add).then_inc(x2_ready, 1)
                        dve.wait_ge(x2_ready, j * 2 + 2)
                program(body, dve)

            @block.tensor
            def _(pe):
                pe.wait_ge(loaded, 16 * NLOAD)
                pe.wait_ge(rows_loaded, 16 * NLOAD)
                pe.wait_ge(prep, 10)
                pe.wait_ge(scaled, KB)

                def body(i, front, back):
                    j = i - 1
                    if front:
                        pe.wait_ge(xn_ready, i * 2 + 2)
                        if back:
                            pe.wait_ge(fx_copied, i)
                        for m in range(KB):
                            for k in range(SB):
                                last = nc.tensor.matmul(bank[0][:, m * S:(m + 1) * S], xn[:, k, m * P:(m + 1) * P], fwd[:, k, :], start=(k == 0), stop=(k == SB - 1))
                        last.then_inc(dft_done, 1)
                    if back:
                        pe.wait_ge(p_ready, j * 2 + 2)
                        nc.tensor.matmul(bank[4][:, 0:E], minus0[:, :], pm[:, :], start=True, stop=False)
                        nc.tensor.matmul(bank[4][:, 0:E], rows[:, 0:NF], pn[:, :], start=False, stop=True)
                        nc.tensor.matmul(bank[4][0:1, E:2 * E], cols[:, 0:1], pm[:, :], start=True, stop=True).then_inc(a_done, 1)
                    if front:
                        pe.wait_ge(fx_copied, i + 1)
                        if back:
                            pe.wait_ge(sq_done, 2 * i)
                        for f in range(2):
                            for k in range(KB):
                                last = nc.tensor.matmul(bank[1 + f][:, :], fxt[:, k, f * P:(f + 1) * P], wqk[:, k, :], start=(k == 0), stop=(k == KB - 1 and f == 1))
                            if f == 0:
                                nc.tensor.matmul(bank[1][:, :], dc3[:, :], bias_parts[:, 0:2 * E], start=False, stop=True)
                        last.then_inc(qk_done, 1)
                    if back:
                        pe.wait_ge(e_ready, j * 2 + 2)
                        for h in range(2):
                            nc.tensor.matmul(bank[5][:, h * E:(h + 1) * E], evens[:, h * NF:(h + 1) * NF], em[:, :], start=True, stop=False)
                            nc.tensor.matmul(bank[5][:, h * E:(h + 1) * E], rows[:, NF:2 * NF], en[:, :], start=False, stop=True)
                        for n in range(KB):
                            nc.tensor.matmul(bank[4][:, n:n + 1], em[:, n * P:(n + 1) * P], evens[:, 0:1], start=True, stop=False)
                            last = nc.tensor.matmul(bank[4][:, n:n + 1], en[:, n * P:(n + 1) * P], one[:, :], start=False, stop=True)
                        last.then_inc(A_done, 1)

                    def v_half(f):
                        for k in range(KB):
                            last = nc.tensor.matmul(bank[3][:, f * E:(f + 1) * E], fxt[:, k, f * P:(f + 1) * P], wv[:, k, :], start=(k == 0), stop=(k == KB - 1 and f == 1))
                        if f == 0:
                            last = nc.tensor.matmul(bank[3][:, 0:E], dc3[:, :], bias_parts[:, 2 * E:3 * E], start=False, stop=True)
                        return last

                    if front:
                        if back:
                            pe.wait_ge(v_copied, i)
                        v_half(0)
                    if back:
                        pe.wait_ge(g_ready, j + 1)
                        for n in range(KB):
                            for f in range(2):
                                last = nc.tensor.matmul(bank[6][:, n * S:(n + 1) * S], gs[:, f, n * P:(n + 1) * P], inv[:, f, :], start=(f == 0), stop=(f == 1))
                        last.then_inc(ot_done, 1)
                    if front:
                        v_half(1).then_inc(v_done, 1)
                    if back:
                        pe.wait_ge(ot_ready, j * 2 + 2)
                        pe.wait_ge(h_ready, j + 1)
                        for s in range(SB):
                            for k in range(KB):
                                nc.tensor.matmul(bank[7][:, s * E:(s + 1) * E], ot[:, k, s * P:(s + 1) * P], wo[:, k, :], start=(k == 0), stop=False)
                            last = nc.tensor.matmul(bank[7][:, s * E:(s + 1) * E], ones3[:, :], bias_parts[:, 3 * E:4 * E], start=False, stop=True)
                        last.then_inc(y_done, 1)
                program(body, pe)


def recurrence_inputs(nc, sb_, sem_, bank, resid, gate_all, inp_all, mhalf, w, cols, ident):
    ctx = ExitStack()
    with ctx:
        def sb(name, shape, dt=F32):
            return sb_(name, shape, dt, ctx)

        def sem(name):
            return sem_(name, ctx)

        st = sb("st", [P, SB, 6])
        mv = sb("mv", [P, SB, 2])
        ve = sb("ve", [P, SB])
        rstd = sb("rstd", [P, SB])
        xq = sb("xq", [P, SB, E])
        decay = sb("decay_row", [P, KB, S])
        ones = sb("ones_row", [P, S])
        hbg = sb("hbg", [P, KB])
        sq = sb("sq", [P, KB, S])
        sums = sb("sums", [P, KB, S])
        ret = sb("ret", [P, KB, S])
        th = sb("th", [P, KB, S])
        waited = sem("waited2")
        fixed, halved = sem("ones_ready"), sem("rows_ready")
        ln_stats, ln_aggr, ln_ve, ln_rstd = sem("q_stats"), sem("q_aggr"), sem("q_ve"), sem("q_rstd")
        xq_ready, xt_done, sq_ready, sums_ready, ret_ready = sem("xq_ready"), sem("xt_done"), sem("sq_ready"), sem("sums_ready"), sem("ret_ready")
        inp_done, inp_ready, z_done, th_ready, gate_ready = sem("inp_done"), sem("inp_ready"), sem("z_done"), sem("th_ready"), sem("gate_ready")

        def program(body, eng):
            body(0, (0,))
            body(1, (0, 1))
            with eng.Fori(2, B) as i:
                body(i, (0, 1, 2))
            body(B, (1, 2))
            body(B + 1, (2,))

        with nc.Block() as block:
            @block.gpsimd
            def _(pool):
                nc.gpsimd.memset(ones[:, :], 1.0).then_inc(fixed, 1)

                def body(i, stages):
                    if 0 in stages:
                        if 1 in stages:
                            pool.wait_ge(sums_ready, i * 2)
                        nc.gpsimd.tensor_tensor(sq[:, :, :], inp_all[:, :, i, :], inp_all[:, :, i, :], ALU.mult).then_inc(sq_ready, 1)
                        pool.wait_ge(ln_aggr, i * 2 + 2)
                        pool.sem_inc(waited, 1)
                        nc.gpsimd.tensor_scalar(ve[:, :], mv[:, :, 1], EPS, None, ALU.add).then_inc(ln_ve, 1)
                        pool.wait_ge(ln_ve, i + 1)
                        nc.gpsimd.tensor_tensor(rstd[:, :], ve[:, :], mhalf[:, :], ALU.pow).then_inc(ln_rstd, 1)
                program(body, pool)

            @block.vector
            def _(dve):
                dve.wait_ge(fixed, 1)
                for k in range(KB):
                    nc.vector.tensor_scalar(decay[:, k, :], ones[:, :], cols["decay"][:, k:k + 1], None, ALU.mult).then_inc(halved, 1)
                dve.sem_inc(gate_ready, 1)
                nc.vector.tensor_scalar(hbg[:, :], cols["bg"][:, :], 0.5, None, ALU.mult).then_inc(halved, 1)
                dve.wait_ge(halved, 3)

                def body(i, stages):
                    if 0 in stages:
                        for k in range(SB):
                            nc.vector.bn_stats(st[:, k, :], resid[:, i, k, :]).then_inc(ln_stats, 1)
                        dve.wait_ge(ln_stats, i * 2 + 2)
                        if 1 in stages:
                            dve.wait_ge(ln_rstd, i)
                        dve.sem_inc(waited, 1)
                        for k in range(SB):
                            nc.vector.bn_aggr(mv[:, k, :], st[:, k, :]).then_inc(ln_aggr, 1)
                        dve.wait_ge(sq_ready, i + 1)
                        if 1 in stages:
                            dve.wait_ge(ret_ready, i)
                        for k in range(KB):
                            nc.vector.tensor_tensor_scan(sums[:, k, :], decay[:, k, :], sq[:, k, :], 0.0, ALU.mult, ALU.add).then_inc(sums_ready, 1)
                        dve.wait_ge(ln_rstd, i + 1)
                        if 1 in stages:
                            dve.wait_ge(xt_done, i)
                        for k in range(SB):
                            nc.vector.tensor_scalar(xq[:, k, :], resid[:, i, k, :], mv[:, k, 0:1], rstd[:, k:k + 1], ALU.subtract, ALU.mult).then_inc(xq_ready, 1)
                    if 2 in stages:
                        dve.wait_ge(th_ready, i * 2 - 1)
                        nc.vector.tensor_scalar(gate_all[:, :, i - 2, :], th[:, :, :], 0.5, 0.5, ALU.mult, ALU.add).then_inc(gate_ready, 1)
                    if 0 in stages:
                        dve.wait_ge(xt_done, i + 1)
                        dve.wait_ge(sums_ready, i * 2 + 2)
                        if 1 in stages:
                            dve.wait_ge(inp_done, i)
                        nc.vector.tensor_tensor(ret[:, :, :].rearrange("p k s -> p (k s)"), bank[0][:, :], sums[:, :, :].rearrange("p k s -> p (k s)"), ALU.mult).then_inc(ret_ready, 1)
                program(body, dve)

            @block.scalar
            def _(act):
                act.sem_inc(th_ready, 1)
                act.wait_ge(halved, 3)

                def body(i, stages):
                    if 1 in stages:
                        act.wait_ge(inp_done, i)
                        act.sem_inc(waited, 1)
                        for n in range(KB):
                            nc.scalar.activation(inp_all[:, n, i - 1, :], bank[1][:, n * S:(n + 1) * S], ACT.Identity, bias=cols["bi"][:, n:n + 1]).then_inc(inp_ready, 1)
                    if 2 in stages:
                        act.wait_ge(z_done, i - 1)
                        act.wait_ge(gate_ready, i - 1)
                        for n in range(KB):
                            nc.scalar.activation(th[:, n, :], bank[2][:, n * S:(n + 1) * S], ACT.Tanh, bias=hbg[:, n:n + 1], scale=0.5).then_inc(th_ready, 1)
                program(body, act)

            @block.tensor
            def _(pe):
                def body(i, stages):
                    if 0 in stages:
                        pe.wait_ge(xq_ready, i * 2 + 2)
                        if 1 in stages:
                            pe.wait_ge(ret_ready, i)
                        for k in range(KB):
                            for s in range(SB):
                                last = nc.tensor.transpose(bank[0][:, k * S + s * P:k * S + (s + 1) * P], xq[:, s, k * P:(k + 1) * P], ident[:, :])
                        last.then_inc(xt_done, 1)
                    if 1 in stages:
                        pe.wait_ge(ret_ready, i)
                        if 2 in stages:
                            pe.wait_ge(inp_ready, i * 2 - 2)
                        for n in range(KB):
                            for k in range(KB):
                                last = nc.tensor.matmul(bank[1][:, n * S:(n + 1) * S], w["wi_t"][:, k, n * P:(n + 1) * P], ret[:, k, :], start=(k == 0), stop=(k == KB - 1))
                        last.then_inc(inp_done, 1)
                    if 2 in stages:
                        pe.wait_ge(inp_ready, i * 2 - 2)
                        pe.wait_ge(th_ready, i * 2 - 3)
                        for n in range(KB):
                            for k in range(KB):
                                last = nc.tensor.matmul(bank[2][:, n * S:(n + 1) * S], w["wg_t"][:, k, n * P:(n + 1) * P], inp_all[:, k, i - 2, :], start=(k == 0), stop=(k == KB - 1))
                        last.then_inc(z_done, 1)
                program(body, pe)


def recurrence(nc, sb_, sem_, bank, gate_all, state_all, w):
    ctx = ExitStack()
    NCH = S // CH
    W = KB * B
    with ctx:
        def sb(name, shape, dt=F32):
            return sb_(name, shape, dt, ctx)

        def sem(name):
            return sem_(name, ctx)

        gate = [sb(f"gate_chunk{q}", [P, CH, KB, B]) for q in range(2)]
        inp = [sb(f"inp_chunk{q}", [P, CH, KB, B]) for q in range(2)]
        prod = sb("prod_chunk", [P, CH, KB, B])
        rest = [sb(f"rest_chunk{q}", [P, CH, KB, B]) for q in range(2)]
        state = [sb(f"state_chunk{q}", [P, CH, KB, B]) for q in range(2)]
        blend = sb("blend", [P, KB, B])
        acc = [bank[3 + q][:, :].rearrange("p (t n b) -> p t n b", t=CH, n=KB) for q in range(2)]
        waited = sem("waited3")
        staged, step_staged, prodded = sem("chunk_staged"), sem("chunk_copied"), sem("prod_ready")
        blended, stepped, tanh_done, saved = sem("blended"), sem("stepped"), sem("tanh_done"), sem("states_saved")
        zeroed = sem("state_zeroed")
        laid = sem("inputs_laid")

        def program(chunk, eng):
            with eng.Fori(0, NCH // 2 - 1) as h:
                chunk(h * 2, 0, True, True)
                chunk(h * 2 + 1, 1, True, True)
            chunk(NCH - 2, 0, True, False)
            chunk(NCH - 1, 1, False, False)

        with nc.Block() as block:
            @block.gpsimd
            def _(pool):
                def stage(c, q):
                    for k in range(KB):
                        nc.gpsimd.tensor_copy(gate[q][:, :, k, :], gate_all[:, k, :, bass.ts(c, CH)].rearrange("p b t -> p t b")).then_inc(step_staged, 1)
                        nc.gpsimd.tensor_copy(inp[q][:, :, k, :], state_all[:, k, :, bass.ts(c, CH)].rearrange("p b t -> p t b")).then_inc(step_staged, 1)
                    pool.wait_ge(step_staged, c * 4 + 4)
                    nc.gpsimd.tensor_tensor(prod[:, :, :, :], gate[q][:, :, :, :], inp[q][:, :, :, :], ALU.mult).then_inc(prodded, 1)
                    pool.wait_ge(prodded, c + 1)
                    nc.gpsimd.tensor_tensor(rest[q][:, :, :, :], inp[q][:, :, :, :], prod[:, :, :, :], ALU.subtract).then_inc(staged, 1)

                nc.gpsimd.memset(state[1][:, CH - 1], 0.0).then_inc(zeroed, 1)
                for _ in range(2):
                    pool.sem_inc(saved, 1)
                stage(0, 0)
                stage(1, 1)

                def chunk(c, q, more, two):
                    pool.wait_ge(tanh_done, c * CH + (CH + 1))
                    pool.sem_inc(waited, 1)
                    for k in range(KB):
                        last = nc.gpsimd.tensor_copy(state_all[:, k, :, bass.ts(c, CH)].rearrange("p b t -> p t b"), state[q][:, :, k, :])
                        if k < KB - 1:
                            last.then_inc(waited, 1)
                    last.then_inc(saved, 1)
                    if two:
                        stage(c + 2, q)
                program(chunk, pool)

            @block.tensor
            def _(pe):
                def pieces(q):
                    for g in range(0, CH, 4):
                        for n in range(KB):
                            for m, (lhs, rhs) in enumerate(((w["bm_t"], inp[q]), (w["a_t"], rest[q]))):
                                for k in range(KB):
                                    first = g == 0 and n == 0 and m == 0 and k == 0
                                    yield nc.tensor.matmul(acc[q][:, g:g + 4, n, :], lhs[:, k, n * P:(n + 1) * P], rhs[:, g:g + 4, k, :],
                                                           start=first, stop=False, skip_group_check=True)

                pe.wait_ge(staged, 1)
                for _ in pieces(0):
                    pass

                def chunk(c, q, more, two):
                    ahead = pieces(1 - q) if more else iter(())
                    for t in range(CH):
                        pe.wait_ge(blended, c * CH + (t + 1))
                        for n in range(KB):
                            for k in range(KB):
                                last = nc.tensor.matmul(acc[q][:, t, n, :], w["a_t"][:, k, n * P:(n + 1) * P], blend[:, k, :],
                                                        start=False, stop=False, skip_group_check=True)
                        last.then_inc(stepped, 1)
                        if more:
                            if t == 0:
                                pe.wait_ge(staged, c + 2)
                            for _ in range(2):
                                next(ahead)
                program(chunk, pe)

            @block.vector
            def _(dve):
                def chunk(c, q, more, two):
                    for t in range(CH):
                        before = state[q][:, t - 1] if t else state[1 - q][:, CH - 1]
                        if t == 0:
                            dve.wait_ge(staged, c + 1)
                        dve.wait_ge(tanh_done, c * CH + (t + 1))
                        nc.vector.tensor_tensor(blend[:, :, :].rearrange("p k b -> p (k b)"), gate[q][:, t].rearrange("p k b -> p (k b)"), before.rearrange("p k b -> p (k b)"), ALU.mult).then_inc(blended, 1)
                program(chunk, dve)

            @block.scalar
            def _(act):
                act.wait_ge(zeroed, 1)
                act.sem_inc(tanh_done, 1)

                def chunk(c, q, more, two):
                    for t in range(CH):
                        if t == 0:
                            act.wait_ge(saved, c + 1)
                        act.wait_ge(stepped, c * CH + (t + 1))
                        nc.scalar.activation(state[q][:, t].rearrange("p k b -> p (k b)"), acc[q][:, t].rearrange("p n b -> p (n b)"), ACT.Tanh).then_inc(tanh_done, 1)
                program(chunk, act)


def ffn(nc, a, sb, sem, bank, resid, rows_all, state_all, mhalf, out, w, ident, bxo, dispatched, expert_out):
    ctx = ExitStack()
    with ctx:
        logits = sb("logits", [P, NT, NEXP], F32, ctx)
        slot = [sb(f"slot_rank{k}", [P, NT], U32, ctx) for k in range(2)]
        share = [sb(f"share_rank{k}", [P, NT], F32, ctx) for k in range(2)]
        shared_experts(nc, sb, sem, bank, resid, rows_all, state_all, mhalf, w, ident, bxo, logits)
        route(nc, a, sb, sem, bank, rows_all, logits, slot, share, dispatched)
        routed_experts(nc, a, sb, sem, bank, ident, dispatched, expert_out)
        combine(nc, sb, sem, resid, slot, share, expert_out, out)


def shared_experts(nc, sb_, sem_, bank, resid, rows_all, state_all, mhalf, w, ident, bxo, logits):
    ctx = ExitStack()
    with ctx:
        def sb(name, shape, dt=F32):
            return sb_(name, shape, dt, ctx)

        def sem(name):
            return sem_(name, ctx)

        stt = sb("states_tile", [P, KB, S])
        st = sb("st3", [P, SB, 6])
        mv = sb("mv3", [P, SB, 2])
        ve = sb("ve3", [P, SB])
        rstd = sb("rstd3", [P, SB])
        xf = sb("xf", [P, SB, E])
        xt = sb("xt", [P, KB, S])
        th = sb("th3", [P, NSH, S])
        ga = sb("ga3", [P, NSH, S])
        hid = sb("hid3", [P, NSH, S])
        waited = sem("waited4")
        st_ready, y_done, x_ready, bx_ready = sem("st_ready"), sem("yx_done"), sem("x3_ready"), sem("bxo_added")
        ln_stats, ln_aggr, ln_ve, ln_rstd = sem("f_stats"), sem("f_aggr"), sem("f_ve"), sem("f_rstd")
        xf_ready, xf_saved, xt_done, xt_ready, lg_done, lg_ready = sem("xf_ready"), sem("xf_saved"), sem("xft_done"), sem("xft_ready"), sem("logits_done"), sem("logits_ready")
        up_done, th_ready, ga_ready, hid_ready, down_done, sh_added = sem("up_done"), sem("f_th_ready"), sem("ga_ready"), sem("hid_ready"), sem("down_done"), sem("sh_added")

        def program(body, eng):
            body(0, (0,))
            body(1, (0, 1))
            body(2, (0, 1, 2))
            with eng.Fori(3, B) as i:
                body(i, (0, 1, 2))
            body(B, (1, 2))
            body(B + 1, (2,))

        def flat(ap):
            return ap.rearrange("p k s -> p (k s)")

        with nc.Block() as block:
            @block.gpsimd
            def _(pool):
                def body(i, stages):
                    if 0 in stages:
                        nc.gpsimd.tensor_tensor(resid[:, i], resid[:, i], bxo[:, :].rearrange("p (o e) -> p o e", o=1).broadcast_to([P, SB, E]), ALU.add).then_inc(bx_ready, 1)
                        pool.wait_ge(ln_aggr, i * 2 + 2)
                        pool.sem_inc(waited, 1)
                        nc.gpsimd.tensor_scalar(ve[:, :], mv[:, :, 1], EPS, None, ALU.add).then_inc(ln_ve, 1)
                        pool.wait_ge(ln_ve, i + 1)
                        nc.gpsimd.tensor_tensor(rstd[:, :], ve[:, :], mhalf[:, :], ALU.pow).then_inc(ln_rstd, 1)
                        pool.wait_ge(xf_ready, i * 2 + 2)
                        nc.gpsimd.tensor_copy(rows_all[:, i], xf[:, :, :]).then_inc(xf_saved, 1)
                program(body, pool)

            @block.scalar
            def _(act):
                def body(i, stages):
                    if 0 in stages:
                        if 1 in stages:
                            act.wait_ge(y_done, i)
                        nc.scalar.activation(stt[:, :, :], state_all[:, :, i, :], ACT.Copy).then_inc(st_ready, 1)
                    if 1 in stages:
                        act.wait_ge(up_done, i)
                        if 2 in stages:
                            act.wait_ge(ga_ready, i * 2 - 2)
                        for h in range(2):
                            nc.scalar.activation(flat(th[:, 2 * h:2 * h + 2, :]), bank[3 + h][:, :], ACT.Tanh, scale=0.5).then_inc(th_ready, 1)
                    if 0 in stages:
                        act.wait_ge(xt_done, i + 1)
                        if 1 in stages:
                            act.wait_ge(up_done, i)
                        nc.scalar.activation(flat(xt[:, :, :]), bank[1][:, :], ACT.Copy).then_inc(xt_ready, 1)
                program(body, act)

            @block.vector
            def _(dve):
                def body(i, stages):
                    if 0 in stages:
                        dve.wait_ge(y_done, i + 1)
                        dve.wait_ge(bx_ready, i + 1)
                        nc.vector.tensor_tensor(flat(resid[:, i]), bank[0][:, :], flat(resid[:, i]), ALU.add).then_inc(x_ready, 1)
                        dve.wait_ge(x_ready, i + 1)
                        dve.sem_inc(waited, 1)
                        for k in range(SB):
                            nc.vector.bn_stats(st[:, k, :], resid[:, i, k, :]).then_inc(ln_stats, 1)
                        dve.wait_ge(ln_stats, i * 2 + 2)
                        dve.sem_inc(waited, 1)
                        for k in range(SB):
                            nc.vector.bn_aggr(mv[:, k, :], st[:, k, :]).then_inc(ln_aggr, 1)
                        dve.wait_ge(ln_rstd, i + 1)
                        if 1 in stages:
                            dve.wait_ge(xt_done, i)
                            dve.wait_ge(xf_saved, i)
                        for k in range(SB):
                            nc.vector.tensor_scalar(xf[:, k, :], resid[:, i, k, :], mv[:, k, 0:1], rstd[:, k:k + 1], ALU.subtract, ALU.mult).then_inc(xf_ready, 1)
                    if 2 in stages:
                        dve.wait_ge(down_done, i - 1)
                        nc.vector.tensor_tensor(flat(resid[:, i - 2]), bank[7][:, :], flat(resid[:, i - 2]), ALU.add).then_inc(sh_added, 1)
                    if 1 in stages:
                        dve.wait_ge(th_ready, i * 2)
                        for h in range(2):
                            nc.vector.scalar_tensor_tensor(flat(ga[:, 2 * h:2 * h + 2, :]), flat(th[:, 2 * h:2 * h + 2, :]), 1.0, bank[3 + h][:, :], ALU.add, ALU.mult).then_inc(ga_ready, 1)
                        dve.wait_ge(ga_ready, i * 2)
                        if 2 in stages:
                            dve.wait_ge(down_done, i - 1)
                        for h in range(2):
                            nc.vector.scalar_tensor_tensor(flat(hid[:, 2 * h:2 * h + 2, :]), flat(ga[:, 2 * h:2 * h + 2, :]), 0.5, bank[5 + h][:, :], ALU.mult, ALU.mult).then_inc(hid_ready, 1)
                    if 0 in stages:
                        dve.wait_ge(lg_done, i + 1)
                        nc.vector.tensor_copy(logits[:, bass.ts(i, SB), :].rearrange("p s e -> p (s e)"), bank[2][:, 0:SB * NEXP]).then_inc(lg_ready, 1)
                program(body, dve)

            @block.tensor
            def _(pe):
                def body(i, stages):
                    if 0 in stages:
                        pe.wait_ge(st_ready, i + 1)
                        if 1 in stages:
                            pe.wait_ge(x_ready, i)
                        for s in range(SB):
                            for k in range(KB):
                                last = nc.tensor.matmul(bank[0][:, s * E:(s + 1) * E], stt[:, k, s * P:(s + 1) * P], w["wxo_t"][:, k, :], start=(k == 0), stop=(k == KB - 1))
                        last.then_inc(y_done, 1)
                    if 2 in stages:
                        pe.wait_ge(hid_ready, i * 2 - 2)
                        if not isinstance(i, int) or i > 2:
                            pe.wait_ge(sh_added, i - 2)
                        for s in range(SB):
                            for m in range(NSH):
                                last = nc.tensor.matmul(bank[7][:, s * E:(s + 1) * E], hid[:, m, s * P:(s + 1) * P], w["ws_down_t"][:, m, :], start=(m == 0), stop=(m == NSH - 1))
                        last.then_inc(down_done, 1)
                    if 1 in stages:
                        pe.wait_ge(xt_ready, i)
                        for name, b0 in (("ws_gate_t", 3), ("ws_up_t", 5)):
                            for m in range(NSH):
                                for k in range(KB):
                                    last = nc.tensor.matmul(bank[b0 + m // 2][:, m % 2 * S:(m % 2 + 1) * S], w[name][:, k, m * P:(m + 1) * P], xt[:, k, :], start=(k == 0), stop=(k == KB - 1))
                        last.then_inc(up_done, 1)
                    if 0 in stages:
                        pe.wait_ge(xf_ready, i * 2 + 2)
                        if 1 in stages:
                            pe.wait_ge(lg_ready, i)
                        for k in range(KB):
                            for s in range(SB):
                                last = nc.tensor.transpose(bank[1][:, k * S + s * P:k * S + (s + 1) * P], xf[:, s, k * P:(k + 1) * P], ident[:, :])
                        last.then_inc(xt_done, 1)
                        pe.wait_ge(xt_ready, i + 1)
                        for s in range(SB):
                            for k in range(KB):
                                last = nc.tensor.matmul(bank[2][:, s * NEXP:(s + 1) * NEXP], xt[:, k, s * P:(s + 1) * P], w["gate_t"][:, k, :], start=(k == 0), stop=(k == KB - 1))
                        last.then_inc(lg_done, 1)
                program(body, pe)


def route(nc, a, sb_, sem_, bank, rows_all, logits, slot, share, dispatched):
    ctx = ExitStack()
    with ctx:
        def sb(name, shape, dt=F32):
            return sb_(name, shape, dt, ctx)

        def sem(name):
            return sem_(name, ctx)

        top = sb("top_logit", [P, NT])
        expo = sb("expo", [P, NT, NEXP])
        total = sb("total", [P, NT])
        prob = sb("prob", [P, NT, NEXP])
        above = sb("above", [P, NT, NEXP * NEXP])
        equal = sb("equal", [P, NT, NEXP * NEXP])
        tie = sb("rank_tie", [P, NEXP * NEXP])
        rank = sb("rank", [P, NT, NEXP])
        picked = sb("picked", [P, NT, NEXP])
        picked_bf = sb("picked_bf", [P, NT * NEXP], BF16)
        earlier_f = sb("earlier_f", [P, P])
        earlier = sb("earlier", [P, P], BF16)
        ones = sb("ones_bf", [P, P], BF16)
        ones_row = sb("ones_nt", [P, NT])
        slot0 = sb("slot0", [P, NEXP])
        cum = sb("cum", [P, NT, NEXP])
        totals = sb("totals", [P, NT, NEXP])
        pos = sb("pos", [P, NT, NEXP])
        keep = sb("keep", [P, NT, NEXP])
        weight = sb("weight", [P, NT, NEXP])
        place = sb("place", [P, NT, NEXP])
        tmp = sb("tmp_route", [P, NT, NEXP])
        slot_f = sb("slot_f", [P, NT])
        loaded, fixed, step = sem("route_loaded"), sem("route_fixed"), sem("route_steps")
        exp_done, counted, routed, sent = sem("exp_done"), sem("counted"), sem("routed"), sem("sent")

        def over_tiles(row, n):
            return row.rearrange("p (o e) -> p o e", o=1).broadcast_to([P, NT, n])

        def over_experts(col):
            return col.rearrange("p (t o) -> p t o", o=1).broadcast_to([P, NT, NEXP])

        with nc.Block() as block:
            @block.sync
            def _(sp):
                sp.dma_start(tie[:, :], a["rank_tie"]).then_inc(loaded, 16)
                sp.dma_start(earlier_f[:, :], a["earlier"]).then_inc(loaded, 16)
                sp.dma_start(slot0[:, :], a["slot0"]).then_inc(loaded, 16)

            @block.scalar
            def _(act):
                act.wait_ge(step, 2)
                nc.scalar.activation(expo[:, :, :], tmp[:, :, :], ACT.Exp).then_inc(exp_done, 1)

            @block.tensor
            def _(pe):
                pe.wait_ge(fixed, 2)
                pe.wait_ge(step, 11)
                nc.tensor.matmul(bank[0][:, 0:NT * NEXP], earlier[:, :], picked_bf[:, :], start=True, stop=True)
                nc.tensor.matmul(bank[1][:, 0:NT * NEXP], ones[:, :], picked_bf[:, :], start=True, stop=True).then_inc(counted, 1)

            @block.gpsimd
            def _(pool):
                nc.gpsimd.memset(ones[:, :], 1.0).then_inc(fixed, 1)
                nc.gpsimd.memset(ones_row[:, :], 1.0).then_inc(fixed, 1)
                for k in range(2):
                    pool.wait_ge(routed, k + 1)
                    for n in range(NT):
                        nc.gpsimd.indirect_dma_start(out=dispatched, out_offset=bass.IndirectOffsetOnAxis(slot[k][:, n:n + 1], 0),
                                                     in_=rows_all[:, n // SB, n % SB, :], in_offset=None,
                                                     bounds_check=NSLOT - 1, oob_is_err=False).then_inc(sent, 16)
                pool.wait_ge(sent, 16 * 2 * NT)

            @block.vector
            def _(dve):
                done = 0

                def chain(ins):
                    nonlocal done
                    done += 1
                    ins.then_inc(step, 1)
                    dve.wait_ge(step, done)

                v = nc.vector
                chain(v.tensor_reduce(top[:, :], logits[:, :, :], AX.X, ALU.max))
                chain(v.tensor_tensor(tmp[:, :, :], logits[:, :, :], over_experts(top[:, :]), ALU.subtract))
                dve.wait_ge(exp_done, 1)
                chain(v.tensor_reduce(total[:, :], expo[:, :, :], AX.X, ALU.add))
                chain(v.reciprocal(top[:, :], total[:, :]))
                chain(v.tensor_tensor(prob[:, :, :], expo[:, :, :], over_experts(top[:, :]), ALU.mult))
                for n in range(NEXP):
                    mine = prob[:, :, n:n + 1].broadcast_to([P, NT, NEXP])
                    v.tensor_tensor(above[:, :, n * NEXP:(n + 1) * NEXP], prob[:, :, :], mine, ALU.is_gt)
                    v.tensor_tensor(equal[:, :, n * NEXP:(n + 1) * NEXP], prob[:, :, :], mine, ALU.is_equal)
                dve.drain()
                dve.wait_ge(loaded, 48)
                chain(v.tensor_tensor(equal[:, :, :], equal[:, :, :], over_tiles(tie[:, :], NEXP * NEXP), ALU.mult))
                chain(v.tensor_tensor(above[:, :, :], above[:, :, :], equal[:, :, :], ALU.add))
                chain(v.tensor_reduce(rank[:, :, :], above[:, :, :].rearrange("p t (e f) -> p t e f", e=NEXP), AX.X, ALU.add))
                chain(v.tensor_scalar(picked[:, :, :], rank[:, :, :], 2.0, None, ALU.is_lt))
                chain(v.tensor_copy(earlier[:, :], earlier_f[:, :]))
                chain(v.tensor_copy(picked_bf[:, :], picked[:, :, :].rearrange("p t e -> p (t e)")))
                chain(v.tensor_tensor(tmp[:, :, :], prob[:, :, :], picked[:, :, :], ALU.mult))
                chain(v.tensor_reduce(total[:, :], tmp[:, :, :], AX.X, ALU.add))
                chain(v.tensor_scalar(total[:, :], total[:, :], 1e-20, None, ALU.add))
                chain(v.reciprocal(top[:, :], total[:, :]))
                chain(v.tensor_tensor(weight[:, :, :], prob[:, :, :], over_experts(top[:, :]), ALU.mult))
                dve.wait_ge(counted, 1)
                dve.wait_ge(fixed, 2)
                chain(v.tensor_copy(totals[:, :, :].rearrange("p t e -> p (t e)"), bank[1][:, 0:NT * NEXP]))
                for n in range(NEXP):
                    v.tensor_tensor_scan(cum[:, :, n], ones_row[:, :], totals[:, :, n], 0.0, ALU.mult, ALU.add)
                dve.drain()
                chain(v.tensor_tensor(cum[:, :, :], cum[:, :, :], totals[:, :, :], ALU.subtract))
                chain(v.tensor_tensor(pos[:, :, :].rearrange("p t e -> p (t e)"), bank[0][:, 0:NT * NEXP], cum[:, :, :].rearrange("p t e -> p (t e)"), ALU.add))
                chain(v.tensor_scalar(keep[:, :, :], pos[:, :, :], float(CAP), None, ALU.is_lt))
                chain(v.tensor_tensor(weight[:, :, :], weight[:, :, :], keep[:, :, :], ALU.mult))
                chain(v.tensor_tensor(place[:, :, :], pos[:, :, :], over_tiles(slot0[:, :], NEXP), ALU.add))
                chain(v.tensor_scalar(place[:, :, :], place[:, :, :], float(NSLOT), None, ALU.subtract))
                chain(v.tensor_tensor(place[:, :, :], place[:, :, :], keep[:, :, :], ALU.mult))
                chain(v.tensor_scalar(place[:, :, :], place[:, :, :], float(NSLOT), None, ALU.add))
                for k in range(2):
                    chain(v.tensor_scalar(picked[:, :, :], rank[:, :, :], float(k), None, ALU.is_equal))
                    chain(v.tensor_tensor(tmp[:, :, :], place[:, :, :], picked[:, :, :], ALU.mult))
                    chain(v.tensor_reduce(slot_f[:, :], tmp[:, :, :], AX.X, ALU.add))
                    v.tensor_copy(slot[k][:, :], slot_f[:, :]).then_inc(routed, 1)
                    dve.wait_ge(routed, k + 1)
                    chain(v.tensor_tensor(tmp[:, :, :], weight[:, :, :], picked[:, :, :], ALU.mult))
                    chain(v.tensor_reduce(share[k][:, :], tmp[:, :, :], AX.X, ALU.add))


def routed_experts(nc, a, sb_, sem_, bank, ident, dispatched, expert_out):
    ctx = ExitStack()
    with ctx:
        def sb(name, shape, dt=F32):
            return sb_(name, shape, dt, ctx)

        def sem(name):
            return sem_(name, ctx)

        wg = [sb(f"expert_gate{q}", [P, KB, E]) for q in range(2)]
        wu = [sb(f"expert_up{q}", [P, KB, E]) for q in range(2)]
        wd = [sb(f"expert_down{q}", [P, KB, E]) for q in range(2)]
        xd = [sb(f"slots_in{q}", [P, 2, E]) for q in range(2)]
        xt = [sb(f"slots_t{q}", [P, KB, 256]) for q in range(2)]
        th = [sb(f"slots_th{q}", [P, KB, 256]) for q in range(2)]
        ga = [sb(f"slots_ga{q}", [P, KB, 256]) for q in range(2)]
        hid = [sb(f"slots_hid{q}", [P, KB, 256]) for q in range(2)]
        yo = [sb(f"slots_out{q}", [P, 2, E]) for q in range(2)]
        w_loaded = [sem(f"expert_loaded{q}") for q in range(2)]
        x_loaded = [sem(f"slots_loaded{q}") for q in range(2)]
        stored = [sem(f"slots_stored{q}") for q in range(2)]
        xt_done, xt_ready, up_done, th_ready = sem("et_done"), sem("et_ready"), sem("eup_done"), sem("eth_ready")
        ga_ready, hid_ready, down_done, y_ready = sem("ega_ready"), sem("ehid_ready"), sem("edown_done"), sem("ey_ready")
        NG = NEXP * ECH
        PAIR = 2 * ECH

        def flat(ap):
            return ap.rearrange("p k s -> p (k s)")

        def slots(ap):
            return ap.rearrange("(g k p) e -> p g k e", p=P, k=2)

        def program(body, eng):
            for j in range(PAIR):
                body(0, j)
            with eng.Fori(1, NEXP // 2) as turn:
                for j in range(PAIR):
                    body(turn, j)

        with nc.Block() as block:
            @block.sync
            def _(sp):
                def weights(turn, q):
                    e = turn * 2 + q
                    for tile, name in ((wg, "we_gate_t"), (wu, "we_up_t"), (wd, "we_down_t")):
                        sp.dma_start(tile[q][:, :, :], a[name].rearrange("e (k p) n -> p e k n", p=P)[:, e]).then_inc(w_loaded[q], 16)

                def body(turn, j):
                    g = turn * PAIR + j
                    first = isinstance(turn, int)
                    if j % ECH == 0:
                        q = j // ECH
                        if not first:
                            sp.wait_ge(down_done, turn * PAIR + (j - ECH))
                        weights(turn, q)
                    if not (first and j < 2):
                        sp.wait_ge(xt_done, g - 1)
                    sp.dma_start(xd[j % 2][:, :, :], slots(dispatched)[:, g]).then_inc(x_loaded[j % 2], 16)
                program(body, sp)

            @block.tensor
            def _(pe):
                def turn_over(g, j):
                    q = j % 2
                    n = g // 2 if isinstance(g, int) else None
                    return q, n

                def transposes(turn, j):
                    g = turn * PAIR + j
                    q = j % 2
                    pe.wait_ge(x_loaded[q], turn * (PAIR // 2 * 16) + (j // 2 + 1) * 16)
                    if not (isinstance(turn, int) and turn == 0 and j < 2):
                        pe.wait_ge(xt_ready, g - 1)
                    for k in range(KB):
                        for s in range(2):
                            last = nc.tensor.transpose(bank[0 + 7 * q][:, k * 256 + s * P:k * 256 + (s + 1) * P], xd[q][:, s, k * P:(k + 1) * P], ident[:, :])
                    last.then_inc(xt_done, 1)

                def gate_up(turn, j):
                    g = turn * PAIR + j
                    q, x = j % 2, j // ECH
                    if j % ECH == 0:
                        pe.wait_ge(w_loaded[x], turn * 48 + 48)
                    pe.wait_ge(xt_ready, g + 1)
                    if not (isinstance(turn, int) and turn == 0 and j < 2):
                        pe.wait_ge(hid_ready, g - 1)
                    for b0, tile in ((1, wg), (2, wu)):
                        for m in range(KB):
                            for k in range(KB):
                                last = nc.tensor.matmul(bank[b0 + 2 * q][:, m * 256:(m + 1) * 256], tile[x][:, k, m * P:(m + 1) * P], xt[q][:, k, :], start=(k == 0), stop=(k == KB - 1))
                    last.then_inc(up_done, 1)

                def down(turn, j):
                    g = turn * PAIR + j
                    q, x = j % 2, j // ECH
                    pe.wait_ge(hid_ready, g + 1)
                    if not (isinstance(turn, int) and turn == 0 and j < 2):
                        pe.wait_ge(y_ready, g - 1)
                    for s in range(2):
                        for m in range(KB):
                            last = nc.tensor.matmul(bank[5 + q][:, s * E:(s + 1) * E], hid[q][:, m, s * P:(s + 1) * P], wd[x][:, m, :], start=(m == 0), stop=(m == KB - 1))
                    last.then_inc(down_done, 1)

                transposes(0, 0)

                def run(turn, more):
                    for j in range(PAIR):
                        if j + 1 < PAIR:
                            transposes(turn, j + 1)
                        elif more:
                            transposes(turn + 1, 0)
                        gate_up(turn, j)
                        if j > 0:
                            down(turn, j - 1)
                        elif not (isinstance(turn, int) and turn == 0):
                            down(turn - 1, PAIR - 1)

                run(0, True)
                with pe.Fori(1, NEXP // 2 - 1) as turn:
                    run(turn, True)
                run(NEXP // 2 - 1, False)
                down(NEXP // 2 - 1, PAIR - 1)

            @block.scalar
            def _(act):
                def move_in(g, q, first):
                    act.wait_ge(xt_done, g + 1)
                    if not first:
                        act.wait_ge(up_done, g - 1)
                    nc.scalar.activation(flat(xt[q][:, :, :]), bank[0 + 7 * q][:, :], ACT.Copy).then_inc(xt_ready, 1)

                move_in(0, 0, True)

                def run(turn, more):
                    start = isinstance(turn, int) and turn == 0
                    for j in range(PAIR):
                        g, q = turn * PAIR + j, j % 2
                        if j + 1 < PAIR or more:
                            move_in(g + 1, 1 - q, start and j < 1)
                        act.wait_ge(up_done, g + 1)
                        if not (start and j < 2):
                            act.wait_ge(ga_ready, g - 1)
                        nc.scalar.activation(flat(th[q][:, :, :]), bank[1 + 2 * q][:, :], ACT.Tanh, scale=0.5).then_inc(th_ready, 1)
                        if not (start and j == 0):
                            act.wait_ge(down_done, g)
                            if not (start and j < 3):
                                n = turn * (PAIR // 2 * 16) + (j - 1) // 2 * 16
                                act.wait_ge(stored[1 - q], n)
                            nc.scalar.activation(flat(yo[1 - q][:, :, :]), bank[5 + 1 - q][:, :], ACT.Copy).then_inc(y_ready, 1)
                            act.wait_ge(y_ready, g)
                            act.dma_start(slots(expert_out[0:NSLOT, :])[:, g - 1], yo[1 - q][:, :, :]).then_inc(stored[1 - q], 16)

                run(0, True)
                with act.Fori(1, NEXP // 2 - 1) as turn:
                    run(turn, True)
                run(NEXP // 2 - 1, False)
                act.wait_ge(down_done, NG)
                act.wait_ge(stored[1], (NG // 2 - 1) * 16)
                nc.scalar.activation(flat(yo[1][:, :, :]), bank[6][:, :], ACT.Copy).then_inc(y_ready, 1)
                act.wait_ge(y_ready, NG)
                act.dma_start(slots(expert_out[0:NSLOT, :])[:, NG - 1], yo[1][:, :, :]).then_inc(stored[1], 16)
                act.wait_ge(stored[0], NG // 2 * 16)
                act.wait_ge(stored[1], NG // 2 * 16)

            @block.vector
            def _(dve):
                def body(turn, j):
                    g, q = turn * PAIR + j, j % 2
                    start = isinstance(turn, int)
                    dve.wait_ge(th_ready, g + 1)
                    nc.vector.scalar_tensor_tensor(flat(ga[q][:, :, :]), flat(th[q][:, :, :]), 1.0, bank[1 + 2 * q][:, :], ALU.add, ALU.mult).then_inc(ga_ready, 1)
                    dve.wait_ge(ga_ready, g + 1)
                    if not (start and j < 2):
                        dve.wait_ge(down_done, g - 1)
                    nc.vector.scalar_tensor_tensor(flat(hid[q][:, :, :]), flat(ga[q][:, :, :]), 0.5, bank[2 + 2 * q][:, :], ALU.mult, ALU.mult).then_inc(hid_ready, 1)
                program(body, dve)


def combine(nc, sb_, sem_, resid, slot, share, expert_out, out):
    ctx = ExitStack()
    with ctx:
        NBUF = 4
        rows = [[sb_(f"picked_rows{k}{q}", [P, E], F32, ctx) for q in range(NBUF)] for k in range(2)]
        fetched = [[sem_(f"fetched{k}{q}", ctx) for q in range(NBUF)] for k in range(2)]
        added, stored = sem_("added", ctx), sem_("out_stored", ctx)

        with nc.Block() as block:
            @block.gpsimd
            def _(pool):
                for n in range(NT):
                    for k in range(2):
                        if n >= NBUF:
                            pool.wait_ge(added, 2 * (n - NBUF) + k + 1)
                        nc.gpsimd.indirect_dma_start(out=rows[k][n % NBUF][:, :], out_offset=None, in_=expert_out,
                                                     in_offset=bass.IndirectOffsetOnAxis(slot[k][:, n:n + 1], 0)).then_inc(fetched[k][n % NBUF], 16)

            @block.vector
            def _(dve):
                for n in range(NT):
                    for k in range(2):
                        dve.wait_ge(fetched[k][n % NBUF], 16 * (n // NBUF + 1))
                        if k == 1:
                            dve.wait_ge(added, 2 * n + 1)
                        tile = resid[:, n // SB, n % SB, :]
                        nc.vector.scalar_tensor_tensor(tile, rows[k][n % NBUF][:, :], share[k][:, n:n + 1], tile, ALU.mult, ALU.add).then_inc(added, 1)

            @block.sync
            def _(sp):
                view = out.rearrange("b (k p) e -> p b k e", p=P)
                with sp.Fori(0, B) as i:
                    sp.wait_ge(added, i * (2 * SB) + 2 * SB)
                    sp.dma_start(view[:, i], resid[:, i]).then_inc(stored, 16)
                sp.wait_ge(stored, 16 * B)


def kernel(**inputs):
    import numpy as _np
    import concourse.bacc as _bacc
    from concourse import mybir as _mybir
    from concourse.bass_utils import run_bass_kernel_spmd as _run

    g = {k: _np.asarray(v) for k, v in inputs.items()}
    arrays = {
        "x": g["x"],
        "ctx_t": g["ctx_1024"].transpose(0, 2, 1).reshape(B, KB, P, S).transpose(0, 2, 1, 3),
        "wq_t": g["L0_attn_wq"].T, "wk_t": g["L0_attn_wk"].T, "wv_t": g["L0_attn_wv"].T, "wo_t": g["L0_attn_wo"].T,
        "bq": g["L0_attn_bq"], "bk": g["L0_attn_bk"], "bv": g["L0_attn_bv"], "bo": g["L0_attn_bo"],
        "freq_filter": g["L0_attn_freq_filter"].reshape(-1),
        "ln_gamma": g["L0_attn_ln_gamma"], "ln_beta": g["L0_attn_ln_beta"],
        "wi_t": g["L0_xattn_Wi"].T, "wg_t": g["L0_xattn_Wg"].T, "a_t": g["L0_xattn_A"].T, "bm_t": g["L0_xattn_Bm"].T,
        "wxo_t": g["L0_xattn_Wo"].T, "bi": g["L0_xattn_bi"], "bg": g["L0_xattn_bg"], "bxo": g["L0_xattn_bo"],
        "decay": _np.repeat(g["L0_xattn_decay"].reshape(-1), E // HEADS),
        "gate_t": g["L0_ffn_gate_w"].T,
        "we_gate_t": g["L0_ffn_we_gate"].transpose(0, 2, 1), "we_up_t": g["L0_ffn_we_up"].transpose(0, 2, 1),
        "we_down_t": g["L0_ffn_we_down"].transpose(0, 2, 1),
        "ws_gate_t": g["L0_ffn_ws_gate"].T, "ws_up_t": g["L0_ffn_ws_up"].T, "ws_down_t": g["L0_ffn_ws_down"].T,
    }
    arrays.update(dft_constants())
    arrays.update(misc_constants())
    arrays = {k: _np.ascontiguousarray(v) for k, v in arrays.items()}
    nc = _bacc.Bacc("TRN2", target_bir_lowering=False, num_devices=1)
    args = {k: nc.dram_tensor(f"in_{k}", v.shape, _mybir.dt.from_np(v.dtype), kind="ExternalInput").ap() for k, v in arrays.items()}
    out = nc.dram_tensor("out_0", (B, S, E), F32, kind="ExternalOutput").ap()
    build(nc, args, out)
    r = _run(nc, [{f"in_{k}": v for k, v in arrays.items()}], core_ids=[0])
    return r.results[0]["out_0"]
```

```python
from contextlib import ExitStack

import numpy as np

import concourse.bass as bass
from concourse import mybir

P = 128
B, S, E = 16, 256, 256
KB = E // P
SB = S // P
NF = S // 2
HEADS = 16
EPS = 1e-5
F32 = mybir.dt.float32
BF16 = mybir.dt.bfloat16
F16 = mybir.dt.float16
U32 = mybir.dt.uint32
ALU = mybir.AluOpType
ACT = mybir.ActivationFunctionType
AX = mybir.AxisListType


def dft_constants():
    t = np.arange(S, dtype=np.float64)
    f = np.arange(NF, dtype=np.float64)
    ang = 2 * np.pi / S * ((np.outer(t, f)) % S)
    nyq = 1.0 - 2.0 * (t % 2)
    weight = np.where(f == 0, 1.0, 2.0)
    sin = np.sin(ang)
    sin[:, 0] = nyq
    forward = np.concatenate([np.cos(ang), sin], 1)
    inverse = np.concatenate([weight * np.cos(ang), np.where(f == 0, 1.0, 2.0) * sin], 1).T / S
    sym = np.cos(ang[:NF]).T
    minus0 = weight[:, None] * (sym - 1.0) / S
    nyq_minus0 = (nyq[:NF] - 1.0) / S
    last_minus0 = weight * ((1.0 - 2.0 * (f % 2)) - 1.0) / S
    tw = np.where(t[:NF] == 0, 1.0, 2.0)
    even = tw[:, None] * np.cos(ang[:NF])
    even_ny = even.copy()
    even_ny[:, 0] = tw * nyq[:NF]
    last = 1.0 - 2.0 * (f % 2)
    row = np.concatenate([nyq_minus0, last])[None, :]
    col = last_minus0[:, None]
    mask = np.where(f == 0, 0.0, 1.0)[:, None]
    cast = lambda a: np.ascontiguousarray(a, dtype=np.float32)
    return {
        "forward": cast(forward), "inverse": cast(inverse),
        "minus0": cast(minus0), "evens": cast(np.concatenate([even, even_ny], 1)),
        "rows": cast(row), "cols": cast(np.concatenate([col, mask], 1)),
    }


def misc_constants():
    k = np.arange(P)
    return {
        "ident": np.eye(P, dtype=np.float32),
        "earlier": (k[:, None] < k[None, :]).astype(np.float32),
        "dc3": np.repeat(np.where(np.arange(P) == 0, float(S), 0.0)[None, :], 3, 0).astype(np.float32),
        "eye3": np.eye(3, dtype=np.float32),
        "rank_tie": np.broadcast_to((np.arange(8)[:, None] > np.arange(8)[None, :]).astype(np.float32).reshape(1, 64), (P, 64)).copy(),
        "slot0": np.broadcast_to((np.arange(8) * CAP).astype(np.float32)[None, :], (P, 8)).copy(),
    }


NEXP = 8
CAP = 1280
NT = B * SB
CH = 16
UP = 2.0 ** 14
NSH = 4
NSLOT = NEXP * CAP
NEARLY = 8
ECH = CAP // 256


def build(nc, a, out):
    ctx = ExitStack()
    with ctx:
        def sb(name, shape, dt=F32, stack=ctx):
            return stack.enter_context(nc.sbuf_tensor(name, shape, dt))

        def sem(name, stack=ctx):
            return stack.enter_context(nc.semaphore(name))

        bank = [ctx.enter_context(nc.psum_tensor(f"bank{i}", [P, 512], F32)) for i in range(8)]
        resid = sb("resid", [P, B, SB, E])
        tok2 = sb("tok2", [P, B * SB * E])
        tok3 = sb("tok3", [P, B * SB * E])
        ln_x = tok2[:, :].rearrange("p (b k e) -> p b k e", b=B, k=SB)
        gate_all = tok2[:, :].rearrange("p (k b s) -> p k b s", k=KB, b=B)
        inp_all = tok3[:, :].rearrange("p (k b s) -> p k b s", k=KB, b=B)
        mhalf = sb("mhalf", [P, 2])

        w = {name: sb(name, [P, KB, E]) for name in ("wi_t", "wg_t", "a_t", "bm_t", "wxo_t")}
        w["ws_gate_t"] = sb("ws_gate_t", [P, KB, NSH * P])
        w["ws_up_t"] = sb("ws_up_t", [P, KB, NSH * P])
        w["ws_down_t"] = sb("ws_down_t", [P, NSH, E])
        w["gate_t"] = sb("gate_t", [P, KB, NEXP])
        cols = {name: sb("col_" + name, [P, KB]) for name in ("bi", "bg", "decay")}
        ident = sb("ident", [P, P])
        dispatched = nc.dram_tensor("dispatched", (NSLOT, E), F32, kind="Internal").ap()
        expert_out = nc.dram_tensor("expert_out", (NSLOT + P, E), F32, kind="Internal").ap()
        ones3 = sb("ones3", [3, P], BF16)
        bias_parts = sb("bias_parts", [3, 5 * E], BF16)

        attention(nc, a, sb, sem, bank, resid, ln_x, mhalf, inp_all, w, cols, ident, ones3, bias_parts, dispatched, expert_out)
        recurrence_inputs(nc, sb, sem, bank, resid, gate_all, inp_all, mhalf, w, cols, ident)
        recurrence(nc, sb, sem, bank, gate_all, inp_all, w)
        ffn(nc, a, sb, sem, bank, resid, ln_x, inp_all, mhalf, out, w, ident, ones3, bias_parts, dispatched, expert_out)


def attention(nc, a, sb_, sem_, bank, resid, ln_x, mhalf, ctx_all, later_w, later_cols, ident, ones3, bias_parts, dispatched, expert_out):
    ctx = ExitStack()
    with ctx:
        def sb(name, shape, dt=F32):
            return sb_(name, shape, dt, ctx)

        def sem(name):
            return sem_(name, ctx)

        wqk = sb("wqk", [P, KB, 2 * E])
        wv = sb("wv", [P, KB, E])
        wo = sb("wo", [P, KB, E])
        fwd = sb("fwd", [P, SB, 2 * NF])
        inv = sb("inv", [P, 2, S])
        minus0 = sb("minus0", [P, NF])
        evens = sb("evens", [P, 2 * NF])
        rows = sb("rows", [1, 2 * NF])
        cols = sb("cols", [P, 2])
        gamma = sb("gamma", [P, E])
        beta = sb("beta", [P, E])
        filt = sb("filt", [P, 2 * E])
        bias3 = sb("bias3", [3, 5 * E])
        bias_hi = sb("bias_hi", [3, 5 * E], BF16)
        bias_mid = sb("bias_mid", [3, 5 * E], BF16)
        bias_lo = sb("bias_lo", [3, 5 * E], BF16)
        bias_r = sb("bias_r", [3, 5 * E])
        bias_p = sb("bias_p", [3, 5 * E])
        dc3f = sb("dc3f", [3, P])
        dc3 = sb("dc3", [3, P], BF16)
        eye3 = sb("eye3", [3, 3])
        one = sb("one", [1, 1])
        st1 = sb("st1", [P, SB, 6])
        mv1 = sb("mv1", [P, SB, 2])
        ve1 = sb("ve1", [P, SB])
        rstd1 = sb("rstd1", [P, SB])
        xn = sb("xn", [P, SB, E])
        fxt = sb("fxt", [P, KB, 2 * NF])
        sqc = sb("sqc", [P, 2 * E])
        sqs = sb("sqs", [P, 2 * E])
        mag = sb("mag", [P, 2 * E])
        p2 = sb("p2", [P, 2 * E])
        pm = sb("pm", [P, E])
        pn = sb("pn", [1, E])
        em = sb("em", [P, E])
        en = sb("en", [1, E])
        vs = sb("vs", [P, 2, E])
        gs = sb("gs", [P, 2, E])
        rz = sb("rz", [P, KB])
        zrow = sb("zrow", [1, E])
        ot = sb("ot", [P, KB, S])
        hh = sb("hh", [P, SB, E])
        tt = sb("tt", [P, SB, E])
        st2 = sb("st2", [P, SB, 6])
        mv2 = sb("mv2", [P, SB, 2])
        ve2 = sb("ve2", [P, SB])
        rstd2 = sb("rstd2", [P, SB])

        waited = sem("waited")
        loaded = sem("weights_loaded")
        rows_loaded = sem("rows_loaded")
        x_loaded = sem("x_loaded")
        fixed = sem("constants_ready")
        prep = sem("bias_steps")
        scaled = sem("filter_applied")
        ln1_stats, ln1_aggr, ln1_ve, ln1_rstd = sem("ln1_stats"), sem("ln1_aggr"), sem("ln1_ve"), sem("ln1_rstd")
        xn_ready, xn_saved = sem("xn_ready"), sem("xn_saved")
        dft_done, fx_copied, qk_done, v_done, v_copied = sem("dft_done"), sem("fx_copied"), sem("qk_done"), sem("v_done"), sem("v_copied")
        sq_done, mag_done, p2_done, p_ready, a_done = sem("sq_done"), sem("mag_done"), sem("p2_done"), sem("p_ready"), sem("a_done")
        e_ready, A_done, g_ready, rz_ready = sem("e_ready"), sem("A_done"), sem("g_ready"), sem("rz_ready")
        zrow_ready, z_turned = sem("zrow_ready"), sem("z_turned")
        ot_done, ot_ready, y_done, h_ready = sem("ot_done"), sem("ot_ready"), sem("y_done"), sem("h_ready")
        ln2_stats, ln2_aggr, ln2_ve, ln2_rstd = sem("ln2_stats"), sem("ln2_aggr"), sem("ln2_ve"), sem("ln2_rstd")
        bx_ready, t_ready, x2_ready = sem("bx_ready"), sem("t_ready"), sem("x2_ready")

        def kxm(w):
            return w.rearrange("(k p) n -> p k n", p=P)

        def bcast(v, n):
            return v.rearrange("(o n) -> o n", o=1).broadcast_to([n, v.shape[0]])

        later = sem("later_loaded")
        zeros_ready, zero_stored = sem("zeros_ready"), sem("zero_stored")
        zeros = sb("zeros", [P, 8 * E])

        NLOAD = 10

        def program(body, eng):
            body(0, front=True, back=False, ahead=True)
            with eng.Fori(1, B - 1) as i:
                body(i, front=True, back=True, ahead=True)
            body(B - 1, front=True, back=True, ahead=False)
            body(B, front=False, back=True, ahead=False)

        with nc.Block() as block:
            @block.sync
            def _(sp):
                sp.dma_start(resid[:, 0], a["x"][0].rearrange("(k p) e -> p k e", p=P)).then_inc(x_loaded, 16)
                sp.dma_start(fwd[:, :, :], kxm(a["forward"])).then_inc(loaded, 16)
                sp.dma_start(wqk[:, :, 0:E], kxm(a["wq_t"])).then_inc(loaded, 16)
                sp.dma_start(wqk[:, :, E:2 * E], kxm(a["wk_t"])).then_inc(loaded, 16)
                sp.dma_start(wv[:, :, :], kxm(a["wv_t"])).then_inc(loaded, 16)
                sp.dma_start(wo[:, :, :], kxm(a["wo_t"])).then_inc(loaded, 16)
                sp.dma_start(inv[:, :, :], kxm(a["inverse"])).then_inc(loaded, 16)
                sp.dma_start(minus0[:, :], a["minus0"]).then_inc(loaded, 16)
                sp.dma_start(evens[:, :], a["evens"]).then_inc(loaded, 16)
                sp.dma_start(rows[:, :], a["rows"]).then_inc(loaded, 16)
                sp.dma_start(cols[:, :], a["cols"]).then_inc(loaded, 16)
                with sp.Fori(1, B) as i:
                    sp.wait_ge(x_loaded, i * 16)
                    sp.dma_start(resid[:, i], a["x"].rearrange("b (k p) e -> p b k e", p=P)[:, i]).then_inc(x_loaded, 16)
                for k in range(KB):
                    sp.dma_start(ctx_all[:, k], a["ctx_t"].rearrange("b p k s -> k p b s")[k]).then_inc(later, 16)
                for name, tile in later_w.items():
                    sp.dma_start(tile[:, :, :], kxm(a[name])).then_inc(later, 16)
                for name, tile in later_cols.items():
                    sp.dma_start(tile[:, :], a[name].rearrange("(k p) -> p k", p=P), allow_slow_non_contiguous=True).then_inc(later, 16)
                sp.dma_start(ident[:, :], a["ident"]).then_inc(later, 16)
                sp.wait_ge(zeros_ready, 1)
                with sp.Fori(0, NSLOT // (P * 8)) as r:
                    sp.dma_start(dispatched.rearrange("(r p j) e -> p r (j e)", p=P, j=8)[:, r, :], zeros[:, :]).then_inc(zero_stored, 16)
                sp.dma_start(expert_out[NSLOT:NSLOT + P, :], zeros[:, 0:E]).then_inc(zero_stored, 16)
                sp.wait_ge(zero_stored, 16 * (NSLOT // (P * 8) + 1))
                sp.wait_ge(later, 16 * (KB + len(later_w) + len(later_cols) + 1))

            @block.gpsimd
            def _(pool):
                nc.gpsimd.memset(zeros[:, :], 0.0).then_inc(zeros_ready, 1)
                nc.gpsimd.memset(mhalf[:, :], -0.5).then_inc(fixed, 1)
                nc.gpsimd.memset(ones3[:, :], 1.0).then_inc(fixed, 1)
                nc.gpsimd.memset(one[:, :], 1.0).then_inc(fixed, 1)
                pool.wait_ge(fixed, 3)

                def deviation1(i):
                    pool.wait_ge(ln1_aggr, (i + 1) * 2)
                    pool.sem_inc(waited, 1)
                    nc.gpsimd.tensor_scalar(ve1[:, :], mv1[:, :, 1], EPS, None, ALU.add).then_inc(ln1_ve, 1)
                    pool.wait_ge(ln1_ve, i + 1)
                    nc.gpsimd.tensor_tensor(rstd1[:, :], ve1[:, :], mhalf[:, :], ALU.pow).then_inc(ln1_rstd, 1)

                def body(i, front, back, ahead):
                    if front:
                        pool.wait_ge(xn_ready, (i + 1) * 2)
                        nc.gpsimd.tensor_copy(ln_x[:, i], xn[:, :, :]).then_inc(xn_saved, 1)
                    if ahead:
                        deviation1(i + 1)
                    if back:
                        j = i - 1
                        nc.gpsimd.tensor_tensor(resid[:, j], resid[:, j], beta[:, :].rearrange("p (o e) -> p o e", o=1).broadcast_to([P, SB, E]), ALU.add).then_inc(bx_ready, 1)
                        pool.wait_ge(ln2_aggr, (j + 1) * 2)
                        pool.sem_inc(waited, 1)
                        nc.gpsimd.tensor_scalar(ve2[:, :], mv2[:, :, 1], EPS, None, ALU.add).then_inc(ln2_ve, 1)
                        pool.wait_ge(ln2_ve, j + 1)
                        nc.gpsimd.tensor_tensor(rstd2[:, :], ve2[:, :], mhalf[:, :], ALU.pow).then_inc(ln2_rstd, 1)
                pool.wait_ge(loaded, 16 * NLOAD)
                pool.wait_ge(rows_loaded, 16 * (NLOAD + 1))
                deviation1(0)
                program(body, pool)

            @block.scalar
            def _(act):
                act.dma_start(gamma[:, :], bcast(a["ln_gamma"], P)).then_inc(rows_loaded, 16)
                act.dma_start(beta[:, :], bcast(a["ln_beta"], P)).then_inc(rows_loaded, 16)
                for h in range(2):
                    act.dma_start(filt[:, h * E:(h + 1) * E], bcast(a["freq_filter"], P)).then_inc(rows_loaded, 16)
                for n, v in enumerate(("bq", "bk", "bv", "bo", "bxo")):
                    act.dma_start(bias3[:, n * E:(n + 1) * E], bcast(a[v], 3)).then_inc(rows_loaded, 16)
                act.dma_start(dc3f[:, :], a["dc3"]).then_inc(rows_loaded, 16)
                act.dma_start(eye3[:, :], a["eye3"]).then_inc(rows_loaded, 16)

                def body(i, front, back, ahead):
                    j = i - 1
                    if front:
                        act.wait_ge(dft_done, i + 1)
                        if back:
                            act.wait_ge(v_done, i)
                        nc.scalar.activation(fxt[:, :, :].rearrange("p k f -> p (k f)"), bank[0][:, :], ACT.Copy).then_inc(fx_copied, 1)
                    if back:
                        act.wait_ge(a_done, j + 1)
                        nc.scalar.activation(em[:, :], bank[4][:, 0:E], ACT.Exp).then_inc(e_ready, 1)
                        nc.scalar.activation(en[:, :], bank[4][0:1, E:2 * E], ACT.Exp).then_inc(e_ready, 1)
                    if front:
                        act.wait_ge(qk_done, i + 1)
                        if back:
                            act.wait_ge(p2_done, 2 * i)
                        nc.scalar.activation(sqc[:, :], bank[1][:, :], ACT.Square).then_inc(sq_done, 1)
                        nc.scalar.activation(sqs[:, :], bank[2][:, :], ACT.Square).then_inc(sq_done, 1)
                        act.wait_ge(p2_done, i * 2 + 2)
                        if back:
                            act.wait_ge(a_done, i)
                        nc.scalar.activation(pm[:, :], p2[:, 0:E], ACT.Sqrt).then_inc(p_ready, 1)
                        nc.scalar.activation(pn[:, :], p2[0:1, E:2 * E], ACT.Sqrt).then_inc(p_ready, 1)
                    if back:
                        act.wait_ge(ot_done, j + 1)
                        act.wait_ge(rz_ready, j + 1)
                        for n in range(KB):
                            nc.scalar.activation(ot[:, n, :], bank[6][:, n * S:(n + 1) * S], ACT.Copy, scale=rz[:, n:n + 1]).then_inc(ot_ready, 1)
                    if front:
                        act.wait_ge(v_done, i + 1)
                        if back:
                            act.wait_ge(g_ready, i)
                        nc.scalar.activation(vs[:, :, :].rearrange("p k f -> p (k f)"), bank[3][:, :], ACT.Copy).then_inc(v_copied, 1)
                program(body, act)

            @block.vector
            def _(dve):
                dve.sem_inc(h_ready, 1)
                dve.wait_ge(fixed, 3)
                dve.wait_ge(loaded, 16 * NLOAD)
                dve.wait_ge(rows_loaded, 16 * (NLOAD + 1))
                nc.vector.tensor_tensor(bias3[:, 0:2 * E], bias3[:, 0:2 * E], filt[0:3, :], ALU.mult).then_inc(prep, 1)
                nc.vector.tensor_copy(dc3[:, :], dc3f[:, :]).then_inc(prep, 1)
                dve.wait_ge(prep, 2)
                nc.vector.tensor_copy(bias_hi[:, :], bias3[:, :]).then_inc(prep, 1)
                dve.wait_ge(prep, 3)
                nc.vector.tensor_tensor(bias_r[:, :], bias3[:, :], bias_hi[:, :], ALU.subtract).then_inc(prep, 1)
                dve.wait_ge(prep, 4)
                nc.vector.tensor_copy(bias_mid[:, :], bias_r[:, :]).then_inc(prep, 1)
                dve.wait_ge(prep, 5)
                nc.vector.tensor_tensor(bias3[:, :], bias_r[:, :], bias_mid[:, :], ALU.subtract).then_inc(prep, 1)
                dve.wait_ge(prep, 6)
                nc.vector.tensor_copy(bias_lo[:, :], bias3[:, :]).then_inc(prep, 1)
                dve.wait_ge(prep, 7)
                nc.vector.tensor_scalar(bias_r[:, :], bias_hi[:, :], eye3[:, 0:1], None, ALU.mult).then_inc(prep, 1)
                dve.wait_ge(prep, 8)
                nc.vector.scalar_tensor_tensor(bias_p[:, :], bias_mid[:, :], eye3[:, 1:2], bias_r[:, :], ALU.mult, ALU.add).then_inc(prep, 1)
                dve.wait_ge(prep, 9)
                nc.vector.scalar_tensor_tensor(bias_parts[:, :], bias_lo[:, :], eye3[:, 2:3], bias_p[:, :], ALU.mult, ALU.add).then_inc(prep, 1)
                for k in range(KB):
                    nc.vector.tensor_tensor(wqk[:, k, :], wqk[:, k, :], filt[:, :], ALU.mult).then_inc(scaled, 1)

                def stats1(i):
                    dve.wait_ge(x_loaded, (i + 1) * 16)
                    for k in range(SB):
                        nc.vector.bn_stats(st1[:, k, :], resid[:, i, k, :]).then_inc(ln1_stats, 1)

                def layernorm1(i, first):
                    dve.wait_ge(ln1_stats, (i + 1) * 2)
                    if not first:
                        dve.wait_ge(ln1_rstd, i)
                    dve.sem_inc(waited, 1)
                    for k in range(SB):
                        nc.vector.bn_aggr(mv1[:, k, :], st1[:, k, :]).then_inc(ln1_aggr, 1)
                    dve.wait_ge(ln1_rstd, i + 1)
                    if not first:
                        dve.wait_ge(dft_done, i)
                        dve.wait_ge(xn_saved, i)
                    for k in range(SB):
                        nc.vector.tensor_scalar(xn[:, k, :], resid[:, i, k, :], mv1[:, k, 0:1], rstd1[:, k:k + 1], ALU.subtract, ALU.mult).then_inc(xn_ready, 1)

                def body(i, front, back, ahead):
                    j = i - 1
                    if front:
                        dve.wait_ge(sq_done, i * 2 + 2)
                        nc.vector.scalar_tensor_tensor(mag[:, :], sqs[:, :], cols[:, 1:2], sqc[:, :], ALU.mult, ALU.add).then_inc(mag_done, 1)
                        if back:
                            dve.wait_ge(p_ready, 2 * i)
                        nc.vector.tensor_tensor(p2[0:1, E:2 * E], sqs[0:1, 0:E], sqs[0:1, E:2 * E], ALU.mult).then_inc(p2_done, 1)
                        dve.wait_ge(mag_done, i + 1)
                        nc.vector.tensor_tensor(p2[:, 0:E], mag[:, 0:E], mag[:, E:2 * E], ALU.mult).then_inc(p2_done, 1)
                    if back:
                        dve.wait_ge(A_done, j + 1)
                        dve.wait_ge(v_copied, j + 1)
                        nc.vector.tensor_tensor(gs[:, :, :].rearrange("p k f -> p (k f)"), bank[5][:, :], vs[:, :, :].rearrange("p k f -> p (k f)"), ALU.mult).then_inc(g_ready, 1)
                        nc.vector.tensor_copy(zrow[:, :], bank[5][0:1, 0:E]).then_inc(zrow_ready, 1)
                    if ahead:
                        stats1(i + 1)
                    if back:
                        dve.wait_ge(z_turned, j + 1)
                        nc.vector.reciprocal(rz[:, :], bank[4][:, 0:KB]).then_inc(rz_ready, 1)
                    if ahead:
                        layernorm1(i + 1, False)
                    if back:
                        dve.wait_ge(y_done, j + 1)
                        dve.wait_ge(xn_saved, j + 1)
                        nc.vector.tensor_tensor(hh[:, :, :].rearrange("p k e -> p (k e)"), bank[7][:, :], ln_x[:, j].rearrange("p k e -> p (k e)"), ALU.add).then_inc(h_ready, 1)
                        dve.wait_ge(h_ready, j + 2)
                        for k in range(SB):
                            nc.vector.bn_stats(st2[:, k, :], hh[:, k, :]).then_inc(ln2_stats, 1)
                        dve.wait_ge(ln2_stats, j * 2 + 2)
                        dve.sem_inc(waited, 1)
                        for k in range(SB):
                            nc.vector.bn_aggr(mv2[:, k, :], st2[:, k, :]).then_inc(ln2_aggr, 1)
                        dve.wait_ge(ln2_aggr, j * 2 + 2)
                        for k in range(SB):
                            nc.vector.scalar_tensor_tensor(tt[:, k, :], hh[:, k, :], mv2[:, k, 0:1], gamma[:, :], ALU.subtract, ALU.mult).then_inc(t_ready, 1)
                        dve.wait_ge(t_ready, j * 2 + 2)
                        dve.wait_ge(ln2_rstd, j + 1)
                        dve.wait_ge(bx_ready, j + 1)
                        for k in range(SB):
                            nc.vector.scalar_tensor_tensor(resid[:, j, k, :], tt[:, k, :], rstd2[:, k:k + 1], resid[:, j, k, :], ALU.mult, ALU.add).then_inc(x2_ready, 1)
                        dve.wait_ge(x2_ready, j * 2 + 2)
                stats1(0)
                layernorm1(0, True)
                program(body, dve)

            @block.tensor
            def _(pe):
                pe.wait_ge(loaded, 16 * NLOAD)
                pe.wait_ge(rows_loaded, 16 * (NLOAD + 1))
                pe.wait_ge(prep, 10)
                pe.wait_ge(scaled, KB)

                def body(i, front, back, ahead):
                    j = i - 1
                    if front:
                        pe.wait_ge(xn_ready, i * 2 + 2)
                        if back:
                            pe.wait_ge(fx_copied, i)
                        for m in range(KB):
                            for k in range(SB):
                                last = nc.tensor.matmul(bank[0][:, m * S:(m + 1) * S], xn[:, k, m * P:(m + 1) * P], fwd[:, k, :], start=(k == 0), stop=(k == SB - 1))
                        last.then_inc(dft_done, 1)
                    if back:
                        pe.wait_ge(p_ready, j * 2 + 2)
                        nc.tensor.matmul(bank[4][:, 0:E], minus0[:, :], pm[:, :], start=True, stop=False)
                        nc.tensor.matmul(bank[4][:, 0:E], rows[:, 0:NF], pn[:, :], start=False, stop=True)
                        nc.tensor.matmul(bank[4][0:1, E:2 * E], cols[:, 0:1], pm[:, :], start=True, stop=True).then_inc(a_done, 1)
                    if front:
                        pe.wait_ge(fx_copied, i + 1)
                        if back:
                            pe.wait_ge(sq_done, 2 * i)
                        for f in range(2):
                            for k in range(KB):
                                last = nc.tensor.matmul(bank[1 + f][:, :], fxt[:, k, f * P:(f + 1) * P], wqk[:, k, :], start=(k == 0), stop=(k == KB - 1 and f == 1))
                            if f == 0:
                                nc.tensor.matmul(bank[1][:, :], dc3[:, :], bias_parts[:, 0:2 * E], start=False, stop=True)
                        last.then_inc(qk_done, 1)
                    if back:
                        pe.wait_ge(e_ready, j * 2 + 2)
                        for h in range(2):
                            nc.tensor.matmul(bank[5][:, h * E:(h + 1) * E], evens[:, h * NF:(h + 1) * NF], em[:, :], start=True, stop=False)
                            last = nc.tensor.matmul(bank[5][:, h * E:(h + 1) * E], rows[:, NF:2 * NF], en[:, :], start=False, stop=True)
                        last.then_inc(A_done, 1)

                    def v_half(f):
                        for k in range(KB):
                            last = nc.tensor.matmul(bank[3][:, f * E:(f + 1) * E], fxt[:, k, f * P:(f + 1) * P], wv[:, k, :], start=(k == 0), stop=(k == KB - 1 and f == 1))
                        if f == 0:
                            last = nc.tensor.matmul(bank[3][:, 0:E], dc3[:, :], bias_parts[:, 2 * E:3 * E], start=False, stop=True)
                        return last

                    if front:
                        if back:
                            pe.wait_ge(v_copied, i)
                        v_half(0)
                    if back:
                        pe.wait_ge(g_ready, j + 1)
                        for n in range(KB):
                            for f in range(2):
                                last = nc.tensor.matmul(bank[6][:, n * S:(n + 1) * S], gs[:, f, n * P:(n + 1) * P], inv[:, f, :], start=(f == 0), stop=(f == 1))
                            if n == 0:
                                pe.wait_ge(zrow_ready, j + 1)
                                pe.sem_inc(waited, 1)
                                for m in range(KB):
                                    turned = nc.tensor.transpose(bank[4][:, m:m + 1], zrow[:, m * P:(m + 1) * P], one[:, :])
                                turned.then_inc(z_turned, 1)
                        last.then_inc(ot_done, 1)
                    if front:
                        v_half(1).then_inc(v_done, 1)
                    if back:
                        pe.wait_ge(ot_ready, j * 2 + 2)
                        pe.wait_ge(h_ready, j + 1)
                        for s in range(SB):
                            for k in range(KB):
                                nc.tensor.matmul(bank[7][:, s * E:(s + 1) * E], ot[:, k, s * P:(s + 1) * P], wo[:, k, :], start=(k == 0), stop=False)
                            last = nc.tensor.matmul(bank[7][:, s * E:(s + 1) * E], ones3[:, :], bias_parts[:, 3 * E:4 * E], start=False, stop=True)
                        last.then_inc(y_done, 1)
                program(body, pe)


def recurrence_inputs(nc, sb_, sem_, bank, resid, gate_all, inp_all, mhalf, w, cols, ident):
    ctx = ExitStack()
    with ctx:
        def sb(name, shape, dt=F32):
            return sb_(name, shape, dt, ctx)

        def sem(name):
            return sem_(name, ctx)

        st = sb("st", [P, SB, 6])
        mv = sb("mv", [P, SB, 2])
        ve = sb("ve", [P, SB])
        rstd = sb("rstd", [P, SB])
        xq = sb("xq", [P, SB, E])
        decay = sb("decay_row", [P, KB, S])
        ones = sb("ones_row", [P, S])
        hbg = sb("hbg", [P, KB])
        sq = sb("sq", [P, KB, S])
        sums = sb("sums", [P, KB, S])
        ret = sb("ret", [P, KB, S])
        th = sb("th", [P, KB, S])
        waited = sem("waited2")
        fixed, halved = sem("ones_ready"), sem("rows_ready")
        ln_stats, ln_aggr, ln_ve, ln_rstd = sem("q_stats"), sem("q_aggr"), sem("q_ve"), sem("q_rstd")
        xq_ready, xt_done, sq_ready, sums_ready, ret_ready = sem("xq_ready"), sem("xt_done"), sem("sq_ready"), sem("sums_ready"), sem("ret_ready")
        inp_done, inp_ready, z_done, th_ready, gate_ready = sem("inp_done"), sem("inp_ready"), sem("z_done"), sem("th_ready"), sem("gate_ready")

        def program(body, eng):
            body(0, (0,))
            body(1, (0, 1))
            body(2, (0, 1, 2))
            body(3, (0, 1, 2, 3))
            with eng.Fori(4, B) as i:
                body(i, (0, 1, 2, 3))
            body(B, (1, 2, 3))
            body(B + 1, (2, 3))
            body(B + 2, (3,))

        with nc.Block() as block:
            @block.gpsimd
            def _(pool):
                nc.gpsimd.memset(ones[:, :], 1.0).then_inc(fixed, 1)

                def body(i, stages):
                    if 0 in stages:
                        if 1 in stages:
                            pool.wait_ge(sums_ready, i * 2)
                        nc.gpsimd.tensor_tensor(sq[:, :, :], inp_all[:, :, i, :], inp_all[:, :, i, :], ALU.mult).then_inc(sq_ready, 1)
                        pool.wait_ge(ln_aggr, i * 2 + 2)
                        pool.sem_inc(waited, 1)
                        nc.gpsimd.tensor_scalar(ve[:, :], mv[:, :, 1], EPS, None, ALU.add).then_inc(ln_ve, 1)
                        pool.wait_ge(ln_ve, i + 1)
                        nc.gpsimd.tensor_tensor(rstd[:, :], ve[:, :], mhalf[:, :], ALU.pow).then_inc(ln_rstd, 1)
                program(body, pool)

            @block.vector
            def _(dve):
                dve.wait_ge(fixed, 1)
                for k in range(KB):
                    nc.vector.tensor_scalar(decay[:, k, :], ones[:, :], cols["decay"][:, k:k + 1], None, ALU.mult).then_inc(halved, 1)
                nc.vector.tensor_scalar(hbg[:, :], cols["bg"][:, :], 0.5, None, ALU.mult).then_inc(halved, 1)
                dve.wait_ge(halved, 3)

                def body(i, stages):
                    if 0 in stages:
                        for k in range(SB):
                            nc.vector.bn_stats(st[:, k, :], resid[:, i, k, :]).then_inc(ln_stats, 1)
                        dve.wait_ge(ln_stats, i * 2 + 2)
                        dve.sem_inc(waited, 1)
                        for k in range(SB):
                            nc.vector.bn_aggr(mv[:, k, :], st[:, k, :]).then_inc(ln_aggr, 1)
                    if 1 in stages:
                        dve.wait_ge(xt_done, i)
                        dve.wait_ge(sums_ready, i * 2)
                        if 2 in stages:
                            dve.wait_ge(inp_done, i - 1)
                        nc.vector.tensor_tensor(ret[:, :, :].rearrange("p k s -> p (k s)"), bank[0][:, :], sums[:, :, :].rearrange("p k s -> p (k s)"), ALU.mult).then_inc(ret_ready, 1)
                    if 0 in stages:
                        dve.wait_ge(sq_ready, i + 1)
                        if 1 in stages:
                            dve.wait_ge(ret_ready, i)
                        for k in range(KB):
                            nc.vector.tensor_tensor_scan(sums[:, k, :], decay[:, k, :], sq[:, k, :], 0.0, ALU.mult, ALU.add).then_inc(sums_ready, 1)
                        dve.wait_ge(ln_rstd, i + 1)
                        for k in range(SB):
                            nc.vector.tensor_scalar(xq[:, k, :], resid[:, i, k, :], mv[:, k, 0:1], rstd[:, k:k + 1], ALU.subtract, ALU.mult).then_inc(xq_ready, 1)
                    if 3 in stages:
                        dve.wait_ge(th_ready, i * 2 - 4)
                        nc.vector.tensor_scalar(gate_all[:, :, i - 3, :], th[:, :, :], 0.5 * UP, 0.5 * UP, ALU.mult, ALU.add).then_inc(gate_ready, 1)
                program(body, dve)

            @block.scalar
            def _(act):
                act.wait_ge(halved, 3)

                def body(i, stages):
                    if 2 in stages:
                        act.wait_ge(inp_done, i - 1)
                        act.sem_inc(waited, 1)
                        for n in range(KB):
                            nc.scalar.activation(inp_all[:, n, i - 2, :], bank[1][:, n * S:(n + 1) * S], ACT.Identity, bias=cols["bi"][:, n:n + 1]).then_inc(inp_ready, 1)
                    if 3 in stages:
                        act.wait_ge(z_done, i - 2)
                        if not isinstance(i, int) or i > 3:
                            act.wait_ge(gate_ready, i - 3)
                        for n in range(KB):
                            nc.scalar.activation(th[:, n, :], bank[2][:, n * S:(n + 1) * S], ACT.Tanh, bias=hbg[:, n:n + 1], scale=0.5).then_inc(th_ready, 1)
                program(body, act)

            @block.tensor
            def _(pe):
                def body(i, stages):
                    if 2 in stages:
                        pe.wait_ge(ret_ready, i - 1)
                        if 3 in stages:
                            pe.wait_ge(inp_ready, i * 2 - 4)
                        for n in range(KB):
                            for k in range(KB):
                                last = nc.tensor.matmul(bank[1][:, n * S:(n + 1) * S], w["wi_t"][:, k, n * P:(n + 1) * P], ret[:, k, :], start=(k == 0), stop=(k == KB - 1))
                        last.then_inc(inp_done, 1)
                    if 1 in stages:
                        pe.wait_ge(xq_ready, i * 2)
                        for k in range(KB):
                            for s in range(SB):
                                last = nc.tensor.transpose(bank[0][:, k * S + s * P:k * S + (s + 1) * P], xq[:, s, k * P:(k + 1) * P], ident[:, :])
                        last.then_inc(xt_done, 1)
                    if 3 in stages:
                        pe.wait_ge(inp_ready, i * 2 - 4)
                        if not isinstance(i, int) or i > 3:
                            pe.wait_ge(th_ready, i * 2 - 6)
                        for n in range(KB):
                            for k in range(KB):
                                last = nc.tensor.matmul(bank[2][:, n * S:(n + 1) * S], w["wg_t"][:, k, n * P:(n + 1) * P], inp_all[:, k, i - 3, :], start=(k == 0), stop=(k == KB - 1))
                        last.then_inc(z_done, 1)
                program(body, pe)


def recurrence(nc, sb_, sem_, bank, gate_all, state_all, w):
    ctx = ExitStack()
    NCH = S // CH
    W = KB * B
    with ctx:
        def sb(name, shape, dt=F32):
            return sb_(name, shape, dt, ctx)

        def sem(name):
            return sem_(name, ctx)

        gate = [sb(f"gate_chunk{q}", [P, CH, KB, B]) for q in range(2)]
        inp = [sb(f"inp_chunk{q}", [P, CH, KB, B]) for q in range(2)]
        prod = sb("prod_chunk", [P, CH, KB, B])
        gate_next = sb("gate_next", [P, CH, KB, B])
        gated = sem("gates_ready")
        a_down = sb("a_down", [P, KB, E])
        a_rest = [sb(f"a_rest{i}", [P, KB, E]) for i in range(2)]
        a_part = [sb(f"a_part{i}", [P, KB, E], BF16) for i in range(3)]
        rest = [sb(f"rest_chunk{q}", [P, CH, KB, B]) for q in range(2)]
        state = [sb(f"state_chunk{q}", [P, CH, KB, B]) for q in range(2)]
        blend = sb("blend", [P, KB, B])
        blend_hi = sb("blend_hi", [P, KB, B], F16)
        blend_lo = sb("blend_lo", [P, KB, B], F16)
        split = sem("a_split")
        hi_ready, lo_ready = sem("blend_hi_ready"), sem("blend_lo_ready")
        acc = [bank[3 + q][:, :].rearrange("p (t n b) -> p t n b", t=CH, n=KB) for q in range(2)]
        waited = sem("waited3")
        staged, step_staged, prodded = sem("chunk_staged"), sem("chunk_copied"), sem("prod_ready")
        blended, stepped, tanh_done, saved = sem("blended"), sem("stepped"), sem("tanh_done"), sem("states_saved")
        zeroed = sem("state_zeroed")
        laid = sem("inputs_laid")

        def program(chunk, eng):
            with eng.Fori(0, NCH // 2 - 1) as h:
                chunk(h * 2, 0, True, True)
                chunk(h * 2 + 1, 1, True, True)
            chunk(NCH - 2, 0, True, False)
            chunk(NCH - 1, 1, False, False)

        with nc.Block() as block:
            @block.gpsimd
            def _(pool):
                def stage(c, q):
                    if not isinstance(c, int) or c > 0:
                        pool.wait_ge(gated, c)
                        pool.sem_inc(waited, 1)
                    for k in range(KB):
                        nc.gpsimd.tensor_copy(gate_next[:, :, k, :], gate_all[:, k, :, bass.ts(c, CH)].rearrange("p b t -> p t b")).then_inc(step_staged, 1)
                        nc.gpsimd.tensor_copy(inp[q][:, :, k, :], state_all[:, k, :, bass.ts(c, CH)].rearrange("p b t -> p t b")).then_inc(step_staged, 1)
                    pool.wait_ge(step_staged, c * 4 + 4)
                    pool.sem_inc(waited, 1)
                    nc.gpsimd.tensor_scalar(prod[:, :, :, :], gate_next[:, :, :, :], -1.0, UP, ALU.mult, ALU.add).then_inc(prodded, 1)
                    pool.wait_ge(prodded, c + 1)
                    nc.gpsimd.tensor_tensor(rest[q][:, :, :, :], inp[q][:, :, :, :], prod[:, :, :, :], ALU.mult).then_inc(staged, 1)

                def gates(q):
                    nc.gpsimd.tensor_copy(gate[q][:, :, :, :], gate_next[:, :, :, :]).then_inc(gated, 1)

                nc.gpsimd.memset(state[1][:, CH - 1], 0.0).then_inc(zeroed, 1)
                for _ in range(2):
                    pool.sem_inc(saved, 1)
                for q in range(2):
                    stage(q, q)
                    gates(q)

                def chunk(c, q, more, two):
                    if two:
                        pool.wait_ge(stepped, c * CH + 1)
                        pool.sem_inc(waited, 1)
                        stage(c + 2, q)
                    pool.wait_ge(tanh_done, c * CH + (CH + 1))
                    pool.sem_inc(waited, 1)
                    if two:
                        gates(q)
                    for k in range(KB):
                        last = nc.gpsimd.tensor_copy(state_all[:, k, :, bass.ts(c, CH)].rearrange("p b t -> p t b"), state[q][:, :, k, :])
                        if k < KB - 1:
                            last.then_inc(waited, 1)
                    last.then_inc(saved, 1)
                program(chunk, pool)

            @block.tensor
            def _(pe):
                def pieces(q):
                    for t in range(0, CH, CH // 2):
                        for n in range(KB):
                            for lhs, rhs in ((w["bm_t"], inp[q]), (a_down, rest[q])):
                                for k in range(KB):
                                    first = t == 0 and n == 0 and k == 0 and lhs is not a_down
                                    yield nc.tensor.matmul(acc[q][:, t:t + CH // 2, n, :], lhs[:, k, n * P:(n + 1) * P], rhs[:, t:t + CH // 2, k, :],
                                                           start=first, stop=False, skip_group_check=True)

                pe.wait_ge(split, 6)
                pe.wait_ge(staged, 1)
                for _ in pieces(0):
                    pass

                def chunk(c, q, more, two):
                    ahead = pieces(1 - q) if more else iter(())
                    for t in range(CH):
                        for part, (ready, operand, count) in enumerate(((hi_ready, blend_hi, 3), (lo_ready, blend_lo, 2))):
                            pe.wait_ge(ready, c * CH + (t + 1))
                            for n in range(KB):
                                for i in range(count):
                                    for k in range(KB):
                                        last = nc.tensor.matmul(acc[q][:, t, n, :], a_part[i][:, k, n * P:(n + 1) * P], operand[:, k, :],
                                                                start=False, stop=False, skip_group_check=True)
                        last.then_inc(stepped, 1)
                        if more:
                            if t == 0:
                                pe.wait_ge(staged, c + 2)
                            next(ahead)
                program(chunk, pe)

            @block.vector
            def _(dve):
                nc.vector.tensor_scalar(a_down[:, :, :], w["a_t"][:, :, :], 1.0 / UP, None, ALU.mult).then_inc(split, 1)
                before = a_down
                for i in range(3):
                    dve.wait_ge(split, 2 * i + 1)
                    nc.vector.tensor_copy(a_part[i][:, :, :], before[:, :, :]).then_inc(split, 1)
                    if i < 2:
                        dve.wait_ge(split, 2 * i + 2)
                        nc.vector.tensor_tensor(a_rest[i][:, :, :], before[:, :, :], a_part[i][:, :, :], ALU.subtract).then_inc(split, 1)
                        before = a_rest[i]

                def flat(ap):
                    return ap.rearrange("p k b -> p (k b)")

                def chunk(c, q, more, two):
                    for t in range(CH):
                        before = state[q][:, t - 1] if t else state[1 - q][:, CH - 1]
                        if t == 0:
                            dve.wait_ge(gated, c + 1)
                        dve.wait_ge(tanh_done, c * CH + (t + 1))
                        nc.vector.tensor_tensor(flat(blend_hi[:, :, :]), flat(gate[q][:, t]), flat(before), ALU.mult).then_inc(hi_ready, 1)
                        nc.vector.tensor_tensor(flat(blend[:, :, :]), flat(gate[q][:, t]), flat(before), ALU.mult).then_inc(blended, 1)
                        dve.wait_ge(blended, c * CH + (t + 1))
                        nc.vector.tensor_tensor(flat(blend_lo[:, :, :]), flat(blend[:, :, :]), flat(blend_hi[:, :, :]), ALU.subtract).then_inc(lo_ready, 1)
                program(chunk, dve)

            @block.scalar
            def _(act):
                act.wait_ge(zeroed, 1)
                act.sem_inc(tanh_done, 1)

                def chunk(c, q, more, two):
                    for t in range(CH):
                        if t == 0:
                            act.wait_ge(saved, c + 1)
                        act.wait_ge(stepped, c * CH + (t + 1))
                        nc.scalar.activation(state[q][:, t].rearrange("p k b -> p (k b)"), acc[q][:, t].rearrange("p n b -> p (n b)"), ACT.Tanh).then_inc(tanh_done, 1)
                program(chunk, act)


def ffn(nc, a, sb, sem, bank, resid, rows_all, state_all, mhalf, out, w, ident, ones3, bias_parts, dispatched, expert_out):
    ctx = ExitStack()
    with ctx:
        logits = sb("logits", [P, NT, NEXP], F32, ctx)
        slot = [sb(f"slot_rank{k}", [P, NT], U32, ctx) for k in range(2)]
        share = [sb(f"share_rank{k}", [P, NT], F32, ctx) for k in range(2)]
        with ExitStack() as own:
            shared = shared_experts(nc, lambda name, shape: sb(name, shape, F32, own), lambda name: sem(name, own), bank, resid, state_all, w)
            project_states(nc, sb, sem, bank, resid, rows_all, state_all, mhalf, w, ident, ones3, bias_parts, logits, shared)
            route_and_share(nc, a, sb, sem, bank, rows_all, logits, slot, share, dispatched, shared)
        routed_experts(nc, a, sb, sem, bank, ident, dispatched, expert_out)
        combine(nc, sb, sem, resid, slot, share, expert_out, out)


def shared_experts(nc, sb, sem, bank, resid, xt_all, w):
    th = [sb(f"shared_th{h}", [P, 2, S]) for h in range(2)]
    ga = [sb(f"shared_ga{h}", [P, 2, S]) for h in range(2)]
    hid = [sb(f"shared_hid{h}", [P, 2, S]) for h in range(2)]
    up_done, th_ready, ga_ready, hid_ready, down_done, added = sem("up_done"), sem("f_th_ready"), sem("ga_ready"), sem("hid_ready"), sem("down_done"), sem("sh_added")

    def flat(ap):
        return ap.rearrange("p k s -> p (k s)")

    def gate_up(pe, i, h, first):
        if not first:
            pe.wait_ge(hid_ready, i * 2 + (h - 1))
        for name, b0 in (("ws_gate_t", 3), ("ws_up_t", 5)):
            for m in range(2):
                for k in range(KB):
                    last = nc.tensor.matmul(bank[b0 + h][:, m * S:(m + 1) * S], w[name][:, k, (2 * h + m) * P:(2 * h + m + 1) * P], xt_all[:, k, i, :], start=(k == 0), stop=(k == KB - 1))
        last.then_inc(up_done, 1)

    def down(pe, i):
        pe.wait_ge(hid_ready, i * 2)
        pe.wait_ge(added, i)
        for s in range(SB):
            for m in range(NSH):
                last = nc.tensor.matmul(bank[7][:, s * E:(s + 1) * E], hid[m // 2][:, m % 2, s * P:(s + 1) * P], w["ws_down_t"][:, m, :], start=(m == 0), stop=(m == NSH - 1))
        last.then_inc(down_done, 1)

    def tanh(act, i, h):
        act.wait_ge(up_done, i * 2 + (h + 1))
        nc.scalar.activation(flat(th[h][:, :, :]), bank[3 + h][:, :], ACT.Tanh, scale=0.5).then_inc(th_ready, 1)

    def gated(dve, i, h):
        dve.wait_ge(th_ready, i * 2 + (h + 1))
        nc.vector.scalar_tensor_tensor(flat(ga[h][:, :, :]), flat(th[h][:, :, :]), 1.0, bank[3 + h][:, :], ALU.add, ALU.mult).then_inc(ga_ready, 1)

    def hidden(dve, i, h):
        dve.wait_ge(ga_ready, i * 2 + (h + 1))
        nc.vector.scalar_tensor_tensor(flat(hid[h][:, :, :]), flat(ga[h][:, :, :]), 0.5, bank[5 + h][:, :], ALU.mult, ALU.mult).then_inc(hid_ready, 1)

    def add(dve, i):
        dve.wait_ge(down_done, i)
        nc.vector.tensor_tensor(flat(resid[:, i - 1]), bank[7][:, :], flat(resid[:, i - 1]), ALU.add).then_inc(added, 1)

    def bank7_starts_free(dve):
        dve.sem_inc(added, 1)

    return gate_up, down, tanh, gated, hidden, add, bank7_starts_free


def project_states(nc, sb_, sem_, bank, resid, rows_all, state_all, mhalf, w, ident, ones3, bias_parts, logits, shared):
    ctx = ExitStack()
    with ctx:
        def sb(name, shape, dt=F32):
            return sb_(name, shape, dt, ctx)

        def sem(name):
            return sem_(name, ctx)

        stt = sb("states_tile", [P, KB, S])
        bxo_parts = bias_parts[:, 4 * E:5 * E]
        st = sb("st3", [P, SB, 6])
        mv = sb("mv3", [P, SB, 2])
        ve = sb("ve3", [P, SB])
        rstd = sb("rstd3", [P, SB])
        xf = sb("xf", [P, SB, E])
        xt = sb("xt", [P, KB, S])
        waited = sem("waited4")
        st_ready, y_done, x_ready = sem("st_ready"), sem("yx_done"), sem("x3_ready")
        ln_stats, ln_aggr, ln_ve, ln_rstd = sem("f_stats"), sem("f_aggr"), sem("f_ve"), sem("f_rstd")
        xf_ready, xf_saved, xt_done, xt_ready, lg_done, lg_ready = sem("xf_ready"), sem("xf_saved"), sem("xft_done"), sem("xft_ready"), sem("logits_done"), sem("logits_ready")

        def program(body, eng):
            body(0, (0,))
            body(1, (0, 1))
            body(2, (0, 1, 2))
            body(3, (0, 1, 2, 3))
            body(4, (0, 1, 2, 3, 4))
            with eng.Fori(5, NEARLY + 4) as i:
                body(i, (0, 1, 2, 3, 4, 5))
            with eng.Fori(NEARLY + 4, B) as i:
                body(i, (0, 1, 2, 3))
            body(B, (1, 2, 3))
            body(B + 1, (2, 3))
            body(B + 2, (3,))

        gate_up, down, tanh, gated, hidden, add, bank7_starts_free = shared

        def flat(ap):
            return ap.rearrange("p k s -> p (k s)")

        with nc.Block() as block:
            @block.gpsimd
            def _(pool):
                def body(i, stages):
                    if 1 in stages:
                        pool.wait_ge(ln_aggr, i * 2)
                        pool.sem_inc(waited, 1)
                        nc.gpsimd.tensor_scalar(ve[:, :], mv[:, :, 1], EPS, None, ALU.add).then_inc(ln_ve, 1)
                        pool.wait_ge(ln_ve, i)
                        nc.gpsimd.tensor_tensor(rstd[:, :], ve[:, :], mhalf[:, :], ALU.pow).then_inc(ln_rstd, 1)
                program(body, pool)

            @block.scalar
            def _(act):
                def body(i, stages):
                    if 0 in stages:
                        if 1 in stages:
                            act.wait_ge(y_done, i)
                        nc.scalar.activation(stt[:, :, :], state_all[:, :, i, :], ACT.Copy).then_inc(st_ready, 1)
                    if 4 in stages:
                        tanh(act, i - 4, 0)
                    if 1 in stages:
                        act.wait_ge(xf_ready, i * 2)
                        act.sem_inc(waited, 1)
                        nc.scalar.activation(rows_all[:, i - 1], xf[:, :, :], ACT.Copy).then_inc(xf_saved, 1)
                    if 2 in stages:
                        act.wait_ge(xt_done, i - 1)
                        if 3 in stages:
                            act.wait_ge(lg_done, i - 2)
                        nc.scalar.activation(flat(xt[:, :, :]), bank[1][:, :], ACT.Copy).then_inc(xt_ready, 1)
                        nc.scalar.activation(state_all[:, :, i - 2, :], bank[1][:, :].rearrange("p (k s) -> p k s", k=KB), ACT.Copy).then_inc(xt_ready, 1)
                    if 4 in stages:
                        tanh(act, i - 4, 1)
                program(body, act)

            @block.vector
            def _(dve):
                bank7_starts_free(dve)

                def body(i, stages):
                    if 1 in stages:
                        dve.wait_ge(y_done, i)
                        nc.vector.tensor_tensor(flat(resid[:, i - 1]), bank[0][:, :], flat(resid[:, i - 1]), ALU.add).then_inc(x_ready, 1)
                        dve.wait_ge(x_ready, i)
                        dve.sem_inc(waited, 1)
                        for k in range(SB):
                            nc.vector.bn_stats(st[:, k, :], resid[:, i - 1, k, :]).then_inc(ln_stats, 1)
                        dve.wait_ge(ln_stats, i * 2)
                        dve.sem_inc(waited, 1)
                        for k in range(SB):
                            nc.vector.bn_aggr(mv[:, k, :], st[:, k, :]).then_inc(ln_aggr, 1)
                    if 4 in stages:
                        gated(dve, i - 4, 0)
                    if 3 in stages and 4 not in stages:
                        dve.wait_ge(lg_done, i - 2)
                        nc.vector.tensor_copy(logits[:, bass.ts(i - 3, SB), :].rearrange("p s e -> p (s e)"), bank[2][:, 0:SB * NEXP]).then_inc(lg_ready, 1)
                    if 1 in stages:
                        dve.wait_ge(ln_rstd, i)
                        if 2 in stages:
                            dve.wait_ge(xt_done, i - 1)
                            dve.wait_ge(xf_saved, i - 1)
                        for k in range(SB):
                            nc.vector.tensor_scalar(xf[:, k, :], resid[:, i - 1, k, :], mv[:, k, 0:1], rstd[:, k:k + 1], ALU.subtract, ALU.mult).then_inc(xf_ready, 1)
                    if 5 in stages:
                        add(dve, i - 4)
                    if 4 in stages:
                        hidden(dve, i - 4, 0)
                        dve.wait_ge(lg_done, i - 2)
                        nc.vector.tensor_copy(logits[:, bass.ts(i - 3, SB), :].rearrange("p s e -> p (s e)"), bank[2][:, 0:SB * NEXP]).then_inc(lg_ready, 1)
                        gated(dve, i - 4, 1)
                        hidden(dve, i - 4, 1)
                program(body, dve)

            @block.tensor
            def _(pe):
                def body(i, stages):
                    if 1 in stages:
                        pe.wait_ge(st_ready, i)
                        if 2 in stages:
                            pe.wait_ge(x_ready, i - 1)
                        for s in range(SB):
                            for k in range(KB):
                                nc.tensor.matmul(bank[0][:, s * E:(s + 1) * E], stt[:, k, s * P:(s + 1) * P], w["wxo_t"][:, k, :], start=(k == 0), stop=False)
                            last = nc.tensor.matmul(bank[0][:, s * E:(s + 1) * E], ones3[:, :], bxo_parts[:, :], start=False, stop=True)
                        last.then_inc(y_done, 1)
                    if 4 in stages:
                        gate_up(pe, i - 4, 0, 5 not in stages)
                    if 2 in stages:
                        pe.wait_ge(xf_ready, i * 2 - 2)
                        if 3 in stages:
                            pe.wait_ge(xt_ready, i * 2 - 4)
                        for k in range(KB):
                            for s in range(SB):
                                last = nc.tensor.transpose(bank[1][:, k * S + s * P:k * S + (s + 1) * P], xf[:, s, k * P:(k + 1) * P], ident[:, :])
                        last.then_inc(xt_done, 1)
                    if 5 in stages:
                        down(pe, i - 4)
                    if 3 in stages:
                        pe.wait_ge(xt_ready, i * 2 - 4)
                        if not isinstance(i, int) or i > 3:
                            pe.wait_ge(lg_ready, i - 3)
                        for s in range(SB):
                            for k in range(KB):
                                last = nc.tensor.matmul(bank[2][:, s * NEXP:(s + 1) * NEXP], xt[:, k, s * P:(s + 1) * P], w["gate_t"][:, k, :], start=(k == 0), stop=(k == KB - 1))
                        last.then_inc(lg_done, 1)
                    if 4 in stages:
                        gate_up(pe, i - 4, 1, 5 not in stages)
                program(body, pe)


def route_and_share(nc, a, sb_, sem_, bank, rows_all, logits, slot, share, dispatched, shared):
    ctx = ExitStack()
    with ctx:
        def sb(name, shape, dt=F32):
            return sb_(name, shape, dt, ctx)

        def sem(name):
            return sem_(name, ctx)

        top = sb("top_logit", [P, NT])
        expo = sb("expo", [P, NT, NEXP])
        total = sb("total", [P, NT])
        prob = sb("prob", [P, NT, NEXP])
        above = sb("above", [P, NT, NEXP * NEXP])
        equal = sb("equal", [P, NT, NEXP * NEXP])
        tie = sb("rank_tie", [P, NEXP * NEXP])
        rank = sb("rank", [P, NT, NEXP])
        picked = sb("picked", [P, NT, NEXP])
        picked_bf = sb("picked_bf", [P, NT * NEXP], BF16)
        earlier_f = sb("earlier_f", [P, P])
        earlier = sb("earlier", [P, P], BF16)
        ones = sb("ones_bf", [P, P], BF16)
        ones_row = sb("ones_nt", [P, NT])
        slot0 = sb("slot0", [P, NEXP])
        cum = sb("cum", [P, NT, NEXP])
        totals = sb("totals", [P, NT, NEXP])
        pos = sb("pos", [P, NT, NEXP])
        keep = sb("keep", [P, NT, NEXP])
        weight = sb("weight", [P, NT, NEXP])
        place = sb("place", [P, NT, NEXP])
        tmp = sb("tmp_route", [P, NT, NEXP])
        slot_f = sb("slot_f", [P, NT])
        gate_up, down, tanh, gated, hidden, add, _ = shared

        def program(body, eng):
            with eng.Fori(NEARLY, B) as i:
                body(i, True)
            body(B, False)

        loaded, fixed, step = sem("route_loaded"), sem("route_fixed"), sem("route_steps")
        exp_done, counted, routed, sent = sem("exp_done"), sem("counted"), sem("routed"), sem("sent")

        def over_tiles(row, n):
            return row.rearrange("p (o e) -> p o e", o=1).broadcast_to([P, NT, n])

        def over_experts(col):
            return col.rearrange("p (t o) -> p t o", o=1).broadcast_to([P, NT, NEXP])

        with nc.Block() as block:
            @block.sync
            def _(sp):
                sp.dma_start(tie[:, :], a["rank_tie"]).then_inc(loaded, 16)
                sp.dma_start(earlier_f[:, :], a["earlier"]).then_inc(loaded, 16)
                sp.dma_start(slot0[:, :], a["slot0"]).then_inc(loaded, 16)

            @block.scalar
            def _(act):
                act.wait_ge(step, 2)
                nc.scalar.activation(expo[:, :, :], tmp[:, :, :], ACT.Exp).then_inc(exp_done, 1)

                def body(i, up):
                    if up:
                        for h in range(2):
                            tanh(act, i, h)
                program(body, act)

            @block.tensor
            def _(pe):
                pe.wait_ge(fixed, 2)
                pe.wait_ge(step, 11)
                nc.tensor.matmul(bank[0][:, 0:NT * NEXP], earlier[:, :], picked_bf[:, :], start=True, stop=True)
                nc.tensor.matmul(bank[1][:, 0:NT * NEXP], ones[:, :], picked_bf[:, :], start=True, stop=True).then_inc(counted, 1)

                def body(i, up):
                    if up:
                        gate_up(pe, i, 0, False)
                    down(pe, i)
                    if up:
                        gate_up(pe, i, 1, False)
                program(body, pe)

            @block.gpsimd
            def _(pool):
                nc.gpsimd.memset(ones[:, :], 1.0).then_inc(fixed, 1)
                nc.gpsimd.memset(ones_row[:, :], 1.0).then_inc(fixed, 1)
                for k in range(2):
                    pool.wait_ge(routed, k + 1)
                    for n in range(NT):
                        nc.gpsimd.indirect_dma_start(out=dispatched, out_offset=bass.IndirectOffsetOnAxis(slot[k][:, n:n + 1], 0),
                                                     in_=rows_all[:, n // SB, n % SB, :], in_offset=None,
                                                     bounds_check=NSLOT - 1, oob_is_err=False).then_inc(sent, 16)
                pool.wait_ge(sent, 16 * 2 * NT)

            @block.vector
            def _(dve):
                done = 0

                def chain(ins):
                    nonlocal done
                    done += 1
                    ins.then_inc(step, 1)
                    dve.wait_ge(step, done)

                v = nc.vector
                chain(v.tensor_reduce(top[:, :], logits[:, :, :], AX.X, ALU.max))
                chain(v.tensor_tensor(tmp[:, :, :], logits[:, :, :], over_experts(top[:, :]), ALU.subtract))
                dve.wait_ge(exp_done, 1)
                chain(v.tensor_reduce(total[:, :], expo[:, :, :], AX.X, ALU.add))
                chain(v.reciprocal(top[:, :], total[:, :]))
                chain(v.tensor_tensor(prob[:, :, :], expo[:, :, :], over_experts(top[:, :]), ALU.mult))
                for n in range(NEXP):
                    mine = prob[:, :, n:n + 1].broadcast_to([P, NT, NEXP])
                    v.tensor_tensor(above[:, :, n * NEXP:(n + 1) * NEXP], prob[:, :, :], mine, ALU.is_gt)
                    v.tensor_tensor(equal[:, :, n * NEXP:(n + 1) * NEXP], prob[:, :, :], mine, ALU.is_equal)
                dve.drain()
                dve.wait_ge(loaded, 48)
                chain(v.tensor_tensor(equal[:, :, :], equal[:, :, :], over_tiles(tie[:, :], NEXP * NEXP), ALU.mult))
                chain(v.tensor_tensor(above[:, :, :], above[:, :, :], equal[:, :, :], ALU.add))
                chain(v.tensor_reduce(rank[:, :, :], above[:, :, :].rearrange("p t (e f) -> p t e f", e=NEXP), AX.X, ALU.add))
                chain(v.tensor_scalar(picked[:, :, :], rank[:, :, :], 2.0, None, ALU.is_lt))
                chain(v.tensor_copy(earlier[:, :], earlier_f[:, :]))
                chain(v.tensor_copy(picked_bf[:, :], picked[:, :, :].rearrange("p t e -> p (t e)")))
                chain(v.tensor_tensor(tmp[:, :, :], prob[:, :, :], picked[:, :, :], ALU.mult))
                chain(v.tensor_reduce(total[:, :], tmp[:, :, :], AX.X, ALU.add))
                chain(v.tensor_scalar(total[:, :], total[:, :], 1e-20, None, ALU.add))
                chain(v.reciprocal(top[:, :], total[:, :]))
                chain(v.tensor_tensor(weight[:, :, :], prob[:, :, :], over_experts(top[:, :]), ALU.mult))
                dve.wait_ge(counted, 1)
                dve.wait_ge(fixed, 2)
                chain(v.tensor_copy(totals[:, :, :].rearrange("p t e -> p (t e)"), bank[1][:, 0:NT * NEXP]))
                for n in range(NEXP):
                    v.tensor_tensor_scan(cum[:, :, n], ones_row[:, :], totals[:, :, n], 0.0, ALU.mult, ALU.add)
                dve.drain()
                chain(v.tensor_tensor(cum[:, :, :], cum[:, :, :], totals[:, :, :], ALU.subtract))
                chain(v.tensor_tensor(pos[:, :, :].rearrange("p t e -> p (t e)"), bank[0][:, 0:NT * NEXP], cum[:, :, :].rearrange("p t e -> p (t e)"), ALU.add))
                chain(v.tensor_scalar(keep[:, :, :], pos[:, :, :], float(CAP), None, ALU.is_lt))
                chain(v.tensor_tensor(weight[:, :, :], weight[:, :, :], keep[:, :, :], ALU.mult))
                chain(v.tensor_tensor(place[:, :, :], pos[:, :, :], over_tiles(slot0[:, :], NEXP), ALU.add))
                chain(v.tensor_scalar(place[:, :, :], place[:, :, :], float(NSLOT), None, ALU.subtract))
                chain(v.tensor_tensor(place[:, :, :], place[:, :, :], keep[:, :, :], ALU.mult))
                chain(v.tensor_scalar(place[:, :, :], place[:, :, :], float(NSLOT), None, ALU.add))
                for k in range(2):
                    chain(v.tensor_scalar(picked[:, :, :], rank[:, :, :], float(k), None, ALU.is_equal))
                    chain(v.tensor_tensor(tmp[:, :, :], place[:, :, :], picked[:, :, :], ALU.mult))
                    chain(v.tensor_reduce(slot_f[:, :], tmp[:, :, :], AX.X, ALU.add))
                    v.tensor_copy(slot[k][:, :], slot_f[:, :]).then_inc(routed, 1)
                    dve.wait_ge(routed, k + 1)
                    chain(v.tensor_tensor(tmp[:, :, :], weight[:, :, :], picked[:, :, :], ALU.mult))
                    chain(v.tensor_reduce(share[k][:, :], tmp[:, :, :], AX.X, ALU.add))

                def body(i, up):
                    if up:
                        gated(dve, i, 0)
                    add(dve, i)
                    if up:
                        hidden(dve, i, 0)
                        gated(dve, i, 1)
                        hidden(dve, i, 1)
                program(body, dve)


def routed_experts(nc, a, sb_, sem_, bank, ident, dispatched, expert_out):
    ctx = ExitStack()
    with ctx:
        def sb(name, shape, dt=F32):
            return sb_(name, shape, dt, ctx)

        def sem(name):
            return sem_(name, ctx)

        wg = [sb(f"expert_gate{q}", [P, KB, E]) for q in range(2)]
        wu = [sb(f"expert_up{q}", [P, KB, E]) for q in range(2)]
        wd = [sb(f"expert_down{q}", [P, KB, E]) for q in range(2)]
        xd = [sb(f"slots_in{q}", [P, 2, E]) for q in range(2)]
        xt = [sb(f"slots_t{q}", [P, KB, 256]) for q in range(2)]
        th = [sb(f"slots_th{q}", [P, KB, 256]) for q in range(2)]
        ga = [sb(f"slots_ga{q}", [P, KB, 256]) for q in range(2)]
        hid = [sb(f"slots_hid{q}", [P, KB, 256]) for q in range(2)]
        yo = [sb(f"slots_out{q}", [P, 2, E]) for q in range(2)]
        w_loaded = [sem(f"expert_loaded{q}") for q in range(2)]
        x_loaded = [sem(f"slots_loaded{q}") for q in range(2)]
        stored = [sem(f"slots_stored{q}") for q in range(2)]
        xt_done, xt_ready, up_done, th_ready = sem("et_done"), sem("et_ready"), sem("eup_done"), sem("eth_ready")
        ga_ready, hid_ready, down_done, y_ready = sem("ega_ready"), sem("ehid_ready"), sem("edown_done"), sem("ey_ready")
        NG = NEXP * ECH
        PAIR = 2 * ECH

        def flat(ap):
            return ap.rearrange("p k s -> p (k s)")

        def slots(ap):
            return ap.rearrange("(g k p) e -> p g k e", p=P, k=2)

        def program(body, eng):
            for j in range(PAIR):
                body(0, j)
            with eng.Fori(1, NEXP // 2) as turn:
                for j in range(PAIR):
                    body(turn, j)

        with nc.Block() as block:
            @block.sync
            def _(sp):
                def weights(turn, q):
                    e = turn * 2 + q
                    for tile, name in ((wg, "we_gate_t"), (wu, "we_up_t"), (wd, "we_down_t")):
                        sp.dma_start(tile[q][:, :, :], a[name].rearrange("e (k p) n -> p e k n", p=P)[:, e]).then_inc(w_loaded[q], 16)

                def body(turn, j):
                    g = turn * PAIR + j
                    first = isinstance(turn, int)
                    if j % ECH == 0:
                        q = j // ECH
                        if not first:
                            sp.wait_ge(down_done, turn * PAIR + (j - ECH))
                        weights(turn, q)
                    if not (first and j < 2):
                        sp.wait_ge(xt_done, g - 1)
                    sp.dma_start(xd[j % 2][:, :, :], slots(dispatched)[:, g]).then_inc(x_loaded[j % 2], 16)
                program(body, sp)

            @block.tensor
            def _(pe):
                def turn_over(g, j):
                    q = j % 2
                    n = g // 2 if isinstance(g, int) else None
                    return q, n

                def transposes(turn, j):
                    g = turn * PAIR + j
                    q = j % 2
                    pe.wait_ge(x_loaded[q], turn * (PAIR // 2 * 16) + (j // 2 + 1) * 16)
                    if not (isinstance(turn, int) and turn == 0 and j < 2):
                        pe.wait_ge(xt_ready, g - 1)
                    for k in range(KB):
                        for s in range(2):
                            last = nc.tensor.transpose(bank[0 + 7 * q][:, k * 256 + s * P:k * 256 + (s + 1) * P], xd[q][:, s, k * P:(k + 1) * P], ident[:, :])
                    last.then_inc(xt_done, 1)

                def gate_up(turn, j):
                    g = turn * PAIR + j
                    q, x = j % 2, j // ECH
                    if j % ECH == 0:
                        pe.wait_ge(w_loaded[x], turn * 48 + 48)
                    pe.wait_ge(xt_ready, g + 1)
                    if not (isinstance(turn, int) and turn == 0 and j < 2):
                        pe.wait_ge(hid_ready, g - 1)
                    for b0, tile in ((1, wg), (2, wu)):
                        for m in range(KB):
                            for k in range(KB):
                                last = nc.tensor.matmul(bank[b0 + 2 * q][:, m * 256:(m + 1) * 256], tile[x][:, k, m * P:(m + 1) * P], xt[q][:, k, :], start=(k == 0), stop=(k == KB - 1))
                    last.then_inc(up_done, 1)

                def down(turn, j):
                    g = turn * PAIR + j
                    q, x = j % 2, j // ECH
                    pe.wait_ge(hid_ready, g + 1)
                    if not (isinstance(turn, int) and turn == 0 and j < 2):
                        pe.wait_ge(y_ready, g - 1)
                    for s in range(2):
                        for m in range(KB):
                            last = nc.tensor.matmul(bank[5 + q][:, s * E:(s + 1) * E], hid[q][:, m, s * P:(s + 1) * P], wd[x][:, m, :], start=(m == 0), stop=(m == KB - 1))
                    last.then_inc(down_done, 1)

                transposes(0, 0)

                def run(turn, more):
                    for j in range(PAIR):
                        if j + 1 < PAIR:
                            transposes(turn, j + 1)
                        elif more:
                            transposes(turn + 1, 0)
                        gate_up(turn, j)
                        if j > 0:
                            down(turn, j - 1)
                        elif not (isinstance(turn, int) and turn == 0):
                            down(turn - 1, PAIR - 1)

                run(0, True)
                with pe.Fori(1, NEXP // 2 - 1) as turn:
                    run(turn, True)
                run(NEXP // 2 - 1, False)
                down(NEXP // 2 - 1, PAIR - 1)

            @block.scalar
            def _(act):
                def move_in(g, q, first):
                    act.wait_ge(xt_done, g + 1)
                    if not first:
                        act.wait_ge(up_done, g - 1)
                    nc.scalar.activation(flat(xt[q][:, :, :]), bank[0 + 7 * q][:, :], ACT.Copy).then_inc(xt_ready, 1)

                move_in(0, 0, True)

                def run(turn, more):
                    start = isinstance(turn, int) and turn == 0
                    for j in range(PAIR):
                        g, q = turn * PAIR + j, j % 2
                        if j + 1 < PAIR or more:
                            move_in(g + 1, 1 - q, start and j < 1)
                        act.wait_ge(up_done, g + 1)
                        if not (start and j < 2):
                            act.wait_ge(ga_ready, g - 1)
                        nc.scalar.activation(flat(th[q][:, :, :]), bank[1 + 2 * q][:, :], ACT.Tanh, scale=0.5).then_inc(th_ready, 1)
                        if not (start and j == 0):
                            act.wait_ge(down_done, g)
                            if not (start and j < 3):
                                n = turn * (PAIR // 2 * 16) + (j - 1) // 2 * 16
                                act.wait_ge(stored[1 - q], n)
                            nc.scalar.activation(flat(yo[1 - q][:, :, :]), bank[5 + 1 - q][:, :], ACT.Copy).then_inc(y_ready, 1)
                            act.wait_ge(y_ready, g)
                            act.dma_start(slots(expert_out[0:NSLOT, :])[:, g - 1], yo[1 - q][:, :, :]).then_inc(stored[1 - q], 16)

                run(0, True)
                with act.Fori(1, NEXP // 2 - 1) as turn:
                    run(turn, True)
                run(NEXP // 2 - 1, False)
                act.wait_ge(down_done, NG)
                act.wait_ge(stored[1], (NG // 2 - 1) * 16)
                nc.scalar.activation(flat(yo[1][:, :, :]), bank[6][:, :], ACT.Copy).then_inc(y_ready, 1)
                act.wait_ge(y_ready, NG)
                act.dma_start(slots(expert_out[0:NSLOT, :])[:, NG - 1], yo[1][:, :, :]).then_inc(stored[1], 16)
                act.wait_ge(stored[0], NG // 2 * 16)
                act.wait_ge(stored[1], NG // 2 * 16)

            @block.vector
            def _(dve):
                def body(turn, j):
                    g, q = turn * PAIR + j, j % 2
                    start = isinstance(turn, int)
                    dve.wait_ge(th_ready, g + 1)
                    nc.vector.scalar_tensor_tensor(flat(ga[q][:, :, :]), flat(th[q][:, :, :]), 1.0, bank[1 + 2 * q][:, :], ALU.add, ALU.mult).then_inc(ga_ready, 1)
                    dve.wait_ge(ga_ready, g + 1)
                    if not (start and j < 2):
                        dve.wait_ge(down_done, g - 1)
                    nc.vector.scalar_tensor_tensor(flat(hid[q][:, :, :]), flat(ga[q][:, :, :]), 0.5, bank[2 + 2 * q][:, :], ALU.mult, ALU.mult).then_inc(hid_ready, 1)
                program(body, dve)


def combine(nc, sb_, sem_, resid, slot, share, expert_out, out):
    ctx = ExitStack()
    with ctx:
        NBUF = 4
        rows = [[sb_(f"picked_rows{k}{q}", [P, E], F32, ctx) for q in range(NBUF)] for k in range(2)]
        fetched = [[sem_(f"fetched{k}{q}", ctx) for q in range(NBUF)] for k in range(2)]
        added, stored = sem_("added", ctx), sem_("out_stored", ctx)

        with nc.Block() as block:
            @block.gpsimd
            def _(pool):
                for n in range(NT):
                    for k in range(2):
                        if n >= NBUF:
                            pool.wait_ge(added, 2 * (n - NBUF) + k + 1)
                        nc.gpsimd.indirect_dma_start(out=rows[k][n % NBUF][:, :], out_offset=None, in_=expert_out,
                                                     in_offset=bass.IndirectOffsetOnAxis(slot[k][:, n:n + 1], 0)).then_inc(fetched[k][n % NBUF], 16)

            @block.vector
            def _(dve):
                for n in range(NT):
                    for k in range(2):
                        dve.wait_ge(fetched[k][n % NBUF], 16 * (n // NBUF + 1))
                        if k == 1:
                            dve.wait_ge(added, 2 * n + 1)
                        tile = resid[:, n // SB, n % SB, :]
                        nc.vector.scalar_tensor_tensor(tile, rows[k][n % NBUF][:, :], share[k][:, n:n + 1], tile, ALU.mult, ALU.add).then_inc(added, 1)

            @block.sync
            def _(sp):
                view = out.rearrange("b (k p) e -> p b k e", p=P)
                with sp.Fori(0, B) as i:
                    sp.wait_ge(added, i * (2 * SB) + 2 * SB)
                    sp.dma_start(view[:, i], resid[:, i]).then_inc(stored, 16)
                sp.wait_ge(stored, 16 * B)


def kernel(**inputs):
    import numpy as _np
    import concourse.bacc as _bacc
    from concourse import mybir as _mybir
    from concourse.bass_utils import run_bass_kernel_spmd as _run

    g = {k: _np.asarray(v) for k, v in inputs.items()}
    arrays = {
        "x": g["x"],
        "ctx_t": g["ctx_1024"].transpose(0, 2, 1).reshape(B, KB, P, S).transpose(0, 2, 1, 3),
        "wq_t": g["L0_attn_wq"].T, "wk_t": g["L0_attn_wk"].T, "wv_t": g["L0_attn_wv"].T, "wo_t": g["L0_attn_wo"].T,
        "bq": g["L0_attn_bq"], "bk": g["L0_attn_bk"], "bv": g["L0_attn_bv"], "bo": g["L0_attn_bo"],
        "freq_filter": g["L0_attn_freq_filter"].reshape(-1),
        "ln_gamma": g["L0_attn_ln_gamma"], "ln_beta": g["L0_attn_ln_beta"],
        "wi_t": g["L0_xattn_Wi"].T, "wg_t": g["L0_xattn_Wg"].T, "a_t": g["L0_xattn_A"].T, "bm_t": g["L0_xattn_Bm"].T,
        "wxo_t": g["L0_xattn_Wo"].T, "bi": g["L0_xattn_bi"], "bg": g["L0_xattn_bg"], "bxo": g["L0_xattn_bo"],
        "decay": _np.repeat(g["L0_xattn_decay"].reshape(-1), E // HEADS),
        "gate_t": g["L0_ffn_gate_w"].T,
        "we_gate_t": g["L0_ffn_we_gate"].transpose(0, 2, 1), "we_up_t": g["L0_ffn_we_up"].transpose(0, 2, 1),
        "we_down_t": g["L0_ffn_we_down"].transpose(0, 2, 1),
        "ws_gate_t": g["L0_ffn_ws_gate"].T, "ws_up_t": g["L0_ffn_ws_up"].T, "ws_down_t": g["L0_ffn_ws_down"].T,
    }
    arrays.update(dft_constants())
    arrays.update(misc_constants())
    arrays = {k: _np.ascontiguousarray(v) for k, v in arrays.items()}
    nc = _bacc.Bacc("TRN2", target_bir_lowering=False, num_devices=1)
    args = {k: nc.dram_tensor(f"in_{k}", v.shape, _mybir.dt.from_np(v.dtype), kind="ExternalInput").ap() for k, v in arrays.items()}
    out = nc.dram_tensor("out_0", (B, S, E), F32, kind="ExternalOutput").ap()
    build(nc, args, out)
    r = _run(nc, [{f"in_{k}": v for k, v in arrays.items()}], core_ids=[0])
    return r.results[0]["out_0"]
```

```python
from contextlib import ExitStack

import numpy as np

import concourse.bass as bass
from concourse import mybir

P = 128
B, S, E = 16, 256, 256
KB = E // P
SB = S // P
NF = S // 2
HEADS = 16
EPS = 1e-5
F32 = mybir.dt.float32
BF16 = mybir.dt.bfloat16
F16 = mybir.dt.float16
F32R = mybir.dt.float32r
U32 = mybir.dt.uint32
ALU = mybir.AluOpType
ACT = mybir.ActivationFunctionType
AX = mybir.AxisListType


def dft_constants():
    t = np.arange(S, dtype=np.float64)
    f = np.arange(NF, dtype=np.float64)
    ang = 2 * np.pi / S * ((np.outer(t, f)) % S)
    nyq = 1.0 - 2.0 * (t % 2)
    weight = np.where(f == 0, 1.0, 2.0)
    sin = np.sin(ang)
    sin[:, 0] = nyq
    forward = np.concatenate([np.cos(ang), sin], 1)
    inverse = np.concatenate([weight * np.cos(ang), np.where(f == 0, 1.0, 2.0) * sin], 1).T / S
    sym = np.cos(ang[:NF]).T
    minus0 = weight[:, None] * (sym - 1.0) / S
    nyq_minus0 = (nyq[:NF] - 1.0) / S
    last_minus0 = weight * ((1.0 - 2.0 * (f % 2)) - 1.0) / S
    tw = np.where(t[:NF] == 0, 1.0, 2.0)
    even = tw[:, None] * np.cos(ang[:NF])
    even_ny = even.copy()
    even_ny[:, 0] = tw * nyq[:NF]
    last = 1.0 - 2.0 * (f % 2)
    row = np.concatenate([nyq_minus0, last])[None, :]
    col = last_minus0[:, None]
    mask = np.where(f == 0, 0.0, 1.0)[:, None]
    cast = lambda a: np.ascontiguousarray(a, dtype=np.float32)
    return {
        "forward": cast(forward), "inverse": cast(inverse),
        "minus0": cast(minus0), "evens": cast(np.concatenate([even, even_ny], 1)),
        "rows": cast(row), "cols": cast(np.concatenate([col, mask], 1)),
    }


def misc_constants():
    k = np.arange(P)
    return {
        "ident": np.eye(P, dtype=np.float32),
        "earlier": (k[:, None] < k[None, :]).astype(np.float32),
        "dc3": np.repeat(np.where(np.arange(P) == 0, float(S), 0.0)[None, :], 3, 0).astype(np.float32),
        "eye3": np.eye(3, dtype=np.float32),
        "slot0": np.broadcast_to((np.arange(8) * CAP).astype(np.float32)[None, :], (P, 8)).copy(),
    }


NEXP = 8
CAP = 1280
NT = B * SB
CH = 16
UP = 2.0 ** 14
NSH = 4
NSLOT = NEXP * CAP
NEARLY = 8
ECH = CAP // 256


def build(nc, a, out):
    ctx = ExitStack()
    with ctx:
        def sb(name, shape, dt=F32, stack=ctx):
            return stack.enter_context(nc.sbuf_tensor(name, shape, dt))

        def sem(name, stack=ctx):
            return stack.enter_context(nc.semaphore(name))

        bank = [ctx.enter_context(nc.psum_tensor(f"bank{i}", [P, 512], F32)) for i in range(8)]
        resid = sb("resid", [P, B, SB, E])
        tok2 = sb("tok2", [P, B * SB * E])
        tok3 = sb("tok3", [P, B * SB * E])
        ln_x = tok2[:, :].rearrange("p (b k e) -> p b k e", b=B, k=SB)
        gate_all = tok2[:, :].rearrange("p (k b s) -> p k b s", k=KB, b=B)
        inp_all = tok3[:, :].rearrange("p (k b s) -> p k b s", k=KB, b=B)
        mhalf = sb("mhalf", [P, 2])

        w = {name: sb(name, [P, KB, E]) for name in ("wi_t", "wg_t", "a_t", "bm_t", "wxo_t")}
        w["ws_gate_t"] = sb("ws_gate_t", [P, KB, NSH * P])
        w["ws_up_t"] = sb("ws_up_t", [P, KB, NSH * P])
        w["ws_down_t"] = sb("ws_down_t", [P, NSH, E])
        w["gate_t"] = sb("gate_t", [P, KB, NEXP])
        cols = {name: sb("col_" + name, [P, KB]) for name in ("bi", "bg", "decay")}
        ident = sb("ident", [P, P])
        dispatched = nc.dram_tensor("dispatched", (NSLOT, E), F32, kind="Internal").ap()
        expert_out = nc.dram_tensor("expert_out", (NSLOT + P, E), F32, kind="Internal").ap()
        ones3 = sb("ones3", [3, P], BF16)
        bias_parts = sb("bias_parts", [3, 5 * E], BF16)

        attention(nc, a, sb, sem, bank, resid, ln_x, mhalf, tok3, w, cols, ident, ones3, bias_parts, dispatched, expert_out)
        recurrence_inputs(nc, sb, sem, bank, resid, gate_all, inp_all, mhalf, w, cols, ident)
        ws_parts = [{name: sb(f"{name}{part}", list(w[name].shape), F32R) for name in ("ws_gate_t", "ws_up_t", "ws_down_t")} for part in ("_hi", "_lo")]
        recurrence(nc, sb, sem, bank, gate_all, inp_all, w, ws_parts)
        ffn(nc, a, sb, sem, bank, resid, ln_x, inp_all, mhalf, out, w, ws_parts, ident, ones3, bias_parts, dispatched, expert_out, tok2)


def attention(nc, a, sb_, sem_, bank, resid, ln_x, mhalf, tok3, later_w, later_cols, ident, ones3, bias_parts, dispatched, expert_out):
    ctx = ExitStack()
    ctx_all = tok3[:, :].rearrange("p (k b s) -> p k b s", k=KB, b=B)
    with ctx:
        def sb(name, shape, dt=F32):
            return sb_(name, shape, dt, ctx)

        def sem(name):
            return sem_(name, ctx)

        used = 0

        def scratch(n):
            nonlocal used
            used += n
            return tok3[:, used - n:used]

        raw = {"wqk": scratch(KB * 2 * E).rearrange("p (k n) -> p k n", k=KB),
               "wv": scratch(KB * E).rearrange("p (k n) -> p k n", k=KB),
               "minus0": scratch(NF), "evens": scratch(2 * NF)}
        raw["rows"] = scratch(2 * NF)[0:1, :]
        raw["cols"] = scratch(2)
        shape = {"wqk": [P, KB, 2 * E], "wv": [P, KB, E], "minus0": [P, NF], "evens": [P, 2 * NF], "rows": [1, 2 * NF], "cols": [P, 2]}
        hi = {name: sb(name + "_hi", shape[name], F32R) for name in raw}
        lo = {name: sb(name + "_lo", shape[name], F32R) for name in ("wqk", "wv", "minus0", "evens")}
        wo = sb("wo", [P, KB, E])
        fwd = sb("fwd", [P, SB, 2 * NF])
        inv = sb("inv", [P, 2, S])
        mask = sb("mask", [P, 2])
        gamma = sb("gamma", [P, E])
        beta = sb("beta", [P, E])
        filt = scratch(2 * E)
        bias3 = scratch(5 * E)[0:3, :]
        bias_hi = sb("bias_hi", [3, 5 * E], BF16)
        bias_mid = sb("bias_mid", [3, 5 * E], BF16)
        bias_lo = sb("bias_lo", [3, 5 * E], BF16)
        bias_r = scratch(5 * E)[0:3, :]
        bias_p = bias3
        dc3f = sb("dc3f", [3, P])
        dc3 = sb("dc3", [3, P], BF16)
        eye3 = sb("eye3", [3, 3])
        one = sb("one", [1, 1])
        st1 = sb("st1", [P, SB, 6])
        mv1 = sb("mv1", [P, SB, 2])
        ve1 = sb("ve1", [P, SB])
        rstd1 = sb("rstd1", [P, SB])
        xn = sb("xn", [P, SB, E])
        fxt_hi = sb("fxt_hi", [P, KB, 2 * NF], F32R)
        fxt_lo = sb("fxt_lo", [P, KB, 2 * NF], F32R)
        sqc = sb("sqc", [P, 2 * E])
        sqs = sb("sqs", [P, 2 * E])
        mag = sb("mag", [P, 2 * E])
        p2 = sb("p2", [P, 2 * E])
        pm = sb("pm", [P, E])
        pm_hi = sb("pm_hi", [P, E], F32R)
        pm_lo = sb("pm_lo", [P, E], F32R)
        pn = sb("pn", [1, E])
        pn_hi = sb("pn_hi", [1, E], F32R)
        pn_lo = sb("pn_lo", [1, E], F32R)
        em = sb("em", [P, E])
        em_hi = sb("em_hi", [P, E], F32R)
        em_lo = sb("em_lo", [P, E], F32R)
        en = sb("en", [1, E])
        en_hi = sb("en_hi", [1, E], F32R)
        en_lo = sb("en_lo", [1, E], F32R)
        vs = sb("vs", [P, 2, E])
        gs = sb("gs", [P, 2, E])
        rz = sb("rz", [P, KB])
        zrow = sb("zrow", [1, E])
        ot = sb("ot", [P, KB, S])
        hh = sb("hh", [P, SB, E])
        tt = sb("tt", [P, SB, E])
        st2 = sb("st2", [P, SB, 6])
        mv2 = sb("mv2", [P, SB, 2])
        ve2 = sb("ve2", [P, SB])
        rstd2 = sb("rstd2", [P, SB])

        waited, waited_act = sem("waited"), sem("waited_act")
        loaded = sem("weights_loaded")
        rows_loaded = sem("rows_loaded")
        x_loaded = sem("x_loaded")
        fixed = sem("constants_ready")
        prep = sem("bias_steps")
        scaled = sem("filter_applied")
        fwd_loaded, w_hi, w_lo = sem("forward_loaded"), sem("weights_high"), sem("weights_low")
        fx_lo_ready, p_lo_ready, e_lo_ready = sem("fx_lo_ready"), sem("p_lo_ready"), sem("e_lo_ready")
        ln1_stats, ln1_aggr, ln1_ve, ln1_rstd = sem("ln1_stats"), sem("ln1_aggr"), sem("ln1_ve"), sem("ln1_rstd")
        xn_ready, xn_saved = sem("xn_ready"), sem("xn_saved")
        dft_done, fx_copied, qk_done, v_done, v_copied = sem("dft_done"), sem("fx_copied"), sem("qk_done"), sem("v_done"), sem("v_copied")
        sq_done, mag_done, p2_done, p_ready, a_done = sem("sq_done"), sem("mag_done"), sem("p2_done"), sem("p_ready"), sem("a_done")
        e_ready, A_done, g_ready, rz_ready = sem("e_ready"), sem("A_done"), sem("g_ready"), sem("rz_ready")
        zrow_ready, z_turned = sem("zrow_ready"), sem("z_turned")
        ot_done, ot_ready, y_done, h_ready = sem("ot_done"), sem("ot_ready"), sem("y_done"), sem("h_ready")
        ln2_stats, ln2_aggr, ln2_ve, ln2_rstd = sem("ln2_stats"), sem("ln2_aggr"), sem("ln2_ve"), sem("ln2_rstd")
        bx_ready, t_ready, x2_ready = sem("bx_ready"), sem("t_ready"), sem("x2_ready")

        def kxm(w):
            return w.rearrange("(k p) n -> p k n", p=P)

        def bcast(v, n):
            return v.rearrange("(o n) -> o n", o=1).broadcast_to([n, v.shape[0]])

        later = sem("later_loaded")
        zeros_ready, zero_stored = sem("zeros_ready"), sem("zero_stored")
        zeros = sb("zeros", [P, 8 * E])

        NLOAD = 10
        OUTPUT = (6, 0)
        HALVES = len(lo)

        def program(body, eng):
            body(0, front=True, back=False, ahead=True)
            with eng.Fori(1, B - 1) as i:
                body(i, front=True, back=True, ahead=True)
            body(B - 1, front=True, back=True, ahead=False)
            body(B, front=False, back=True, ahead=False)

        with nc.Block() as block:
            @block.sync
            def _(sp):
                sp.dma_start(resid[:, 0], a["x"][0].rearrange("(k p) e -> p k e", p=P)).then_inc(x_loaded, 16)
                sp.dma_start(fwd[:, :, :], kxm(a["forward"])).then_inc(fwd_loaded, 16)
                sp.dma_start(raw["wqk"][:, :, 0:E], kxm(a["wq_t"])).then_inc(loaded, 16)
                sp.dma_start(raw["wqk"][:, :, E:2 * E], kxm(a["wk_t"])).then_inc(loaded, 16)
                sp.dma_start(raw["wv"], kxm(a["wv_t"])).then_inc(loaded, 16)
                for name in ("minus0", "evens", "rows", "cols"):
                    sp.dma_start(raw[name], a[name]).then_inc(loaded, 16)
                sp.dma_start(mask[:, :], a["cols"]).then_inc(loaded, 16)
                sp.dma_start(wo[:, :, :], kxm(a["wo_t"])).then_inc(loaded, 16)
                sp.dma_start(inv[:, :, :], kxm(a["inverse"])).then_inc(loaded, 16)
                with sp.Fori(1, B) as i:
                    sp.wait_ge(x_loaded, i * 16)
                    sp.dma_start(resid[:, i], a["x"].rearrange("b (k p) e -> p b k e", p=P)[:, i]).then_inc(x_loaded, 16)
                sp.wait_ge(prep, 2 + 8)
                sp.wait_ge(w_lo, HALVES)
                for k in range(KB):
                    sp.dma_start(ctx_all[:, k], a["ctx_t"].rearrange("b p k s -> k p b s")[k]).then_inc(later, 16)
                for name, tile in later_w.items():
                    sp.dma_start(tile[:, :, :], kxm(a[name])).then_inc(later, 16)
                for name, tile in later_cols.items():
                    sp.dma_start(tile[:, :], a[name].rearrange("(k p) -> p k", p=P), allow_slow_non_contiguous=True).then_inc(later, 16)
                sp.dma_start(ident[:, :], a["ident"]).then_inc(later, 16)
                sp.wait_ge(zeros_ready, 1)
                with sp.Fori(0, NSLOT // (P * 8)) as r:
                    sp.dma_start(dispatched.rearrange("(r p j) e -> p r (j e)", p=P, j=8)[:, r, :], zeros[:, :]).then_inc(zero_stored, 16)
                sp.dma_start(expert_out[NSLOT:NSLOT + P, :], zeros[:, 0:E]).then_inc(zero_stored, 16)
                sp.wait_ge(zero_stored, 16 * (NSLOT // (P * 8) + 1))
                sp.wait_ge(later, 16 * (KB + len(later_w) + len(later_cols) + 1))

            @block.gpsimd
            def _(pool):
                nc.gpsimd.memset(zeros[:, :], 0.0).then_inc(zeros_ready, 1)
                nc.gpsimd.memset(mhalf[:, :], -0.5).then_inc(fixed, 1)
                nc.gpsimd.memset(ones3[:, :], 1.0).then_inc(fixed, 1)
                nc.gpsimd.memset(one[:, :], 1.0).then_inc(fixed, 1)
                pool.wait_ge(fixed, 3)

                def deviation1(i):
                    pool.wait_ge(ln1_aggr, (i + 1) * 2)
                    pool.sem_inc(waited, 1)
                    nc.gpsimd.tensor_scalar(ve1[:, :], mv1[:, :, 1], EPS, None, ALU.add).then_inc(ln1_ve, 1)
                    pool.wait_ge(ln1_ve, i + 1)
                    nc.gpsimd.tensor_tensor(rstd1[:, :], ve1[:, :], mhalf[:, :], ALU.pow).then_inc(ln1_rstd, 1)

                def body(i, front, back, ahead):
                    if front:
                        pool.wait_ge(xn_ready, (i + 1) * 2)
                        nc.gpsimd.tensor_copy(ln_x[:, i], xn[:, :, :]).then_inc(xn_saved, 1)
                    if ahead:
                        deviation1(i + 1)
                    if back:
                        j = i - 1
                        nc.gpsimd.tensor_tensor(resid[:, j], resid[:, j], beta[:, :].rearrange("p (o e) -> p o e", o=1).broadcast_to([P, SB, E]), ALU.add).then_inc(bx_ready, 1)
                        pool.wait_ge(ln2_aggr, (j + 1) * 2)
                        pool.sem_inc(waited, 1)
                        nc.gpsimd.tensor_scalar(ve2[:, :], mv2[:, :, 1], EPS, None, ALU.add).then_inc(ln2_ve, 1)
                        pool.wait_ge(ln2_ve, j + 1)
                        nc.gpsimd.tensor_tensor(rstd2[:, :], ve2[:, :], mhalf[:, :], ALU.pow).then_inc(ln2_rstd, 1)
                deviation1(0)
                pool.wait_ge(w_hi, len(hi))
                for name in lo:
                    every = tuple([slice(None)] * len(shape[name]))
                    nc.gpsimd.tensor_tensor(lo[name][every], raw[name], hi[name][every], ALU.subtract).then_inc(w_lo, 1)
                pool.wait_ge(rows_loaded, 16 * (NLOAD + 1))
                program(body, pool)

            @block.scalar
            def _(act):
                for h in range(2):
                    act.dma_start(filt[:, h * E:(h + 1) * E], bcast(a["freq_filter"], P)).then_inc(rows_loaded, 16)
                for n, v in enumerate(("bq", "bk", "bv", "bo", "bxo")):
                    act.dma_start(bias3[:, n * E:(n + 1) * E], bcast(a[v], 3)).then_inc(rows_loaded, 16)
                act.dma_start(dc3f[:, :], a["dc3"]).then_inc(rows_loaded, 16)
                act.dma_start(eye3[:, :], a["eye3"]).then_inc(rows_loaded, 16)
                act.dma_start(gamma[:, :], bcast(a["ln_gamma"], P)).then_inc(rows_loaded, 16)
                act.dma_start(beta[:, :], bcast(a["ln_beta"], P)).then_inc(rows_loaded, 16)
                act.wait_ge(loaded, 16 * NLOAD)
                for name in ("wv", "minus0", "evens", "rows", "cols"):
                    nc.scalar.activation(hi[name][tuple([slice(None)] * len(shape[name]))], raw[name], ACT.Copy).then_inc(w_hi, 1)
                act.wait_ge(scaled, KB)
                nc.scalar.activation(hi["wqk"][:, :, :], raw["wqk"], ACT.Copy).then_inc(w_hi, 1)

                def body(i, front, back, ahead):
                    j = i - 1
                    if front:
                        act.wait_ge(dft_done, i + 1)
                        if back:
                            act.wait_ge(v_done, i)
                        nc.scalar.activation(fxt_hi[:, :, :].rearrange("p k f -> p (k f)"), bank[0][:, :], ACT.Copy).then_inc(fx_copied, 1)
                    if back:
                        act.wait_ge(a_done, j + 1)
                        for tile, nyquist in ((em_hi, en_hi), (em, en)):
                            nc.scalar.activation(tile[:, :], bank[4][:, 0:E], ACT.Exp).then_inc(e_ready, 1)
                            nc.scalar.activation(nyquist[:, :], bank[4][0:1, E:2 * E], ACT.Exp).then_inc(e_ready, 1)
                    if front:
                        act.wait_ge(qk_done, i + 1)
                        if back:
                            act.wait_ge(p2_done, 2 * i)
                        nc.scalar.activation(sqc[:, :], bank[1][:, :], ACT.Square).then_inc(sq_done, 1)
                        nc.scalar.activation(sqs[:, :], bank[2][:, :], ACT.Square).then_inc(sq_done, 1)
                    if back:
                        act.wait_ge(rz_ready, j + 1)
                        for n in range(KB):
                            act.wait_ge(ot_done, j * KB + (n + 1))
                            act.sem_inc(waited_act, 1)
                            nc.scalar.activation(ot[:, n, :], bank[OUTPUT[n]][:, 0:S], ACT.Copy, scale=rz[:, n:n + 1]).then_inc(ot_ready, 1)
                    if front:
                        act.wait_ge(p2_done, i * 2 + 2)
                        if back:
                            act.wait_ge(a_done, i)
                        for tile, nyquist in ((pm_hi, pn_hi), (pm, pn)):
                            nc.scalar.activation(tile[:, :], p2[:, 0:E], ACT.Sqrt).then_inc(p_ready, 1)
                            nc.scalar.activation(nyquist[:, :], p2[0:1, E:2 * E], ACT.Sqrt).then_inc(p_ready, 1)
                    if front:
                        act.wait_ge(v_done, i + 1)
                        if back:
                            act.wait_ge(g_ready, i)
                        nc.scalar.activation(vs[:, :, :].rearrange("p k f -> p (k f)"), bank[3][:, :], ACT.Copy).then_inc(v_copied, 1)
                program(body, act)

            @block.vector
            def _(dve):
                dve.sem_inc(h_ready, 1)

                def stats1(i):
                    dve.wait_ge(x_loaded, (i + 1) * 16)
                    for k in range(SB):
                        nc.vector.bn_stats(st1[:, k, :], resid[:, i, k, :]).then_inc(ln1_stats, 1)

                def spread1(i, first):
                    dve.wait_ge(ln1_stats, (i + 1) * 2)
                    if not first:
                        dve.wait_ge(ln1_rstd, i)
                    dve.sem_inc(waited, 1)
                    for k in range(SB):
                        nc.vector.bn_aggr(mv1[:, k, :], st1[:, k, :]).then_inc(ln1_aggr, 1)

                def layernorm1(i, first):
                    dve.wait_ge(ln1_rstd, i + 1)
                    if not first:
                        dve.wait_ge(dft_done, i)
                        dve.wait_ge(xn_saved, i)
                    for k in range(SB):
                        nc.vector.tensor_scalar(xn[:, k, :], resid[:, i, k, :], mv1[:, k, 0:1], rstd1[:, k:k + 1], ALU.subtract, ALU.mult).then_inc(xn_ready, 1)

                stats1(0)
                spread1(0, True)
                layernorm1(0, True)
                dve.wait_ge(fixed, 3)
                dve.wait_ge(loaded, 16 * NLOAD)
                dve.wait_ge(rows_loaded, 16 * (NLOAD + 1))
                for k in range(KB):
                    nc.vector.tensor_tensor(raw["wqk"][:, k, :], raw["wqk"][:, k, :], filt, ALU.mult).then_inc(scaled, 1)
                nc.vector.tensor_tensor(bias3[:, 0:2 * E], bias3[:, 0:2 * E], filt[0:3, :], ALU.mult).then_inc(prep, 1)
                nc.vector.tensor_copy(dc3[:, :], dc3f[:, :]).then_inc(prep, 1)
                steps = 2

                def step(ins):
                    nonlocal steps
                    steps += 1
                    ins.then_inc(prep, 1)
                    dve.wait_ge(prep, steps)

                dve.wait_ge(prep, steps)

                def divide_biases(cut):
                    step(nc.vector.tensor_copy(bias_hi[:, cut], bias3[:, cut]))
                    step(nc.vector.tensor_tensor(bias_r[:, cut], bias3[:, cut], bias_hi[:, cut], ALU.subtract))
                    step(nc.vector.tensor_copy(bias_mid[:, cut], bias_r[:, cut]))
                    step(nc.vector.tensor_tensor(bias3[:, cut], bias_r[:, cut], bias_mid[:, cut], ALU.subtract))
                    step(nc.vector.tensor_copy(bias_lo[:, cut], bias3[:, cut]))
                    step(nc.vector.tensor_scalar(bias_r[:, cut], bias_hi[:, cut], eye3[:, 0:1], None, ALU.mult))
                    step(nc.vector.scalar_tensor_tensor(bias_p[:, cut], bias_mid[:, cut], eye3[:, 1:2], bias_r[:, cut], ALU.mult, ALU.add))
                    step(nc.vector.scalar_tensor_tensor(bias_parts[:, cut], bias_lo[:, cut], eye3[:, 2:3], bias_p[:, cut], ALU.mult, ALU.add))

                divide_biases(slice(0, 5 * E))

                def attended(j):
                    dve.wait_ge(y_done, j + 1)
                    dve.wait_ge(xn_saved, j + 1)
                    nc.vector.tensor_tensor(hh[:, :, :].rearrange("p k e -> p (k e)"), bank[7][:, :], ln_x[:, j].rearrange("p k e -> p (k e)"), ALU.add).then_inc(h_ready, 1)
                    dve.wait_ge(h_ready, j + 2)
                    for k in range(SB):
                        nc.vector.bn_stats(st2[:, k, :], hh[:, k, :]).then_inc(ln2_stats, 1)
                    dve.wait_ge(ln2_stats, j * 2 + 2)
                    dve.sem_inc(waited, 1)
                    for k in range(SB):
                        nc.vector.bn_aggr(mv2[:, k, :], st2[:, k, :]).then_inc(ln2_aggr, 1)

                def residual(j):
                    dve.wait_ge(ln2_aggr, j * 2 + 2)
                    for k in range(SB):
                        nc.vector.scalar_tensor_tensor(tt[:, k, :], hh[:, k, :], mv2[:, k, 0:1], gamma[:, :], ALU.subtract, ALU.mult).then_inc(t_ready, 1)
                    dve.wait_ge(t_ready, j * 2 + 2)
                    dve.wait_ge(ln2_rstd, j + 1)
                    dve.wait_ge(bx_ready, j + 1)
                    for k in range(SB):
                        nc.vector.scalar_tensor_tensor(resid[:, j, k, :], tt[:, k, :], rstd2[:, k:k + 1], resid[:, j, k, :], ALU.mult, ALU.add).then_inc(x2_ready, 1)
                    dve.wait_ge(x2_ready, j * 2 + 2)

                def body(i, front, back, ahead, end):
                    j = i - 1
                    if front:
                        dve.wait_ge(fx_copied, i + 1)
                        nc.vector.tensor_tensor(fxt_lo[:, :, :].rearrange("p k f -> p (k f)"), bank[0][:, :], fxt_hi[:, :, :].rearrange("p k f -> p (k f)"), ALU.subtract).then_inc(fx_lo_ready, 1)
                    if back:
                        dve.wait_ge(e_ready, j * 4 + 4)
                        nc.vector.tensor_tensor(em_lo[:, :], em[:, :], em_hi[:, :], ALU.subtract).then_inc(e_lo_ready, 1)
                        nc.vector.tensor_tensor(en_lo[:, :], en[:, :], en_hi[:, :], ALU.subtract).then_inc(e_lo_ready, 1)
                    if end:
                        attended(i - 2)
                    if back:
                        dve.wait_ge(A_done, j + 1)
                        dve.wait_ge(v_copied, j + 1)
                        nc.vector.tensor_tensor(gs[:, :, :].rearrange("p k f -> p (k f)"), bank[5][:, :], vs[:, :, :].rearrange("p k f -> p (k f)"), ALU.mult).then_inc(g_ready, 1)
                        nc.vector.tensor_copy(zrow[:, :], bank[5][0:1, 0:E]).then_inc(zrow_ready, 1)
                    if ahead:
                        stats1(i + 1)
                        spread1(i + 1, False)
                    if back:
                        dve.wait_ge(z_turned, j + 1)
                        nc.vector.reciprocal(rz[:, :], bank[4][:, 0:KB]).then_inc(rz_ready, 1)
                    if front:
                        dve.wait_ge(sq_done, i * 2 + 2)
                        nc.vector.scalar_tensor_tensor(mag[:, :], sqs[:, :], mask[:, 1:2], sqc[:, :], ALU.mult, ALU.add).then_inc(mag_done, 1)
                        if back:
                            dve.wait_ge(p_ready, 4 * i)
                        nc.vector.tensor_tensor(p2[0:1, E:2 * E], sqs[0:1, 0:E], sqs[0:1, E:2 * E], ALU.mult).then_inc(p2_done, 1)
                        dve.wait_ge(mag_done, i + 1)
                        nc.vector.tensor_tensor(p2[:, 0:E], mag[:, 0:E], mag[:, E:2 * E], ALU.mult).then_inc(p2_done, 1)
                    if ahead:
                        layernorm1(i + 1, False)
                    if end:
                        residual(i - 2)
                    if front:
                        dve.wait_ge(p_ready, i * 4 + 4)
                        nc.vector.tensor_tensor(pm_lo[:, :], pm[:, :], pm_hi[:, :], ALU.subtract).then_inc(p_lo_ready, 1)
                        nc.vector.tensor_tensor(pn_lo[:, :], pn[:, :], pn_hi[:, :], ALU.subtract).then_inc(p_lo_ready, 1)

                body(0, True, False, True, False)
                body(1, True, True, True, False)
                with dve.Fori(2, B - 1) as i:
                    body(i, True, True, True, True)
                body(B - 1, True, True, False, True)
                body(B, False, True, False, True)
                attended(B - 1)
                residual(B - 1)

            @block.tensor
            def _(pe):
                pe.wait_ge(fwd_loaded, 16)

                def body(i, front, back, ahead):
                    j = i - 1
                    if front:
                        pe.wait_ge(xn_ready, i * 2 + 2)
                        if back:
                            pe.wait_ge(fx_lo_ready, i)
                        for m in range(KB):
                            for k in range(SB):
                                last = nc.tensor.matmul(bank[0][:, m * S:(m + 1) * S], xn[:, k, m * P:(m + 1) * P], fwd[:, k, :], start=(k == 0), stop=(k == SB - 1))
                        last.then_inc(dft_done, 1)
                    if back:
                        pe.wait_ge(p_lo_ready, j * 2 + 2)
                        for n, (lhs, rhs) in enumerate(three_products((hi["minus0"], lo["minus0"]), (pm_hi, pm_lo))):
                            nc.tensor.matmul(bank[4][:, 0:E], lhs[:, :], rhs[:, :], start=(n == 0), stop=False)
                        for part in (pn_hi, pn_lo):
                            nc.tensor.matmul(bank[4][:, 0:E], hi["rows"][:, 0:NF], part[:, :], start=False, stop=(part is pn_lo))
                        for part in (pm_hi, pm_lo):
                            last = nc.tensor.matmul(bank[4][0:1, E:2 * E], hi["cols"][:, 0:1], part[:, :], start=(part is pm_hi), stop=(part is pm_lo))
                        last.then_inc(a_done, 1)
                    if front:
                        pe.wait_ge(fx_copied, i + 1)
                        if not back:
                            pe.wait_ge(loaded, 16 * NLOAD)
                            pe.wait_ge(prep, 2 + 8)
                            pe.wait_ge(w_lo, HALVES)
                        if back:
                            pe.wait_ge(sq_done, 2 * i)
                        for f in range(2):
                            for n, (lhs, rhs) in enumerate(three_products((fxt_hi, fxt_lo), (hi["wqk"], lo["wqk"]))):
                                if f == 0 and n == 2:
                                    pe.wait_ge(fx_lo_ready, i + 1)
                                for k in range(KB):
                                    last = nc.tensor.matmul(bank[1 + f][:, :], lhs[:, k, f * P:(f + 1) * P], rhs[:, k, :], start=(n == 0 and k == 0), stop=(n == 2 and k == KB - 1 and f == 1))
                            if f == 0:
                                nc.tensor.matmul(bank[1][:, :], dc3[:, :], bias_parts[:, 0:2 * E], start=False, stop=True)
                        last.then_inc(qk_done, 1)
                    if back:
                        pe.wait_ge(e_lo_ready, j * 2 + 2)
                        for h in range(2):
                            for n, (lhs, rhs) in enumerate(three_products((hi["evens"], lo["evens"]), (em_hi, em_lo))):
                                nc.tensor.matmul(bank[5][:, h * E:(h + 1) * E], lhs[:, h * NF:(h + 1) * NF], rhs[:, :], start=(n == 0), stop=False)
                            for part in (en_hi, en_lo):
                                last = nc.tensor.matmul(bank[5][:, h * E:(h + 1) * E], hi["rows"][:, NF:2 * NF], part[:, :], start=False, stop=(part is en_lo))
                        last.then_inc(A_done, 1)

                    def v_half(f):
                        for n, (lhs, rhs) in enumerate(three_products((fxt_hi, fxt_lo), (hi["wv"], lo["wv"]))):
                            for k in range(KB):
                                last = nc.tensor.matmul(bank[3][:, f * E:(f + 1) * E], lhs[:, k, f * P:(f + 1) * P], rhs[:, k, :], start=(n == 0 and k == 0), stop=(n == 2 and k == KB - 1 and f == 1))
                        if f == 0:
                            last = nc.tensor.matmul(bank[3][:, 0:E], dc3[:, :], bias_parts[:, 2 * E:3 * E], start=False, stop=True)
                        return last

                    if front:
                        if back:
                            pe.wait_ge(v_copied, i)
                        v_half(0)
                    if back:
                        pe.wait_ge(g_ready, j + 1)
                        for n in range(KB):
                            for f in range(2):
                                last = nc.tensor.matmul(bank[OUTPUT[n]][:, 0:S], gs[:, f, n * P:(n + 1) * P], inv[:, f, :], start=(f == 0), stop=(f == 1))
                            last.then_inc(ot_done, 1)
                            if n == 0:
                                pe.wait_ge(zrow_ready, j + 1)
                                pe.sem_inc(waited, 1)
                                for m in range(KB):
                                    turned = nc.tensor.transpose(bank[4][:, m:m + 1], zrow[:, m * P:(m + 1) * P], one[:, :])
                                turned.then_inc(z_turned, 1)
                    if front:
                        v_half(1).then_inc(v_done, 1)
                    if back:
                        pe.wait_ge(ot_ready, j * 2 + 2)
                        pe.wait_ge(h_ready, j + 1)
                        for s in range(SB):
                            for k in range(KB):
                                nc.tensor.matmul(bank[7][:, s * E:(s + 1) * E], ot[:, k, s * P:(s + 1) * P], wo[:, k, :], start=(k == 0), stop=False)
                            last = nc.tensor.matmul(bank[7][:, s * E:(s + 1) * E], ones3[:, :], bias_parts[:, 3 * E:4 * E], start=False, stop=True)
                        last.then_inc(y_done, 1)
                program(body, pe)


def recurrence_inputs(nc, sb_, sem_, bank, resid, gate_all, inp_all, mhalf, w, cols, ident):
    ctx = ExitStack()
    with ctx:
        def sb(name, shape, dt=F32):
            return sb_(name, shape, dt, ctx)

        def sem(name):
            return sem_(name, ctx)

        st = sb("st", [P, SB, 6])
        mv = sb("mv", [P, SB, 2])
        ve = sb("ve", [P, SB])
        rstd = sb("rstd", [P, SB])
        xq = sb("xq", [P, SB, E])
        decay = sb("decay_row", [P, KB, S])
        ones = sb("ones_row", [P, S])
        hbg = sb("hbg", [P, KB])
        sq = sb("sq", [P, KB, S])
        sums = sb("sums", [P, KB, S])
        ret = sb("ret", [P, KB, S])
        th = sb("th", [P, KB, S])
        waited = sem("waited2")
        fixed, halved = sem("ones_ready"), sem("rows_ready")
        ln_stats, ln_aggr, ln_ve, ln_rstd = sem("q_stats"), sem("q_aggr"), sem("q_ve"), sem("q_rstd")
        xq_ready, xt_done, sq_ready, sums_ready, ret_ready = sem("xq_ready"), sem("xt_done"), sem("sq_ready"), sem("sums_ready"), sem("ret_ready")
        inp_done, inp_ready, z_done, th_ready, gate_ready = sem("inp_done"), sem("inp_ready"), sem("z_done"), sem("th_ready"), sem("gate_ready")

        def program(body, eng):
            body(0, (0,))
            body(1, (0, 1))
            body(2, (0, 1, 2))
            body(3, (0, 1, 2, 3))
            with eng.Fori(4, B) as i:
                body(i, (0, 1, 2, 3))
            body(B, (1, 2, 3))
            body(B + 1, (2, 3))
            body(B + 2, (3,))

        with nc.Block() as block:
            @block.gpsimd
            def _(pool):
                nc.gpsimd.memset(ones[:, :], 1.0).then_inc(fixed, 1)

                def body(i, stages):
                    if 0 in stages:
                        if 1 in stages:
                            pool.wait_ge(sums_ready, i * 2)
                        nc.gpsimd.tensor_tensor(sq[:, :, :], inp_all[:, :, i, :], inp_all[:, :, i, :], ALU.mult).then_inc(sq_ready, 1)
                        pool.wait_ge(ln_aggr, i * 2 + 2)
                        pool.sem_inc(waited, 1)
                        nc.gpsimd.tensor_scalar(ve[:, :], mv[:, :, 1], EPS, None, ALU.add).then_inc(ln_ve, 1)
                        pool.wait_ge(ln_ve, i + 1)
                        nc.gpsimd.tensor_tensor(rstd[:, :], ve[:, :], mhalf[:, :], ALU.pow).then_inc(ln_rstd, 1)
                program(body, pool)

            @block.vector
            def _(dve):
                dve.wait_ge(fixed, 1)
                for k in range(KB):
                    nc.vector.tensor_scalar(decay[:, k, :], ones[:, :], cols["decay"][:, k:k + 1], None, ALU.mult).then_inc(halved, 1)
                nc.vector.tensor_scalar(hbg[:, :], cols["bg"][:, :], 0.5, None, ALU.mult).then_inc(halved, 1)
                dve.wait_ge(halved, 3)

                def body(i, stages):
                    if 0 in stages:
                        for k in range(SB):
                            nc.vector.bn_stats(st[:, k, :], resid[:, i, k, :]).then_inc(ln_stats, 1)
                        dve.wait_ge(ln_stats, i * 2 + 2)
                        dve.sem_inc(waited, 1)
                        for k in range(SB):
                            nc.vector.bn_aggr(mv[:, k, :], st[:, k, :]).then_inc(ln_aggr, 1)
                    if 1 in stages:
                        dve.wait_ge(xt_done, i)
                        dve.wait_ge(sums_ready, i * 2)
                        if 2 in stages:
                            dve.wait_ge(inp_done, i - 1)
                        nc.vector.tensor_tensor(ret[:, :, :].rearrange("p k s -> p (k s)"), bank[0][:, :], sums[:, :, :].rearrange("p k s -> p (k s)"), ALU.mult).then_inc(ret_ready, 1)
                    if 0 in stages:
                        dve.wait_ge(sq_ready, i + 1)
                        if 1 in stages:
                            dve.wait_ge(ret_ready, i)
                        for k in range(KB):
                            nc.vector.tensor_tensor_scan(sums[:, k, :], decay[:, k, :], sq[:, k, :], 0.0, ALU.mult, ALU.add).then_inc(sums_ready, 1)
                        dve.wait_ge(ln_rstd, i + 1)
                        for k in range(SB):
                            nc.vector.tensor_scalar(xq[:, k, :], resid[:, i, k, :], mv[:, k, 0:1], rstd[:, k:k + 1], ALU.subtract, ALU.mult).then_inc(xq_ready, 1)
                    if 3 in stages:
                        dve.wait_ge(th_ready, i * 2 - 4)
                        nc.vector.tensor_scalar(gate_all[:, :, i - 3, :], th[:, :, :], 0.5 * UP, 0.5 * UP, ALU.mult, ALU.add).then_inc(gate_ready, 1)
                program(body, dve)

            @block.scalar
            def _(act):
                act.wait_ge(halved, 3)

                def body(i, stages):
                    if 2 in stages:
                        act.wait_ge(inp_done, i - 1)
                        act.sem_inc(waited, 1)
                        for n in range(KB):
                            nc.scalar.activation(inp_all[:, n, i - 2, :], bank[1][:, n * S:(n + 1) * S], ACT.Identity, bias=cols["bi"][:, n:n + 1]).then_inc(inp_ready, 1)
                    if 3 in stages:
                        act.wait_ge(z_done, i - 2)
                        if not isinstance(i, int) or i > 3:
                            act.wait_ge(gate_ready, i - 3)
                        for n in range(KB):
                            nc.scalar.activation(th[:, n, :], bank[2][:, n * S:(n + 1) * S], ACT.Tanh, bias=hbg[:, n:n + 1], scale=0.5).then_inc(th_ready, 1)
                program(body, act)

            @block.tensor
            def _(pe):
                def body(i, stages):
                    if 2 in stages:
                        pe.wait_ge(ret_ready, i - 1)
                        if 3 in stages:
                            pe.wait_ge(inp_ready, i * 2 - 4)
                        for n in range(KB):
                            for k in range(KB):
                                last = nc.tensor.matmul(bank[1][:, n * S:(n + 1) * S], w["wi_t"][:, k, n * P:(n + 1) * P], ret[:, k, :], start=(k == 0), stop=(k == KB - 1))
                        last.then_inc(inp_done, 1)
                    if 1 in stages:
                        pe.wait_ge(xq_ready, i * 2)
                        for k in range(KB):
                            for s in range(SB):
                                last = nc.tensor.transpose(bank[0][:, k * S + s * P:k * S + (s + 1) * P], xq[:, s, k * P:(k + 1) * P], ident[:, :])
                        last.then_inc(xt_done, 1)
                    if 3 in stages:
                        pe.wait_ge(inp_ready, i * 2 - 4)
                        if not isinstance(i, int) or i > 3:
                            pe.wait_ge(th_ready, i * 2 - 6)
                        for n in range(KB):
                            for k in range(KB):
                                last = nc.tensor.matmul(bank[2][:, n * S:(n + 1) * S], w["wg_t"][:, k, n * P:(n + 1) * P], inp_all[:, k, i - 3, :], start=(k == 0), stop=(k == KB - 1))
                        last.then_inc(z_done, 1)
                program(body, pe)


def recurrence(nc, sb_, sem_, bank, gate_all, state_all, w, ws_parts):
    ctx = ExitStack()
    NCH = S // CH
    W = KB * B
    with ctx:
        def sb(name, shape, dt=F32):
            return sb_(name, shape, dt, ctx)

        def sem(name):
            return sem_(name, ctx)

        gate = [sb(f"gate_chunk{q}", [P, CH, KB, B]) for q in range(2)]
        inp = [sb(f"inp_chunk{q}", [P, CH, KB, B]) for q in range(2)]
        prod = sb("prod_chunk", [P, CH, KB, B])
        gate_next = sb("gate_next", [P, CH, KB, B])
        gated = sem("gates_ready")
        a_down = sb("a_down", [P, KB, E])
        a_rest = [sb(f"a_rest{i}", [P, KB, E]) for i in range(2)]
        a_part = [sb(f"a_part{i}", [P, KB, E], BF16) for i in range(3)]
        rest = [sb(f"rest_chunk{q}", [P, CH, KB, B]) for q in range(2)]
        state = [sb(f"state_chunk{q}", [P, CH, KB, B]) for q in range(2)]
        blend = sb("blend", [P, KB, B])
        blend_hi = sb("blend_hi", [P, KB, B], F16)
        blend_lo = sb("blend_lo", [P, KB, B], F16)
        split = sem("a_split")
        hi_ready, lo_ready = sem("blend_hi_ready"), sem("blend_lo_ready")
        acc = [bank[3 + q][:, :].rearrange("p (t n b) -> p t n b", t=CH, n=KB) for q in range(2)]
        waited = sem("waited3")
        ws_hi, ws_lo = sem("ws_hi_ready"), sem("ws_lo_ready")
        staged, step_staged, prodded = sem("chunk_staged"), sem("chunk_copied"), sem("prod_ready")
        blended, stepped, tanh_done, saved = sem("blended"), sem("stepped"), sem("tanh_done"), sem("states_saved")
        zeroed = sem("state_zeroed")
        laid = sem("inputs_laid")

        def program(chunk, eng):
            with eng.Fori(0, NCH // 2 - 1) as h:
                chunk(h * 2, 0, True, True)
                chunk(h * 2 + 1, 1, True, True)
            chunk(NCH - 2, 0, True, False)
            chunk(NCH - 1, 1, False, False)

        with nc.Block() as block:
            @block.gpsimd
            def _(pool):
                def stage(c, q):
                    if not isinstance(c, int) or c > 0:
                        pool.wait_ge(gated, c)
                        pool.sem_inc(waited, 1)
                    for k in range(KB):
                        nc.gpsimd.tensor_copy(gate_next[:, :, k, :], gate_all[:, k, :, bass.ts(c, CH)].rearrange("p b t -> p t b")).then_inc(step_staged, 1)
                        nc.gpsimd.tensor_copy(inp[q][:, :, k, :], state_all[:, k, :, bass.ts(c, CH)].rearrange("p b t -> p t b")).then_inc(step_staged, 1)
                    pool.wait_ge(step_staged, c * 4 + 4)
                    pool.sem_inc(waited, 1)
                    nc.gpsimd.tensor_scalar(prod[:, :, :, :], gate_next[:, :, :, :], -1.0, UP, ALU.mult, ALU.add).then_inc(prodded, 1)
                    pool.wait_ge(prodded, c + 1)
                    nc.gpsimd.tensor_tensor(rest[q][:, :, :, :], inp[q][:, :, :, :], prod[:, :, :, :], ALU.mult).then_inc(staged, 1)

                def gates(q):
                    nc.gpsimd.tensor_copy(gate[q][:, :, :, :], gate_next[:, :, :, :]).then_inc(gated, 1)

                nc.gpsimd.memset(state[1][:, CH - 1], 0.0).then_inc(zeroed, 1)
                for _ in range(2):
                    pool.sem_inc(saved, 1)
                for q in range(2):
                    stage(q, q)
                    gates(q)

                def chunk(c, q, more, two):
                    if two:
                        pool.wait_ge(stepped, c * CH + 1)
                        pool.sem_inc(waited, 1)
                        stage(c + 2, q)
                    pool.wait_ge(tanh_done, c * CH + (CH + 1))
                    pool.sem_inc(waited, 1)
                    if two:
                        gates(q)
                    for k in range(KB):
                        last = nc.gpsimd.tensor_copy(state_all[:, k, :, bass.ts(c, CH)].rearrange("p b t -> p t b"), state[q][:, :, k, :])
                        if k < KB - 1:
                            last.then_inc(waited, 1)
                    last.then_inc(saved, 1)

                with pool.Fori(0, NCH // 2 - 1) as h:
                    chunk(h * 2, 0, True, True)
                    chunk(h * 2 + 1, 1, True, True)
                hi, lo = ws_parts
                for name in hi:
                    nc.gpsimd.tensor_copy(hi[name][:, :, :], w[name][:, :, :]).then_inc(ws_hi, 1)
                pool.wait_ge(ws_hi, len(hi))
                for name in hi:
                    nc.gpsimd.tensor_tensor(lo[name][:, :, :], w[name][:, :, :], hi[name][:, :, :], ALU.subtract).then_inc(ws_lo, 1)
                chunk(NCH - 2, 0, True, False)
                chunk(NCH - 1, 1, False, False)
                pool.wait_ge(ws_lo, len(lo))

            @block.tensor
            def _(pe):
                def pieces(q):
                    for t in range(0, CH, CH // 2):
                        for n in range(KB):
                            for lhs, rhs in ((w["bm_t"], inp[q]), (a_down, rest[q])):
                                for k in range(KB):
                                    first = t == 0 and n == 0 and k == 0 and lhs is not a_down
                                    yield nc.tensor.matmul(acc[q][:, t:t + CH // 2, n, :], lhs[:, k, n * P:(n + 1) * P], rhs[:, t:t + CH // 2, k, :],
                                                           start=first, stop=False, skip_group_check=True)

                pe.wait_ge(split, 6)
                pe.wait_ge(staged, 1)
                for _ in pieces(0):
                    pass

                def chunk(c, q, more, two):
                    ahead = pieces(1 - q) if more else iter(())
                    for t in range(CH):
                        for part, (ready, operand, count) in enumerate(((hi_ready, blend_hi, 3), (lo_ready, blend_lo, 2))):
                            pe.wait_ge(ready, c * CH + (t + 1))
                            for n in range(KB):
                                for i in range(count):
                                    for k in range(KB):
                                        last = nc.tensor.matmul(acc[q][:, t, n, :], a_part[i][:, k, n * P:(n + 1) * P], operand[:, k, :],
                                                                start=False, stop=False, skip_group_check=True)
                        last.then_inc(stepped, 1)
                        if more:
                            if t == 0:
                                pe.wait_ge(staged, c + 2)
                            next(ahead)
                program(chunk, pe)

            @block.vector
            def _(dve):
                nc.vector.tensor_scalar(a_down[:, :, :], w["a_t"][:, :, :], 1.0 / UP, None, ALU.mult).then_inc(split, 1)
                before = a_down
                for i in range(3):
                    dve.wait_ge(split, 2 * i + 1)
                    nc.vector.tensor_copy(a_part[i][:, :, :], before[:, :, :]).then_inc(split, 1)
                    if i < 2:
                        dve.wait_ge(split, 2 * i + 2)
                        nc.vector.tensor_tensor(a_rest[i][:, :, :], before[:, :, :], a_part[i][:, :, :], ALU.subtract).then_inc(split, 1)
                        before = a_rest[i]

                def flat(ap):
                    return ap.rearrange("p k b -> p (k b)")

                def chunk(c, q, more, two):
                    for t in range(CH):
                        before = state[q][:, t - 1] if t else state[1 - q][:, CH - 1]
                        if t == 0:
                            dve.wait_ge(gated, c + 1)
                        dve.wait_ge(tanh_done, c * CH + (t + 1))
                        nc.vector.tensor_tensor(flat(blend_hi[:, :, :]), flat(gate[q][:, t]), flat(before), ALU.mult).then_inc(hi_ready, 1)
                        nc.vector.tensor_tensor(flat(blend[:, :, :]), flat(gate[q][:, t]), flat(before), ALU.mult).then_inc(blended, 1)
                        dve.wait_ge(blended, c * CH + (t + 1))
                        nc.vector.tensor_tensor(flat(blend_lo[:, :, :]), flat(blend[:, :, :]), flat(blend_hi[:, :, :]), ALU.subtract).then_inc(lo_ready, 1)
                program(chunk, dve)

            @block.scalar
            def _(act):
                act.wait_ge(zeroed, 1)
                act.sem_inc(tanh_done, 1)

                def chunk(c, q, more, two):
                    for t in range(CH):
                        if t == 0:
                            act.wait_ge(saved, c + 1)
                        act.wait_ge(stepped, c * CH + (t + 1))
                        nc.scalar.activation(state[q][:, t].rearrange("p k b -> p (k b)"), acc[q][:, t].rearrange("p n b -> p (n b)"), ACT.Tanh).then_inc(tanh_done, 1)
                program(chunk, act)


def ffn(nc, a, sb, sem, bank, resid, rows_all, state_all, mhalf, out, w, ws_parts, ident, ones3, bias_parts, dispatched, expert_out, tok2):
    ctx = ExitStack()
    with ctx:
        slot = [sb(f"slot_rank{k}", [P, NT], U32, ctx) for k in range(2)]
        share = [sb(f"share_rank{k}", [P, NT], F32, ctx) for k in range(2)]
        logits = sb("logits", [P, NT, NEXP], F32, ctx)
        project_states(nc, sb, sem, bank, resid, rows_all, state_all, mhalf, w, ident, ones3, bias_parts, logits)
        shared = shared_experts(nc, lambda name, shape, dt=F32: sb(name, shape, dt, ctx), lambda name: sem(name, ctx), bank, resid, state_all, ws_parts)
        experts = expert_weights(nc, a, lambda name, shape, dt=F32: sb(name, shape, dt, ctx), lambda name: sem(name, ctx), w)
        route_and_share(nc, a, sb, sem, bank, rows_all, logits, slot, share, dispatched, shared, experts)
        routed_experts(nc, sb, sem, bank, ident, dispatched, expert_out, experts, tok2, shared)
        combine(nc, sb, sem, resid, slot, share, expert_out, out, shared)


def three_products(parts_l, parts_r):
    (lhs_hi, lhs_lo), (rhs_hi, rhs_lo) = parts_l, parts_r
    return ((lhs_hi, rhs_hi), (lhs_hi, rhs_lo), (lhs_lo, rhs_hi))


class Stages:
    pass


def shared_experts(nc, sb, sem, bank, resid, xt_all, ws_parts):
    x_hi = sb("shared_x_hi", [P, KB, S], F32R)
    x_lo = sb("shared_x_lo", [P, KB, S], F32R)
    h_all = [sb(f"shared_h{h}", [P, 2, S]) for h in range(2)]
    hid_hi = [[sb(f"shared_hid_hi{q}{h}", [P, 2, S], F32R) for h in range(2)] for q in range(2)]
    hid_lo = [[sb(f"shared_hid_lo{q}{h}", [P, 2, S], F32R) for h in range(2)] for q in range(2)]
    x_hi_ready, x_lo_ready, up_done, th_ready, ga_ready = sem("sh_x_hi_ready"), sem("sh_x_lo_ready"), sem("up_done"), sem("f_th_ready"), sem("ga_ready")
    hid_ready, hid_hi_ready, hid_lo_ready, down_done, added = sem("hid_ready"), sem("hid_hi_ready"), sem("hid_lo_ready"), sem("down_done"), sem("sh_added")
    waited = sem("sh_waited")

    def flat(ap):
        return ap.rearrange("p k s -> p (k s)")

    def gate_up(pe, i, h, first):
        if h == 0:
            pe.wait_ge(x_lo_ready, i + 1)
        if not first:
            pe.wait_ge(hid_ready, i * 2 + (h - 1))
        for name, b0 in (("ws_gate_t", 3), ("ws_up_t", 5)):
            for m in range(2):
                out = bank[b0 + h][:, m * S:(m + 1) * S]
                cut = slice((2 * h + m) * P, (2 * h + m + 1) * P)
                products = [(lhs[:, k, cut], rhs[:, k, :]) for lhs, rhs in three_products((ws_parts[0][name], ws_parts[1][name]), (x_hi, x_lo)) for k in range(KB)]
                for n, (lhs, rhs) in enumerate(products):
                    last = nc.tensor.matmul(out, lhs, rhs, start=(n == 0), stop=(n == len(products) - 1))
        last.then_inc(up_done, 1)

    def down(pe, i, q, first):
        pe.wait_ge(hid_lo_ready, i * 2 + 2)
        if not first:
            pe.wait_ge(added, i)
        for s in range(SB):
            cut = slice(s * P, (s + 1) * P)
            products = []
            for m in range(NSH):
                lhs_parts = (hid_hi[q][m // 2], hid_lo[q][m // 2])
                for lhs, rhs in three_products(lhs_parts, (ws_parts[0]["ws_down_t"], ws_parts[1]["ws_down_t"])):
                    products.append((lhs[:, m % 2, cut], rhs[:, m, :]))
            for n, (lhs, rhs) in enumerate(products):
                last = nc.tensor.matmul(bank[7][:, s * E:(s + 1) * E], lhs, rhs, start=(n == 0), stop=(n == len(products) - 1))
        last.then_inc(down_done, 1)

    def x_high(act, i, first):
        if not first:
            act.wait_ge(up_done, i * 2)
            act.sem_inc(waited, 1)
        nc.scalar.activation(x_hi[:, :, :], xt_all[:, :, i, :], ACT.Copy).then_inc(x_hi_ready, 1)

    def x_low(dve, i):
        dve.wait_ge(x_hi_ready, i + 1)
        dve.sem_inc(waited_dve, 1)
        nc.vector.tensor_tensor(x_lo[:, :, :], xt_all[:, :, i, :], x_hi[:, :, :], ALU.subtract).then_inc(x_lo_ready, 1)

    waited_dve = sem("sh_waited_dve")

    def tanh(act, i, h, first):
        act.wait_ge(up_done, i * 2 + (h + 1))
        if not first:
            act.wait_ge(hid_lo_ready, i * 2 + (h - 1))
        nc.scalar.activation(flat(h_all[h][:, :, :]), bank[3 + h][:, :], ACT.Tanh, scale=0.5).then_inc(th_ready, 1)

    def hidden_high(act, i, q, h, early):
        act.wait_ge(hid_ready, i * 2 + (h + 1))
        if not early:
            act.wait_ge(down_done, i - 1)
        nc.scalar.activation(flat(hid_hi[q][h][:, :, :]), flat(h_all[h][:, :, :]), ACT.Copy).then_inc(hid_hi_ready, 1)

    def hidden(dve, i, q, h, between):
        between()
        tile = flat(h_all[h][:, :, :])
        dve.wait_ge(th_ready, i * 2 + (h + 1))
        nc.vector.scalar_tensor_tensor(tile, tile, 1.0, bank[3 + h][:, :], ALU.add, ALU.mult).then_inc(ga_ready, 1)
        dve.wait_ge(ga_ready, i * 2 + (h + 1))
        nc.vector.scalar_tensor_tensor(tile, tile, 0.5, bank[5 + h][:, :], ALU.mult, ALU.mult).then_inc(hid_ready, 1)
        between()
        dve.wait_ge(hid_hi_ready, i * 2 + (h + 1))
        nc.vector.tensor_tensor(flat(hid_lo[q][h][:, :, :]), tile, flat(hid_hi[q][h][:, :, :]), ALU.subtract).then_inc(hid_lo_ready, 1)

    def add(dve, i):
        dve.wait_ge(down_done, i + 1)
        nc.vector.tensor_tensor(flat(resid[:, i]), bank[7][:, :], flat(resid[:, i]), ALU.add).then_inc(added, 1)

    def pe_turn(pe, i, q, first=False, early=False):
        for h in range(2):
            gate_up(pe, i, h, first)
        if not first:
            down(pe, i - 1, 1 - q, early)

    def act_turn(act, i, q, first=False, early=False, last=False):
        if first:
            x_high(act, i, True)
        tanh(act, i, 0, first)
        hidden_high(act, i, q, 0, early)
        if not last:
            x_high(act, i + 1, False)
        tanh(act, i, 1, first)
        hidden_high(act, i, q, 1, early)

    def dve_turn(dve, i, q, first=False, early=False, last=False, between=lambda: None, before_add=lambda: None):
        if first:
            x_low(dve, i)
        hidden(dve, i, q, 0, between)
        if not last:
            x_low(dve, i + 1)
        hidden(dve, i, q, 1, between)
        before_add()
        if not first:
            add(dve, i - 1)

    shared = Stages()
    shared.pe_turn, shared.act_turn, shared.dve_turn = pe_turn, act_turn, dve_turn
    shared.down, shared.add, shared.added = down, add, added
    shared.hid_hi, shared.hid_lo = hid_hi, hid_lo
    return shared


def expert_weights(nc, a, sb, sem, w):
    held = []

    def hold(sb):
        held.append([{name: sb(f"expert_{name}{part}{len(held)}", [P, KB, E], F32R) for name in ("gate", "up", "down")} for part in ("_hi", "_lo")])

    hold(sb)
    raw = [{"gate": w["ws_gate_t"][:, :, q * E:(q + 1) * E], "up": w["ws_up_t"][:, :, q * E:(q + 1) * E],
            "down": w["ws_down_t"][:, q * KB:(q + 1) * KB, :]} for q in range(2)]
    loaded = [sem(f"expert_loaded{q}") for q in range(2)]
    hi_ready, lo_ready, waited = sem("expert_hi_ready"), sem("expert_lo_ready"), sem("ew_waited")

    def load(sp, turn, q):
        for name in ("gate", "up", "down"):
            sp.dma_start(raw[q][name], a[f"we_{name}_t"].rearrange("e (k p) n -> p e k n", p=P)[:, turn * 2 + q]).then_inc(loaded[q], 16)

    def divide(pool, turn, q):
        hi, lo = held[q]
        pool.wait_ge(loaded[q], turn * 48 + 48)
        pool.sem_inc(waited, 1)
        for name in hi:
            nc.gpsimd.tensor_copy(hi[name][:, :, :], raw[q][name]).then_inc(hi_ready, 1)
        pool.wait_ge(hi_ready, turn * 6 + (q * 3 + 3))
        pool.sem_inc(waited, 1)
        for name in hi:
            nc.gpsimd.tensor_tensor(lo[name][:, :, :], raw[q][name], hi[name][:, :, :], ALU.subtract).then_inc(lo_ready, 1)

    experts = Stages()
    experts.held, experts.hold, experts.load, experts.divide, experts.lo_ready = held, hold, load, divide, lo_ready
    return experts


def project_states(nc, sb_, sem_, bank, resid, rows_all, state_all, mhalf, w, ident, ones3, bias_parts, logits):
    ctx = ExitStack()
    with ctx:
        def sb(name, shape, dt=F32):
            return sb_(name, shape, dt, ctx)

        def sem(name):
            return sem_(name, ctx)

        stt = sb("states_tile", [P, KB, S])
        bxo_parts = bias_parts[:, 4 * E:5 * E]
        st = sb("st3", [P, SB, 6])
        mv = sb("mv3", [P, SB, 2])
        ve = sb("ve3", [P, SB])
        rstd = sb("rstd3", [P, SB])
        xf = sb("xf", [P, SB, E])
        xt = sb("xt", [P, KB, S])
        waited = sem("waited4")
        st_ready, y_done, x_ready = sem("st_ready"), sem("yx_done"), sem("x3_ready")
        ln_stats, ln_aggr, ln_ve, ln_rstd = sem("f_stats"), sem("f_aggr"), sem("f_ve"), sem("f_rstd")
        xf_ready, xf_saved, xt_done, xt_ready, lg_done, lg_ready = sem("xf_ready"), sem("xf_saved"), sem("xft_done"), sem("xft_ready"), sem("logits_done"), sem("logits_ready")

        def program(body, eng):
            body(0, (0,))
            body(1, (0, 1))
            body(2, (0, 1, 2))
            body(3, (0, 1, 2, 3))
            with eng.Fori(4, B) as i:
                body(i, (0, 1, 2, 3))
            body(B, (1, 2, 3))
            body(B + 1, (2, 3))
            body(B + 2, (3,))

        def flat(ap):
            return ap.rearrange("p k s -> p (k s)")

        with nc.Block() as block:
            @block.gpsimd
            def _(pool):
                def body(i, stages):
                    if 1 in stages:
                        pool.wait_ge(ln_aggr, i * 2)
                        pool.sem_inc(waited, 1)
                        nc.gpsimd.tensor_scalar(ve[:, :], mv[:, :, 1], EPS, None, ALU.add).then_inc(ln_ve, 1)
                        pool.wait_ge(ln_ve, i)
                        nc.gpsimd.tensor_tensor(rstd[:, :], ve[:, :], mhalf[:, :], ALU.pow).then_inc(ln_rstd, 1)
                program(body, pool)

            @block.scalar
            def _(act):
                def body(i, stages):
                    if 0 in stages:
                        if 1 in stages:
                            act.wait_ge(y_done, i)
                        nc.scalar.activation(stt[:, :, :], state_all[:, :, i, :], ACT.Copy).then_inc(st_ready, 1)
                    if 2 in stages:
                        act.wait_ge(xt_done, i - 1)
                        if 3 in stages:
                            act.wait_ge(lg_done, i - 2)
                        nc.scalar.activation(flat(xt[:, :, :]), bank[1][:, :], ACT.Copy).then_inc(xt_ready, 1)
                        nc.scalar.activation(state_all[:, :, i - 2, :], bank[1][:, :].rearrange("p (k s) -> p k s", k=KB), ACT.Copy).then_inc(xt_ready, 1)
                    if 1 in stages:
                        act.wait_ge(xf_ready, i * 2)
                        act.sem_inc(waited, 1)
                        nc.scalar.activation(rows_all[:, i - 1], xf[:, :, :], ACT.Copy).then_inc(xf_saved, 1)
                program(body, act)

            @block.vector
            def _(dve):
                def body(i, stages):
                    if 1 in stages:
                        dve.wait_ge(y_done, i)
                        nc.vector.tensor_tensor(flat(resid[:, i - 1]), bank[0][:, :], flat(resid[:, i - 1]), ALU.add).then_inc(x_ready, 1)
                        dve.wait_ge(x_ready, i)
                        dve.sem_inc(waited, 1)
                        for k in range(SB):
                            nc.vector.bn_stats(st[:, k, :], resid[:, i - 1, k, :]).then_inc(ln_stats, 1)
                        dve.wait_ge(ln_stats, i * 2)
                        dve.sem_inc(waited, 1)
                        for k in range(SB):
                            nc.vector.bn_aggr(mv[:, k, :], st[:, k, :]).then_inc(ln_aggr, 1)
                    if 3 in stages:
                        dve.wait_ge(lg_done, i - 2)
                        nc.vector.tensor_copy(logits[:, bass.ts(i - 3, SB), :].rearrange("p s e -> p (s e)"), bank[2][:, 0:SB * NEXP]).then_inc(lg_ready, 1)
                    if 1 in stages:
                        dve.wait_ge(ln_rstd, i)
                        if 2 in stages:
                            dve.wait_ge(xt_done, i - 1)
                            dve.wait_ge(xf_saved, i - 1)
                        for k in range(SB):
                            nc.vector.tensor_scalar(xf[:, k, :], resid[:, i - 1, k, :], mv[:, k, 0:1], rstd[:, k:k + 1], ALU.subtract, ALU.mult).then_inc(xf_ready, 1)
                program(body, dve)

            @block.tensor
            def _(pe):
                def body(i, stages):
                    if 1 in stages:
                        pe.wait_ge(st_ready, i)
                        if 2 in stages:
                            pe.wait_ge(x_ready, i - 1)
                        for s in range(SB):
                            for k in range(KB):
                                nc.tensor.matmul(bank[0][:, s * E:(s + 1) * E], stt[:, k, s * P:(s + 1) * P], w["wxo_t"][:, k, :], start=(k == 0), stop=False)
                            last = nc.tensor.matmul(bank[0][:, s * E:(s + 1) * E], ones3[:, :], bxo_parts[:, :], start=False, stop=True)
                        last.then_inc(y_done, 1)
                    if 2 in stages:
                        pe.wait_ge(xf_ready, i * 2 - 2)
                        if 3 in stages:
                            pe.wait_ge(xt_ready, i * 2 - 4)
                        for k in range(KB):
                            for s in range(SB):
                                last = nc.tensor.transpose(bank[1][:, k * S + s * P:k * S + (s + 1) * P], xf[:, s, k * P:(k + 1) * P], ident[:, :])
                        last.then_inc(xt_done, 1)
                    if 3 in stages:
                        pe.wait_ge(xt_ready, i * 2 - 4)
                        if not isinstance(i, int) or i > 3:
                            pe.wait_ge(lg_ready, i - 3)
                        for s in range(SB):
                            for k in range(KB):
                                last = nc.tensor.matmul(bank[2][:, s * NEXP:(s + 1) * NEXP], xt[:, k, s * P:(s + 1) * P], w["gate_t"][:, k, :], start=(k == 0), stop=(k == KB - 1))
                        last.then_inc(lg_done, 1)
                program(body, pe)


def route_and_share(nc, a, sb_, sem_, bank, rows_all, logits, slot, share, dispatched, shared, experts):
    ctx = ExitStack()
    with ctx:
        def sb(name, shape, dt=F32):
            return sb_(name, shape, dt, ctx)

        def sem(name):
            return sem_(name, ctx)

        top = sb("top_logit", [P, NT])
        expo = sb("expo", [P, NT, NEXP])
        total = sb("total", [P, NT])
        prob = sb("prob", [P, NT, NEXP])
        above = sb("above", [P, NT, NEXP * NEXP])
        rank = sb("rank", [P, NT, NEXP])
        picked = sb("picked", [P, NT, NEXP])
        picked_bf = sb("picked_bf", [P, NT * NEXP], BF16)
        earlier_f = sb("earlier_f", [P, P])
        earlier = sb("earlier", [P, P], BF16)
        ones = sb("ones_bf", [P, P], BF16)
        ones_row = sb("ones_nt", [P, NT])
        slot0 = sb("slot0", [P, NEXP])
        cum = sb("cum", [P, NT, NEXP])
        totals = sb("totals", [P, NT, NEXP])
        pos = sb("pos", [P, NT, NEXP])
        keep = sb("keep", [P, NT, NEXP])
        weight = sb("weight", [P, NT, NEXP])
        place = sb("place", [P, NT, NEXP])
        tmp = sb("tmp_route", [P, NT, NEXP])
        slot_f = sb("slot_f", [P, NT])

        def program(turn, eng):
            turn(eng, 0, 0, first=True, early=True)
            turn(eng, 1, 1, early=True)
            with eng.Fori(1, NEARLY // 2) as pair:
                for q in range(2):
                    turn(eng, pair * 2 + q, q)

        loaded, fixed, step = sem("route_loaded"), sem("route_fixed"), sem("route_steps")
        exp_done, counted, routed, sent = sem("exp_done"), sem("counted"), sem("routed"), sem("sent")

        def over_tiles(row, n):
            return row.rearrange("p (o e) -> p o e", o=1).broadcast_to([P, NT, n])

        def over_experts(col):
            return col.rearrange("p (t o) -> p t o", o=1).broadcast_to([P, NT, NEXP])

        with nc.Block() as block:
            @block.sync
            def _(sp):
                for q in range(2):
                    experts.load(sp, 0, q)
                sp.dma_start(earlier_f[:, :], a["earlier"]).then_inc(loaded, 16)
                sp.dma_start(slot0[:, :], a["slot0"]).then_inc(loaded, 16)

            @block.scalar
            def _(act):
                act.wait_ge(step, 2)
                nc.scalar.activation(expo[:, :, :], tmp[:, :, :], ACT.Exp).then_inc(exp_done, 1)

                program(shared.act_turn, act)

            @block.tensor
            def _(pe):
                pe.wait_ge(fixed, 2)
                pe.wait_ge(step, 9)
                nc.tensor.matmul(bank[0][:, 0:NT * NEXP], earlier[:, :], picked_bf[:, :], start=True, stop=True)
                nc.tensor.matmul(bank[1][:, 0:NT * NEXP], ones[:, :], picked_bf[:, :], start=True, stop=True).then_inc(counted, 1)

                program(shared.pe_turn, pe)

            @block.gpsimd
            def _(pool):
                nc.gpsimd.memset(ones[:, :], 1.0).then_inc(fixed, 1)
                nc.gpsimd.memset(ones_row[:, :], 1.0).then_inc(fixed, 1)
                experts.divide(pool, 0, 0)
                for k in range(2):
                    pool.wait_ge(routed, k + 1)
                    for n in range(NT):
                        nc.gpsimd.indirect_dma_start(out=dispatched, out_offset=bass.IndirectOffsetOnAxis(slot[k][:, n:n + 1], 0),
                                                     in_=rows_all[:, n // SB, n % SB, :], in_offset=None,
                                                     bounds_check=NSLOT - 1, oob_is_err=False).then_inc(sent, 16)
                pool.wait_ge(sent, 16 * 2 * NT)

            @block.vector
            def _(dve):
                done = 0

                def chain(ins):
                    nonlocal done
                    done += 1
                    ins.then_inc(step, 1)
                    dve.wait_ge(step, done)

                v = nc.vector
                chain(v.tensor_reduce(top[:, :], logits[:, :, :], AX.X, ALU.max))
                chain(v.tensor_tensor(tmp[:, :, :], logits[:, :, :], over_experts(top[:, :]), ALU.subtract))
                dve.wait_ge(exp_done, 1)
                chain(v.tensor_reduce(total[:, :], expo[:, :, :], AX.X, ALU.add))
                chain(v.reciprocal(top[:, :], total[:, :]))
                chain(v.tensor_tensor(prob[:, :, :], expo[:, :, :], over_experts(top[:, :]), ALU.mult))
                for n in range(NEXP):
                    mine = prob[:, :, n:n + 1].broadcast_to([P, NT, NEXP])
                    if n > 0:
                        v.tensor_tensor(above[:, :, n * NEXP:n * NEXP + n], prob[:, :, 0:n], mine[:, :, 0:n], ALU.is_ge)
                    v.tensor_tensor(above[:, :, n * NEXP + n:(n + 1) * NEXP], prob[:, :, n:NEXP], mine[:, :, n:NEXP], ALU.is_gt)
                dve.drain()
                dve.wait_ge(loaded, 32)
                chain(v.tensor_reduce(rank[:, :, :], above[:, :, :].rearrange("p t (e f) -> p t e f", e=NEXP), AX.X, ALU.add))
                chain(v.tensor_scalar(picked[:, :, :], rank[:, :, :], 2.0, None, ALU.is_lt))
                chain(v.tensor_copy(earlier[:, :], earlier_f[:, :]))
                chain(v.tensor_copy(picked_bf[:, :], picked[:, :, :].rearrange("p t e -> p (t e)")))
                chain(v.tensor_tensor(tmp[:, :, :], prob[:, :, :], picked[:, :, :], ALU.mult))
                chain(v.tensor_reduce(total[:, :], tmp[:, :, :], AX.X, ALU.add))
                chain(v.tensor_scalar(total[:, :], total[:, :], 1e-20, None, ALU.add))
                chain(v.reciprocal(top[:, :], total[:, :]))
                chain(v.tensor_tensor(weight[:, :, :], prob[:, :, :], over_experts(top[:, :]), ALU.mult))
                dve.wait_ge(counted, 1)
                dve.wait_ge(fixed, 2)
                chain(v.tensor_copy(totals[:, :, :].rearrange("p t e -> p (t e)"), bank[1][:, 0:NT * NEXP]))
                for n in range(NEXP):
                    v.tensor_tensor_scan(cum[:, :, n], ones_row[:, :], totals[:, :, n], 0.0, ALU.mult, ALU.add)
                dve.drain()
                chain(v.tensor_tensor(cum[:, :, :], cum[:, :, :], totals[:, :, :], ALU.subtract))
                chain(v.tensor_tensor(pos[:, :, :].rearrange("p t e -> p (t e)"), bank[0][:, 0:NT * NEXP], cum[:, :, :].rearrange("p t e -> p (t e)"), ALU.add))
                chain(v.tensor_scalar(keep[:, :, :], pos[:, :, :], float(CAP), None, ALU.is_lt))
                chain(v.tensor_tensor(weight[:, :, :], weight[:, :, :], keep[:, :, :], ALU.mult))
                chain(v.tensor_tensor(place[:, :, :], pos[:, :, :], over_tiles(slot0[:, :], NEXP), ALU.add))
                chain(v.tensor_scalar(place[:, :, :], place[:, :, :], float(NSLOT), None, ALU.subtract))
                chain(v.tensor_tensor(place[:, :, :], place[:, :, :], keep[:, :, :], ALU.mult))
                chain(v.tensor_scalar(place[:, :, :], place[:, :, :], float(NSLOT), None, ALU.add))
                for k in range(2):
                    chain(v.tensor_scalar(picked[:, :, :], rank[:, :, :], float(k), None, ALU.is_equal))
                    chain(v.tensor_tensor(tmp[:, :, :], place[:, :, :], picked[:, :, :], ALU.mult))
                    chain(v.tensor_reduce(slot_f[:, :], tmp[:, :, :], AX.X, ALU.add))
                    v.tensor_copy(slot[k][:, :], slot_f[:, :]).then_inc(routed, 1)
                    dve.wait_ge(routed, k + 1)
                    chain(v.tensor_tensor(tmp[:, :, :], weight[:, :, :], picked[:, :, :], ALU.mult))
                    chain(v.tensor_reduce(share[k][:, :], tmp[:, :, :], AX.X, ALU.add))

                program(shared.dve_turn, dve)


def routed_experts(nc, sb_, sem_, bank, ident, dispatched, expert_out, experts, tok2, shared):
    ctx = ExitStack()
    with ctx:
        used = 0

        def place():
            nonlocal used
            used += 512
            return tok2[:, used - 512:used].rearrange("p (k s) -> p k s", k=2)

        def sem(name):
            return sem_(name, ctx)

        experts.hold(lambda name, shape, dt: sb_(name, shape, dt, ctx))
        xd = [place() for q in range(2)]
        x_hi = [sb_(f"slots_x_hi{q}", [P, KB, 256], F32R, ctx) for q in range(2)]
        x_lo = [sb_(f"slots_x_lo{q}", [P, KB, 256], F32R, ctx) for q in range(2)]
        h_all = [place() for q in range(2)]
        hid_hi, hid_lo = shared.hid_hi[0], shared.hid_lo[0]
        yo = [place() for q in range(2)]
        x_loaded = [sem(f"slots_loaded{q}") for q in range(2)]
        stored = [sem(f"slots_stored{q}") for q in range(2)]
        xt_done, x_hi_ready, x_lo_ready, up_done, th_ready = sem("et_done"), sem("ex_hi_ready"), sem("ex_lo_ready"), sem("eup_done"), sem("eth_ready")
        ga_ready, hid_ready, hid_hi_ready, hid_lo_ready = sem("ega_ready"), sem("ehid_ready"), sem("ehid_hi_ready"), sem("ehid_lo_ready")
        down_done, y_ready, waited = sem("edown_done"), sem("ey_ready"), sem("e_waited")
        NG = NEXP * ECH
        PAIR = 2 * ECH

        def flat(ap):
            return ap.rearrange("p k s -> p (k s)")

        def slots(ap):
            return ap.rearrange("(g k p) e -> p g k e", p=P, k=2)

        def program(body, eng):
            for j in range(PAIR):
                body(0, j)
            with eng.Fori(1, NEXP // 2) as turn:
                for j in range(PAIR):
                    body(turn, j)

        with nc.Block() as block:
            @block.sync
            def _(sp):
                def run(turn, more):
                    for j in range(PAIR):
                        g = turn * PAIR + j
                        if not (isinstance(turn, int) and turn == 0 and j < 2):
                            sp.wait_ge(xt_done, g - 1)
                        sp.dma_start(xd[j % 2][:, :, :], slots(dispatched)[:, g]).then_inc(x_loaded[j % 2], 16)
                        if more and j % ECH == ECH - 1:
                            q = j // ECH
                            sp.wait_ge(experts.lo_ready, turn * 6 + (q * 3 + 3))
                            sp.sem_inc(waited, 1)
                            experts.load(sp, turn + 1, q)

                run(0, True)
                with sp.Fori(1, NEXP // 2 - 1) as turn:
                    run(turn, True)
                run(NEXP // 2 - 1, False)

            @block.gpsimd
            def _(pool):
                experts.divide(pool, 0, 1)
                with pool.Fori(1, NEXP // 2) as turn:
                    for q in range(2):
                        pool.wait_ge(down_done, (turn - 1) * PAIR + (q + 1) * ECH)
                        experts.divide(pool, turn, q)

            @block.tensor
            def _(pe):
                def transposes(turn, j):
                    g = turn * PAIR + j
                    q = j % 2
                    pe.wait_ge(x_loaded[q], turn * (PAIR // 2 * 16) + (j // 2 + 1) * 16)
                    if not (isinstance(turn, int) and turn == 0 and j < 2):
                        pe.wait_ge(x_lo_ready, g - 1)
                    for k in range(KB):
                        for s in range(2):
                            last = nc.tensor.transpose(bank[0 + 7 * q][:, k * 256 + s * P:k * 256 + (s + 1) * P], xd[q][:, s, k * P:(k + 1) * P], ident[:, :])
                    last.then_inc(xt_done, 1)

                def gate_up(turn, j):
                    g = turn * PAIR + j
                    q, x = j % 2, j // ECH
                    hi, lo = experts.held[x]
                    if j % ECH == 0:
                        pe.wait_ge(experts.lo_ready, turn * 6 + (x * 3 + 3))
                    pe.wait_ge(x_lo_ready, g + 1)
                    if not (isinstance(turn, int) and turn == 0 and j < 2):
                        pe.wait_ge(hid_ready, g - 1)
                    for b0, name in ((1, "gate"), (2, "up")):
                        for m in range(KB):
                            products = [(lhs[:, k, m * P:(m + 1) * P], rhs[:, k, :]) for lhs, rhs in three_products((hi[name], lo[name]), (x_hi[q], x_lo[q])) for k in range(KB)]
                            for n, (lhs, rhs) in enumerate(products):
                                last = nc.tensor.matmul(bank[b0 + 2 * q][:, m * 256:(m + 1) * 256], lhs, rhs, start=(n == 0), stop=(n == len(products) - 1))
                    last.then_inc(up_done, 1)

                def down(turn, j):
                    g = turn * PAIR + j
                    q, x = j % 2, j // ECH
                    hi, lo = experts.held[x]
                    pe.wait_ge(hid_lo_ready, g + 1)
                    if not (isinstance(turn, int) and turn == 0 and j < 2):
                        pe.wait_ge(y_ready, g - 1)
                    for s in range(2):
                        products = [(lhs[:, m, s * P:(s + 1) * P], rhs[:, m, :]) for lhs, rhs in three_products((hid_hi[q], hid_lo[q]), (hi["down"], lo["down"])) for m in range(KB)]
                        for n, (lhs, rhs) in enumerate(products):
                            last = nc.tensor.matmul(bank[5 + q][:, s * E:(s + 1) * E], lhs, rhs, start=(n == 0), stop=(n == len(products) - 1))
                    last.then_inc(down_done, 1)

                transposes(0, 0)

                def run(turn, more):
                    for j in range(PAIR):
                        if j + 1 < PAIR:
                            transposes(turn, j + 1)
                        elif more:
                            transposes(turn + 1, 0)
                        gate_up(turn, j)
                        if j > 0:
                            down(turn, j - 1)
                        elif not (isinstance(turn, int) and turn == 0):
                            down(turn - 1, PAIR - 1)

                run(0, True)
                with pe.Fori(1, NEXP // 2 - 1) as turn:
                    run(turn, True)
                run(NEXP // 2 - 1, False)
                down(NEXP // 2 - 1, PAIR - 1)

            @block.scalar
            def _(act):
                def x_high(g, q, first):
                    act.wait_ge(xt_done, g + 1)
                    if not first:
                        act.wait_ge(up_done, g - 1)
                    nc.scalar.activation(flat(x_hi[q][:, :, :]), bank[0 + 7 * q][:, :], ACT.Copy).then_inc(x_hi_ready, 1)

                def store(turn, j):
                    start = isinstance(turn, int) and turn == 0
                    g, q = turn * PAIR + j, (j + 1) % 2
                    act.wait_ge(down_done, g)
                    if not (start and j < 3):
                        act.wait_ge(stored[q], turn * (PAIR // 2 * 16) + (j - 1) // 2 * 16)
                    nc.scalar.activation(flat(yo[q][:, :, :]), bank[5 + q][:, :], ACT.Copy).then_inc(y_ready, 1)
                    act.wait_ge(y_ready, g)
                    act.dma_start(slots(expert_out[0:NSLOT, :])[:, g - 1], yo[q][:, :, :]).then_inc(stored[q], 16)

                x_high(0, 0, True)

                def run(turn, more):
                    start = isinstance(turn, int) and turn == 0
                    for j in range(PAIR):
                        g, q = turn * PAIR + j, j % 2
                        if j + 1 < PAIR or more:
                            x_high(g + 1, 1 - q, start and j < 1)
                        act.wait_ge(up_done, g + 1)
                        if not (start and j < 2):
                            act.wait_ge(hid_lo_ready, g - 1)
                        nc.scalar.activation(flat(h_all[q][:, :, :]), bank[1 + 2 * q][:, :], ACT.Tanh, scale=0.5).then_inc(th_ready, 1)
                        act.wait_ge(hid_ready, g + 1)
                        if not (start and j < 2):
                            act.wait_ge(down_done, g - 1)
                        nc.scalar.activation(flat(hid_hi[q][:, :, :]), flat(h_all[q][:, :, :]), ACT.Copy).then_inc(hid_hi_ready, 1)
                        if not (start and j == 0):
                            store(turn, j)

                run(0, True)
                with act.Fori(1, NEXP // 2 - 1) as turn:
                    run(turn, True)
                run(NEXP // 2 - 1, False)
                store(NEXP // 2, 0)
                act.wait_ge(stored[0], NG // 2 * 16)
                act.wait_ge(stored[1], NG // 2 * 16)

            @block.vector
            def _(dve):
                def x_low(g, q):
                    dve.wait_ge(x_hi_ready, g + 1)
                    nc.vector.tensor_tensor(flat(x_lo[q][:, :, :]), bank[0 + 7 * q][:, :], flat(x_hi[q][:, :, :]), ALU.subtract).then_inc(x_lo_ready, 1)

                def run(turn, more):
                    for j in range(PAIR):
                        g, q = turn * PAIR + j, j % 2
                        tile = flat(h_all[q][:, :, :])
                        if j + 1 < PAIR or more:
                            x_low(g + 1, 1 - q)
                        dve.wait_ge(th_ready, g + 1)
                        nc.vector.scalar_tensor_tensor(tile, tile, 1.0, bank[1 + 2 * q][:, :], ALU.add, ALU.mult).then_inc(ga_ready, 1)
                        dve.wait_ge(ga_ready, g + 1)
                        nc.vector.scalar_tensor_tensor(tile, tile, 0.5, bank[2 + 2 * q][:, :], ALU.mult, ALU.mult).then_inc(hid_ready, 1)
                        dve.wait_ge(hid_hi_ready, g + 1)
                        nc.vector.tensor_tensor(flat(hid_lo[q][:, :, :]), tile, flat(hid_hi[q][:, :, :]), ALU.subtract).then_inc(hid_lo_ready, 1)

                x_low(0, 0)
                run(0, True)
                with dve.Fori(1, NEXP // 2 - 1) as turn:
                    run(turn, True)
                run(NEXP // 2 - 1, False)


def combine(nc, sb_, sem_, resid, slot, share, expert_out, out, shared):
    ctx = ExitStack()
    with ctx:
        NBUF = 8
        rows = [[sb_(f"picked_rows{k}{q}", [P, E], F32, ctx) for q in range(NBUF)] for k in range(2)]
        fetched = [[sem_(f"fetched{k}{q}", ctx) for q in range(NBUF)] for k in range(2)]
        added, stored, waited = sem_("added", ctx), sem_("out_stored", ctx), sem_("c_waited", ctx)

        with nc.Block() as block:
            @block.gpsimd
            def _(pool):
                for n in range(NT):
                    for k in range(2):
                        if n >= NBUF:
                            pool.wait_ge(added, 2 * (n - NBUF) + k + 1)
                        nc.gpsimd.indirect_dma_start(out=rows[k][n % NBUF][:, :], out_offset=None, in_=expert_out,
                                                     in_offset=bass.IndirectOffsetOnAxis(slot[k][:, n:n + 1], 0)).then_inc(fetched[k][n % NBUF], 16)

            @block.tensor
            def _(pe):
                with pe.Fori(NEARLY // 2, B // 2) as pair:
                    for q in range(2):
                        shared.pe_turn(pe, pair * 2 + q, q)
                shared.down(pe, B - 1, 1, False)

            @block.scalar
            def _(act):
                with act.Fori(NEARLY // 2, B // 2 - 1) as pair:
                    for q in range(2):
                        shared.act_turn(act, pair * 2 + q, q)
                shared.act_turn(act, B - 2, 0)
                shared.act_turn(act, B - 1, 1, last=True)

            @block.vector
            def _(dve):
                def add_rows(n, k):
                    dve.wait_ge(fetched[k][n % NBUF], 16 * (n // NBUF + 1))
                    if k == 1:
                        dve.wait_ge(added, 2 * n + 1)
                    tile = resid[:, n // SB, n % SB, :]
                    nc.vector.scalar_tensor_tensor(tile, rows[k][n % NBUF][:, :], share[k][:, n:n + 1], tile, ALU.mult, ALU.add).then_inc(added, 1)

                tiles = NT // (B - NEARLY)
                for i in range(NEARLY, B):
                    dve.wait_ge(shared.added, i - 1)
                    todo = [(n, k) for n in range((i - NEARLY) * tiles, (i - NEARLY + 1) * tiles) for k in range(2)]

                    def between():
                        for _ in range(tiles // 2):
                            add_rows(*todo.pop(0))

                    def before_add():
                        dve.wait_ge(added, 2 * (i - NEARLY + 1) * tiles)

                    shared.dve_turn(dve, i, i % 2, last=(i == B - 1), between=between, before_add=before_add)
                shared.add(dve, B - 1)

            @block.sync
            def _(sp):
                view = out.rearrange("b (k p) e -> p b k e", p=P)
                with sp.Fori(0, B) as i:
                    sp.wait_ge(added, i * (2 * SB) + 2 * SB)
                    sp.sem_inc(waited, 1)
                    sp.wait_ge(shared.added, i + 1)
                    sp.dma_start(view[:, i], resid[:, i]).then_inc(stored, 16)
                sp.wait_ge(stored, 16 * B)


def kernel(**inputs):
    import numpy as _np
    import concourse.bacc as _bacc
    from concourse import mybir as _mybir
    from concourse.bass_utils import run_bass_kernel_spmd as _run

    g = {k: _np.asarray(v) for k, v in inputs.items()}
    arrays = {
        "x": g["x"],
        "ctx_t": g["ctx_1024"].transpose(0, 2, 1).reshape(B, KB, P, S).transpose(0, 2, 1, 3),
        "wq_t": g["L0_attn_wq"].T, "wk_t": g["L0_attn_wk"].T, "wv_t": g["L0_attn_wv"].T, "wo_t": g["L0_attn_wo"].T,
        "bq": g["L0_attn_bq"], "bk": g["L0_attn_bk"], "bv": g["L0_attn_bv"], "bo": g["L0_attn_bo"],
        "freq_filter": g["L0_attn_freq_filter"].reshape(-1),
        "ln_gamma": g["L0_attn_ln_gamma"], "ln_beta": g["L0_attn_ln_beta"],
        "wi_t": g["L0_xattn_Wi"].T, "wg_t": g["L0_xattn_Wg"].T, "a_t": g["L0_xattn_A"].T, "bm_t": g["L0_xattn_Bm"].T,
        "wxo_t": g["L0_xattn_Wo"].T, "bi": g["L0_xattn_bi"], "bg": g["L0_xattn_bg"], "bxo": g["L0_xattn_bo"],
        "decay": _np.repeat(g["L0_xattn_decay"].reshape(-1), E // HEADS),
        "gate_t": g["L0_ffn_gate_w"].T,
        "we_gate_t": g["L0_ffn_we_gate"].transpose(0, 2, 1), "we_up_t": g["L0_ffn_we_up"].transpose(0, 2, 1),
        "we_down_t": g["L0_ffn_we_down"].transpose(0, 2, 1),
        "ws_gate_t": g["L0_ffn_ws_gate"].T, "ws_up_t": g["L0_ffn_ws_up"].T, "ws_down_t": g["L0_ffn_ws_down"].T,
    }
    arrays.update(dft_constants())
    arrays.update(misc_constants())
    arrays = {k: _np.ascontiguousarray(v) for k, v in arrays.items()}
    nc = _bacc.Bacc("TRN2", target_bir_lowering=False, num_devices=1)
    args = {k: nc.dram_tensor(f"in_{k}", v.shape, _mybir.dt.from_np(v.dtype), kind="ExternalInput").ap() for k, v in arrays.items()}
    out = nc.dram_tensor("out_0", (B, S, E), F32, kind="ExternalOutput").ap()
    build(nc, args, out)
    r = _run(nc, [{f"in_{k}": v for k, v in arrays.items()}], core_ids=[0])
    return r.results[0]["out_0"]
```
